# Optimizing a Trainium2 kernel written in Bass

```python
import numpy as np
import jax
import jax.numpy as jnp

def _softmax(x, axis=-1):
    return jax.nn.softmax(x, axis=axis)

def _gelu(x):
    return jax.nn.gelu(x, approximate=True)

def _silu(x):
    return jax.nn.silu(x)

def _sigmoid(x):
    return jax.nn.sigmoid(x)

def _layernorm(x, axis=-1, eps=1e-05):
    m = jnp.mean(x, axis=axis, keepdims=True)
    v = jnp.var(x, axis=axis, keepdims=True)
    return (x - m) / jnp.sqrt(v + eps)

def _scatter_add(tgt, idx, src, axis=0):
    return tgt.at[idx].add(src)

def _segment_sum(src, seg, n):
    return jax.ops.segment_sum(src, seg, n)
kernel_name = 'mk_gps_d1_gnn_r32_e67354'

def setup_inputs(seed: int=0):
    np.random.seed(seed)
    _w = jnp.asarray

    def _rec_inputs():
        import jax
        import jax.numpy as jnp
        _gk = jax.random.key(seed)
        x = -0.0003713 + 1 * jax.random.normal(jax.random.fold_in(_gk, 1), (3125, 256), jnp.float32)
        _s = jax.random.randint(jax.random.fold_in(_gk, 2), (25000,), 0, 3125, jnp.int32)
        _d = jax.random.randint(jax.random.fold_in(_gk, 3), (25000,), 0, 3125, jnp.int32)
        _loop = jnp.arange(3125, dtype=jnp.int32)
        src = jnp.concatenate([_s, _d, _loop])
        dst = jnp.concatenate([_d, _s, _loop])
        _o = jnp.argsort(dst, stable=True)
        src = src[_o]
        dst = dst[_o]
        return (x, src, dst)
    x, src, dst = _rec_inputs()

    def _L0_gnn_setup():
        import jax, jax.numpy as jnp
        import numpy as np
        N_NODES = 50000
        N_EDGES = 15625
        EPS = 1e-05

        def gcn_conv(x, W, b, src, dst, n):
            h = x @ W
            deg = jax.ops.segment_sum(jnp.ones(src.shape[0], h.dtype), dst, num_segments=n) + 1.0
            dinv = deg ** (-0.5)
            coef = dinv[src] * dinv[dst]
            agg = jax.ops.segment_sum(h[src] * coef[:, None], dst, num_segments=n)
            agg = agg + h * (dinv * dinv)[:, None]
            return agg + b

        def layer_norm(x, gamma, beta):
            m = jnp.mean(x, axis=-1, keepdims=True)
            v = jnp.mean(jnp.square(x - m), axis=-1, keepdims=True)
            return (x - m) * jax.lax.rsqrt(v + EPS) * gamma + beta
        key = jax.random.key(seed)
        ks = jax.random.split(key, 8)
        x = jax.random.normal(ks[0], (N_NODES, 256), dtype=jnp.float32)
        edge_index = jax.random.randint(ks[1], (2, N_EDGES), 0, N_NODES, dtype=jnp.int64)

        def lin(k, i, o):
            return jax.random.normal(k, (i, o), dtype=jnp.float32) * (1.0 / np.sqrt(i))
        W1 = lin(ks[2], 256, 1024)
        W2 = lin(ks[3], 1024, 512)
        W3 = lin(ks[4], 512, 256)
        return {'x': x, 'edge_index': edge_index, 'W1': W1, 'b1': jnp.zeros((1024,), jnp.float32), 'g1': jnp.ones((1024,), jnp.float32), 'beta1': jnp.zeros((1024,), jnp.float32), 'W2': W2, 'b2': jnp.zeros((512,), jnp.float32), 'g2': jnp.ones((512,), jnp.float32), 'beta2': jnp.zeros((512,), jnp.float32), 'W3': W3, 'b3': jnp.zeros((256,), jnp.float32), 'g3': jnp.ones((256,), jnp.float32), 'beta3': jnp.zeros((256,), jnp.float32)}
    _L0_gnn_all = _L0_gnn_setup()
    _L0_gnn_in = {k: v for k, v in _L0_gnn_all.items() if k in ('W1', 'b1', 'g1', 'beta1', 'W2', 'b2', 'g2', 'beta2', 'W3', 'b3', 'g3', 'beta3')}
    del _L0_gnn_all

    def _L0_mix_setup():
        import jax, jax.numpy as jnp
        import numpy as np
        C_CURV = 1.0
        MIN_NORM = 1e-15
        BALL_EPS = 1e-05
        ATT_EPS = 1e-15
        DIM = 32

        def _norm(x):
            return jnp.clip(jnp.linalg.norm(x, axis=-1, keepdims=True), MIN_NORM)

        def proj(x, c):
            maxnorm = (1.0 - BALL_EPS) / jnp.sqrt(c)
            n = _norm(x)
            return jnp.where(n > maxnorm, x / n * maxnorm, x)

        def expmap0(u, c):
            sc = jnp.sqrt(c)
            n = _norm(u)
            return jnp.tanh(sc * n) * u / (sc * n)

        def logmap0(p, c):
            sc = jnp.sqrt(c)
            n = _norm(p)
            return jnp.arctanh(jnp.clip(sc * n, -1.0 + 1e-07, 1.0 - 1e-07)) * p / (sc * n)

        def mobius_add(x, y, c):
            x2 = jnp.sum(x * x, -1, keepdims=True)
            y2 = jnp.sum(y * y, -1, keepdims=True)
            xy = jnp.sum(x * y, -1, keepdims=True)
            num = (1 + 2 * c * xy + c * y2) * x + (1 - c * x2) * y
            den = 1 + 2 * c * xy + c * c * x2 * y2
            return num / jnp.clip(den, MIN_NORM)

        def conv1d(x, w, pad, groups=1):
            return jax.lax.conv_general_dilated(x, w, (1,), [(pad, pad)], dimension_numbers=('NCH', 'OIH', 'NCH'), feature_group_count=groups)

        def batchnorm(x, gamma, beta):
            mean = jnp.mean(x, axis=(0, 2), keepdims=True)
            var = jnp.var(x, axis=(0, 2), keepdims=True)
            xn = (x - mean) * jax.lax.rsqrt(var + 1e-05)
            return gamma[None, :, None] * xn + beta[None, :, None]

        def _reference_tuple_inner(x, w_qkv, bn_gamma, bn_beta, w_dw, w_pw, w_res, b_res):
            c = C_CURV
            h = logmap0(proj(x, c), c)
            h = jnp.transpose(h, (1, 2, 0))
            h = conv1d(h, w_qkv, pad=2)
            h = batchnorm(h, bn_gamma, bn_beta)
            h = jax.nn.relu(jnp.transpose(h, (2, 0, 1)))
            qkv = proj(expmap0(h, c), c)
            t = jnp.transpose(logmap0(proj(qkv, c), c), (1, 2, 0))
            s = conv1d(t, w_dw, pad=2, groups=t.shape[1])
            s = conv1d(s, w_pw, pad=0, groups=t.shape[1] // DIM)
            cat = jnp.concatenate([t, s], axis=1)
            ai = proj(expmap0(jnp.transpose(cat, (2, 0, 1)), c), c)
            t2 = logmap0(proj(ai, c), c)
            L, N, C2 = t2.shape
            g = C2 // (3 * DIM)
            qkv3 = jnp.transpose(t2, (1, 2, 0)).reshape(N, g, 3 * DIM, L)
            q, k, v = jnp.split(qkv3, 3, axis=2)
            q = jax.nn.relu(q)
            k = jax.nn.relu(k)
            vk = jnp.einsum('ngdl,ngel->ngde', v, k)
            out = jnp.einsum('ngde,ngdl->ngdl', vk, q)
            out = out / (jnp.sum(v, -1, keepdims=True) + ATT_EPS)
            out = jnp.transpose(out.reshape(N, g * DIM, L), (2, 0, 1))
            fx_h = proj(expmap0(out, c), c)
            ft = jnp.transpose(logmap0(proj(fx_h, c), c), (1, 2, 0))
            ft = conv1d(ft, w_res, pad=0) + b_res[None, :, None]
            fx = proj(expmap0(jnp.transpose(ft, (2, 0, 1)), c), c)
            residual = mobius_add(fx, x, c)
            return (fx, residual)
        key = jax.random.key(seed)
        ks = jax.random.split(key, 6)
        L, N, C, TD = (64, 16, 256, 256)
        x = jax.random.normal(ks[0], (L, N, C), jnp.float32) * 0.05
        w_qkv = jax.random.normal(ks[1], (3 * TD, C, 5), jnp.float32) / np.sqrt(C * 5)
        bn_gamma = jnp.ones((3 * TD,), jnp.float32)
        bn_beta = jnp.zeros((3 * TD,), jnp.float32)
        w_dw = jax.random.normal(ks[2], (3 * TD, 1, 5), jnp.float32) / np.sqrt(5.0)
        w_pw = jax.random.normal(ks[3], (3 * TD, DIM, 1), jnp.float32) / np.sqrt(DIM)
        w_res = jax.random.normal(ks[4], (C, 2 * TD, 1), jnp.float32) / np.sqrt(2 * TD)
        b_res = jnp.zeros((C,), jnp.float32)
        return {'x': x, 'w_qkv': w_qkv, 'bn_gamma': bn_gamma, 'bn_beta': bn_beta, 'w_dw': w_dw, 'w_pw': w_pw, 'w_res': w_res, 'b_res': b_res}
    _L0_mix_all = _L0_mix_setup()
    _L0_mix_in = {k: v for k, v in _L0_mix_all.items() if k in ('w_qkv', 'bn_gamma', 'bn_beta', 'w_dw', 'w_pw', 'w_res', 'b_res')}
    del _L0_mix_all

    def _L0_ffn_setup():
        import jax, jax.numpy as jnp
        import numpy as np
        B, S, D = (8, 128, 256)
        H = 4 * D
        CAPACITY = 0.5
        key = jax.random.key(seed)
        ks = jax.random.split(key, 6)
        x = jax.random.normal(ks[0], (B, S, D), dtype=jnp.float32)
        attention_mask = jnp.zeros((B, 1, 1, S), dtype=jnp.float32)
        wr = jax.random.normal(ks[1], (D, 1), dtype=jnp.float32) * 0.02
        br = jnp.zeros((1,), dtype=jnp.float32)
        w1 = jax.random.normal(ks[2], (D, H), dtype=jnp.float32) * 0.02
        b1 = jnp.zeros((H,), dtype=jnp.float32)
        w2 = jax.random.normal(ks[3], (H, D), dtype=jnp.float32) * 0.02
        b2 = jnp.zeros((D,), dtype=jnp.float32)
        return {'x': x, 'attention_mask': attention_mask, 'wr': wr, 'br': br, 'w1': w1, 'b1': b1, 'w2': w2, 'b2': b2}
    _L0_ffn_all = _L0_ffn_setup()
    _L0_ffn_in = {k: v for k, v in _L0_ffn_all.items() if k in ('attention_mask', 'wr', 'br', 'w1', 'b1', 'w2', 'b2')}
    del _L0_ffn_all
    return {'x': x, 'src': src, 'dst': dst, 'L0_gnn_W1': _L0_gnn_in['W1'], 'L0_gnn_b1': _L0_gnn_in['b1'], 'L0_gnn_g1': _L0_gnn_in['g1'], 'L0_gnn_beta1': _L0_gnn_in['beta1'], 'L0_gnn_W2': _L0_gnn_in['W2'], 'L0_gnn_b2': _L0_gnn_in['b2'], 'L0_gnn_g2': _L0_gnn_in['g2'], 'L0_gnn_beta2': _L0_gnn_in['beta2'], 'L0_gnn_W3': _L0_gnn_in['W3'], 'L0_gnn_b3': _L0_gnn_in['b3'], 'L0_gnn_g3': _L0_gnn_in['g3'], 'L0_gnn_beta3': _L0_gnn_in['beta3'], 'L0_mix_w_qkv': _L0_mix_in['w_qkv'], 'L0_mix_bn_gamma': _L0_mix_in['bn_gamma'], 'L0_mix_bn_beta': _L0_mix_in['bn_beta'], 'L0_mix_w_dw': _L0_mix_in['w_dw'], 'L0_mix_w_pw': _L0_mix_in['w_pw'], 'L0_mix_w_res': _L0_mix_in['w_res'], 'L0_mix_b_res': _L0_mix_in['b_res'], 'L0_ffn_attention_mask': _L0_ffn_in['attention_mask'], 'L0_ffn_wr': _L0_ffn_in['wr'], 'L0_ffn_br': _L0_ffn_in['br'], 'L0_ffn_w1': _L0_ffn_in['w1'], 'L0_ffn_b1': _L0_ffn_in['b1'], 'L0_ffn_w2': _L0_ffn_in['w2'], 'L0_ffn_b2': _L0_ffn_in['b2']}

def reference(x, src, dst, L0_gnn_W1, L0_gnn_b1, L0_gnn_g1, L0_gnn_beta1, L0_gnn_W2, L0_gnn_b2, L0_gnn_g2, L0_gnn_beta2, L0_gnn_W3, L0_gnn_b3, L0_gnn_g3, L0_gnn_beta3, L0_mix_w_qkv, L0_mix_bn_gamma, L0_mix_bn_beta, L0_mix_w_dw, L0_mix_w_pw, L0_mix_w_res, L0_mix_b_res, L0_ffn_attention_mask, L0_ffn_wr, L0_ffn_br, L0_ffn_w1, L0_ffn_b1, L0_ffn_w2, L0_ffn_b2):
    import jax
    import jax.numpy as jnp

    def _L0_gnn_ref(x, edge_index, W1, b1, g1, beta1, W2, b2, g2, beta2, W3, b3, g3, beta3):
        import jax, jax.numpy as jnp
        import numpy as np
        N_NODES = 50000
        N_EDGES = 15625
        EPS = 1e-05

        def gcn_conv(x, W, b, src, dst, n):
            h = x @ W
            deg = jax.ops.segment_sum(jnp.ones(src.shape[0], h.dtype), dst, num_segments=n) + 1.0
            dinv = deg ** (-0.5)
            coef = dinv[src] * dinv[dst]
            agg = jax.ops.segment_sum(h[src] * coef[:, None], dst, num_segments=n)
            agg = agg + h * (dinv * dinv)[:, None]
            return agg + b

        def layer_norm(x, gamma, beta):
            m = jnp.mean(x, axis=-1, keepdims=True)
            v = jnp.mean(jnp.square(x - m), axis=-1, keepdims=True)
            return (x - m) * jax.lax.rsqrt(v + EPS) * gamma + beta
        src, dst = (edge_index[0], edge_index[1])
        n = x.shape[0]
        x1 = layer_norm(jax.nn.relu(gcn_conv(x, W1, b1, src, dst, n)), g1, beta1)
        x2 = layer_norm(jax.nn.relu(gcn_conv(x1, W2, b2, src, dst, n)), g2, beta2)
        x3 = layer_norm(jax.nn.relu(gcn_conv(x2, W3, b3, src, dst, n)), g3, beta3)
        return x3

    def _L0_mix_ref(x, w_qkv, bn_gamma, bn_beta, w_dw, w_pw, w_res, b_res):
        import jax, jax.numpy as jnp
        import numpy as np
        C_CURV = 1.0
        MIN_NORM = 1e-15
        BALL_EPS = 1e-05
        ATT_EPS = 1e-15
        DIM = 32

        def _norm(x):
            return jnp.clip(jnp.linalg.norm(x, axis=-1, keepdims=True), MIN_NORM)

        def proj(x, c):
            maxnorm = (1.0 - BALL_EPS) / jnp.sqrt(c)
            n = _norm(x)
            return jnp.where(n > maxnorm, x / n * maxnorm, x)

        def expmap0(u, c):
            sc = jnp.sqrt(c)
            n = _norm(u)
            return jnp.tanh(sc * n) * u / (sc * n)

        def logmap0(p, c):
            sc = jnp.sqrt(c)
            n = _norm(p)
            return jnp.arctanh(jnp.clip(sc * n, -1.0 + 1e-07, 1.0 - 1e-07)) * p / (sc * n)

        def mobius_add(x, y, c):
            x2 = jnp.sum(x * x, -1, keepdims=True)
            y2 = jnp.sum(y * y, -1, keepdims=True)
            xy = jnp.sum(x * y, -1, keepdims=True)
            num = (1 + 2 * c * xy + c * y2) * x + (1 - c * x2) * y
            den = 1 + 2 * c * xy + c * c * x2 * y2
            return num / jnp.clip(den, MIN_NORM)

        def conv1d(x, w, pad, groups=1):
            return jax.lax.conv_general_dilated(x, w, (1,), [(pad, pad)], dimension_numbers=('NCH', 'OIH', 'NCH'), feature_group_count=groups)

        def batchnorm(x, gamma, beta):
            mean = jnp.mean(x, axis=(0, 2), keepdims=True)
            var = jnp.var(x, axis=(0, 2), keepdims=True)
            xn = (x - mean) * jax.lax.rsqrt(var + 1e-05)
            return gamma[None, :, None] * xn + beta[None, :, None]

        def _reference_tuple_inner(x, w_qkv, bn_gamma, bn_beta, w_dw, w_pw, w_res, b_res):
            c = C_CURV
            h = logmap0(proj(x, c), c)
            h = jnp.transpose(h, (1, 2, 0))
            h = conv1d(h, w_qkv, pad=2)
            h = batchnorm(h, bn_gamma, bn_beta)
            h = jax.nn.relu(jnp.transpose(h, (2, 0, 1)))
            qkv = proj(expmap0(h, c), c)
            t = jnp.transpose(logmap0(proj(qkv, c), c), (1, 2, 0))
            s = conv1d(t, w_dw, pad=2, groups=t.shape[1])
            s = conv1d(s, w_pw, pad=0, groups=t.shape[1] // DIM)
            cat = jnp.concatenate([t, s], axis=1)
            ai = proj(expmap0(jnp.transpose(cat, (2, 0, 1)), c), c)
            t2 = logmap0(proj(ai, c), c)
            L, N, C2 = t2.shape
            g = C2 // (3 * DIM)
            qkv3 = jnp.transpose(t2, (1, 2, 0)).reshape(N, g, 3 * DIM, L)
            q, k, v = jnp.split(qkv3, 3, axis=2)
            q = jax.nn.relu(q)
            k = jax.nn.relu(k)
            vk = jnp.einsum('ngdl,ngel->ngde', v, k)
            out = jnp.einsum('ngde,ngdl->ngdl', vk, q)
            out = out / (jnp.sum(v, -1, keepdims=True) + ATT_EPS)
            out = jnp.transpose(out.reshape(N, g * DIM, L), (2, 0, 1))
            fx_h = proj(expmap0(out, c), c)
            ft = jnp.transpose(logmap0(proj(fx_h, c), c), (1, 2, 0))
            ft = conv1d(ft, w_res, pad=0) + b_res[None, :, None]
            fx = proj(expmap0(jnp.transpose(ft, (2, 0, 1)), c), c)
            residual = mobius_add(fx, x, c)
            return (fx, residual)
        return _reference_tuple_inner(x, w_qkv, bn_gamma, bn_beta, w_dw, w_pw, w_res, b_res)[0]

    def _L0_ffn_ref(x, attention_mask, wr, br, w1, b1, w2, b2):
        import jax, jax.numpy as jnp
        import numpy as np
        B, S, D = (8, 128, 256)
        H = 4 * D
        CAPACITY = 0.5
        b, s, d = x.shape
        weights = (jnp.einsum('bsd,do->bso', x, wr) + br)[..., 0]
        k = max(1, int(CAPACITY * s))
        kk = k - 1 if k > 1 else 1
        _, idx = jax.lax.top_k(weights, k)
        sel_idx = idx[:, :kk]
        sel = jnp.take_along_axis(x, sel_idx[:, :, None], axis=1)
        h = jax.nn.gelu(jnp.einsum('bkd,dh->bkh', sel, w1) + b1)
        y = jnp.einsum('bkh,hd->bkd', h, w2) + b2
        w_sel = jnp.take_along_axis(weights, sel_idx, axis=1)
        y = y * w_sel[..., None]
        batch_idx = jnp.arange(b)[:, None]
        processed = jnp.zeros_like(x).at[batch_idx, sel_idx].set(y)
        return processed + x
    edge_index = jnp.stack([src, dst])
    xn = _layernorm(x, axis=-1)
    x = x + _L0_gnn_ref(xn, edge_index, L0_gnn_W1, L0_gnn_b1, L0_gnn_g1, L0_gnn_beta1, L0_gnn_W2, L0_gnn_b2, L0_gnn_g2, L0_gnn_beta2, L0_gnn_W3, L0_gnn_b3, L0_gnn_g3, L0_gnn_beta3) + _L0_mix_ref(xn[None], L0_mix_w_qkv, L0_mix_bn_gamma, L0_mix_bn_beta, L0_mix_w_dw, L0_mix_w_pw, L0_mix_w_res, L0_mix_b_res)[0]
    x = x + _L0_ffn_ref(_layernorm(x, axis=-1)[None], L0_ffn_attention_mask, L0_ffn_wr, L0_ffn_br, L0_ffn_w1, L0_ffn_b1, L0_ffn_w2, L0_ffn_b2)[0]
    return x

_drawn_inputs = setup_inputs


def setup_inputs(seed=0):
    import zlib

    import numpy as np

    out = dict(_drawn_inputs(seed))
    spreads = {'L0_gnn_b1': (0.0, 0.1),
     'L0_gnn_g1': (1.0, 0.2),
     'L0_gnn_beta1': (0.0, 0.1),
     'L0_gnn_b2': (0.0, 0.1),
     'L0_gnn_g2': (1.0, 0.2),
     'L0_gnn_beta2': (0.0, 0.1),
     'L0_gnn_b3': (0.0, 0.1),
     'L0_gnn_g3': (1.0, 0.2),
     'L0_gnn_beta3': (0.0, 0.1),
     'L0_mix_bn_gamma': (1.0, 0.6),
     'L0_mix_bn_beta': (0.0, 0.698),
     'L0_mix_b_res': (0.0, 0.531),
     'L0_ffn_b1': (0.0, 0.8),
     'L0_ffn_b2': (0.0, 0.8)}
    factors = {'L0_mix_w_dw': 8.0,
     'L0_mix_w_pw': 8.0,
     'L0_ffn_wr': 4.808,
     'L0_ffn_w1': 7.739,
     'L0_ffn_w2': 7.226}
    for name, (base, spread) in spreads.items():
        noise = np.random.default_rng([zlib.crc32(name.encode()), seed]).standard_normal(out[name].shape)
        drawn = base * np.exp(spread * noise) if base else spread * noise
        out[name] = jnp.asarray(drawn.astype(out[name].dtype))
    for name, factor in factors.items():
        out[name] = (out[name] * factor).astype(out[name].dtype)
    return out
```

```python
from contextlib import ExitStack

import numpy as np
import concourse.bass as bass
from concourse import mybir

F32 = mybir.dt.float32
F16 = mybir.dt.float16
BF16 = mybir.dt.bfloat16
I32 = mybir.dt.int32
ALU = mybir.AluOpType
ACT = mybir.ActivationFunctionType
AX = mybir.AxisListType.X

N = 3125
E = 53125
P = 125
T = N // P
G = 5
D = 256
D1, D2, D3 = 1024, 512, 256
CW = G * P + 1
CH = CW // 2
NC = T // G
EC = E // P
HALO = 40
EW = EC + 2 * HALO
NWIN = -(-E // HALO)
EB = 25
PADE = NWIN * HALO + HALO
SB = EC // 5
KSEL = N // 2 - 1
EPS = 1e-5
F16_TOP = 32000.0
X_SCALE = 2048.0
BALL = float(np.float32(1.0 - 1e-5))
RMAX = float(np.arctanh(np.float64(np.float32(1.0 - 1e-5))))
ROUND = 1.5 * 2 ** 23
NT = 6
RING = 4


class Steps:

    def __init__(self, eng, sem):
        self.eng, self.sem, self.base, self.k = eng, sem, 0, 0

    def did(self, ins):
        ins.then_inc(self.sem, 1)
        self.k += 1

    def settle(self):
        self.eng.wait_ge(self.sem, self.base + self.k)

    def enter(self, i, per):
        self.outer, self.per = self.k, per
        self.base, self.k = i * per + self.outer, 0

    def leave(self, times):
        assert self.k == self.per, (self.k, self.per)
        self.base, self.k = 0, self.outer + times * self.per


def free(ap, offset, dims):
    return bass.AP(ap.tensor, ap.offset + offset, [list(ap.ap[0])] + [list(d) for d in dims])


def build(nc, a, out, scratch):
    with ExitStack() as ctx:
        _build(ctx, nc, a, out, scratch)


def _build(ctx, nc, a, out, scratch):
    counts_dram, w_dram = scratch["counts"], scratch["w"]

    def sb(name, shape, dt):
        return ctx.enter_context(nc.sbuf_tensor(name, shape, dt))

    sems = {}

    def sem(name):
        if name not in sems:
            sems[name] = ctx.enter_context(nc.semaphore(name))
        return sems[name]

    psum = ctx.enter_context(nc.psum_tensor("psum", [128, 8, 512], F32))
    rows = sb("rows", [128, T * D], F32)
    acc = sb("acc", [128, T * D], F32)
    big = sb("big", [128, 12800], F32)
    wa = sb("wa", [128, 2048], F32)
    wb = sb("wb", [128, 4096], F32)
    wc = sb("wc", [128, 1024], F32)
    wm = sb("wm", [128, 3328], F32)
    scr = sb("scr", [128, 15600], F32)
    ident = sb("ident", [128, 128], F32)
    ones = sb("ones", [128, 128], F32)
    kones = sb("kones", [128, 128], F32)
    col = sb("col", [128, 900], F32)

    at = {"scr": 0, "col": 0, "wm": 0, "big": 0}

    def take(region, n):
        t = {"scr": scr, "col": col, "wm": wm, "big": big}[region]
        o = at[region]
        at[region] = o + n
        assert at[region] <= t.shape[1], (region, at[region])
        return t[:, o:o + n]

    x_rows = rows[:P, :].rearrange("p (t d) -> p t d", t=T)
    x2 = rows[:P, :].bitcast(F16).rearrange("p (t h d) -> p t h d", t=T, h=2)
    accv = acc[:P, :].rearrange("p (t d) -> p t d", t=T)
    zv = accv
    zT = take("big", 2 * NC * CW).rearrange("p (k c) -> p k c", k=2)
    hT = take("big", NT * CW).rearrange("p (m c) -> p m c", m=NT)
    sq = take("big", 3 * CW).rearrange("p (m c) -> p m c", m=3)
    umax = take("big", CW)
    h2in = big[:P, :].bitcast(F16).rearrange("p (t h d) -> p t h d", t=T, h=2)
    xn2 = big[:P, 0:6400].rearrange("p (t d) -> p t d", t=T)
    gT = big[:, 6400:6400 + 8 * CW].rearrange("p (m c) -> p m c", m=8)
    w1 = wa[:, :].rearrange("p (k n) -> p k n", k=2)
    w2 = wb[:, :].rearrange("p (k n) -> p k n", k=8)
    w3 = wc[:, :].rearrange("p (k n) -> p k n", k=4)
    f1 = wa[:, :].rearrange("p (k n) -> p k n", k=2)
    f2 = wb[:, 0:2048].rearrange("p (k n) -> p k n", k=8)
    zi = wb[:P, 0:3072].bitcast(F16)
    wq = take("wm", 2 * 768).rearrange("p (k n) -> p k n", k=2)
    wp = take("wm", NT * 128).rearrange("p (m n) -> p m n", m=NT)
    wres = take("wm", 4 * D).rearrange("p (k n) -> p k n", k=4)
    b1r, b2r, b3r = wm[:P, 0:1024], wm[:P, 1024:1536], wm[:P, 1536:1792]
    g3r, be3r = wm[:P, 1792:2048], wm[:P, 2048:2304]
    fb2r, wrr = wm[:P, 2304:2560], wm[:P, 2560:2816]
    sT = take("scr", NT * CW).rearrange("p (m c) -> p m c", m=NT)
    veps = take("scr", CW)
    tdiv = take("scr", CW)
    xbuf = take("scr", G * D)[:P].rearrange("p (t d) -> p t d", t=G)
    gram = take("scr", 512).rearrange("p (k n) -> p k n", k=2)
    bresr = take("scr", 256)[:P]
    sqjunk = take("scr", 256)[:P]
    gw = scr[:, 0:2 * 768].rearrange("p (k n) -> p k n", k=2)
    sqw = scr[:, NT * CW:NT * CW + 512]
    esrc_i = take("scr", EW)[:P].bitcast(I32)
    edst_i = take("scr", EW)[:P].bitcast(I32)
    esrc = take("scr", EW)[:P]
    ekey = take("scr", EW)[:P]
    edp = take("scr", EW)[:P]
    edt = take("scr", EW)[:P]
    fwd = take("scr", EC)[:P]
    bwd = take("scr", EC)[:P]
    eidx = take("scr", EC)[:P].bitcast(I32)
    evalue = take("scr", EC // 2 + 1)[:P].bitcast(F16)
    eq = take("scr", EB * HALO // 2)[:P].bitcast(BF16).rearrange("p (j s) -> p j s", j=EB)
    ohp = take("scr", (EB * P + 1) // 2)[:P].bitcast(BF16)[:, 0:EB * P].rearrange("p (j q) -> p j q", j=EB)
    oht = take("scr", (EB * T + 1) // 2)[:P].bitcast(BF16)[:, 0:EB * T].rearrange("p (j q) -> p j q", j=EB)
    sidx = take("scr", SB)[:P].bitcast(I32)
    svalue = take("scr", (SB + 1) // 2)[:P].bitcast(F16)
    iop = take("scr", (P + 1) // 2)[:P].bitcast(BF16)
    wkey = take("scr", EW)[:P]
    at["scr"] = 0
    ring = take("scr", RING * 1563)[:P].bitcast(F16)
    ring = [ring[:, s * 3126:s * 3126 + N].rearrange("p (t q) -> p t q", t=T) for s in range(RING)]
    pre = [take("scr", 1024)[:P] for _ in range(2)]
    xT = take("scr", 8 * P).rearrange("p (k q) -> p k q", k=8)
    ysum, yhi = take("scr", D)[:P], take("scr", D)[:P]
    yT = take("scr", 2 * P).rearrange("p (k q) -> p k q", k=2)
    hbuf = take("scr", 512)[:P]
    post = take("scr", D)[:P]
    stage = take("scr", G * D)[:P].rearrange("p (t d) -> p t d", t=G)
    nT = take("scr", 2 * CW).rearrange("p (k c) -> p k c", k=2)
    wall = scr[:P, 0:N]
    gtjunk = scr[:P, N + 1:N + 1 + 1563].bitcast(BF16)[:, 0:N]
    sgjunk = scr[:P, N + 1 + 1563:N + 1 + 2 * 1563].bitcast(BF16)[:, 0:N]
    def c_(n):
        return take("col", n)
    stats = c_(T * 6)[:P].rearrange("p (t s) -> p t s", t=T)
    mv = c_(T * 2)[:P].rearrange("p (t s) -> p t s", t=T)
    rstd, dinv, ca, cb, cc, cd = (c_(T)[:P] for _ in range(6))
    dx, d2in, d2out, d3in, d3out = (c_(T)[:P] for _ in range(5))
    st2 = c_(12)[:P].rearrange("p (a s) -> p a s", a=2)
    mv2, rs2, root2 = c_(2)[:P], c_(1)[:P], c_(1)[:P]
    eps = c_(1)
    bng, bnb, bns, bnt, wdw, tmp6 = (c_(NT) for _ in range(6))
    zcol = c_(2)
    zrow = big[0:1, 10016:10016 + 256]
    nzrow = big[0:1, 10016 + 256:10016 + 512]
    g1c, be1c, fb1c, g2c, be2c = c_(8), c_(8), c_(8), c_(4), c_(4)
    ssw, ssg = c_(12), c_(12)
    ssb = c_(12)
    bound = c_(8)
    ucol, ocol = (c_(G)[:P] for _ in range(2))
    n4, f4 = (c_(T)[:P] for _ in range(2))
    flagf, flagi = c_(1), c_(1).bitcast(I32)
    wv, wsel, gt, sg, bnd, pref, brc = (c_(T)[:P] for _ in range(7))
    tri = kones
    pause, pool_pause = c_(1)[:P], c_(1)[:P]

    def bank(b, p, n, o=0):
        return psum[:p, b, o:o + n]

    def pair(i, p=128):
        return psum[:p, 2 * i:2 * i + 2, 0:CH]

    def halves(ap):
        return ap.rearrange("p (h c) -> p h c", h=2)

    block = ctx.enter_context(nc.Block())

    @block.sync
    def _(sp):
        def load(dst, src, name):
            sp.dma_start(dst, src).then_inc(sem(name), 16)

        src_w = bass.AP(a["src_pad"].tensor, PADE - HALO, [[EC, P], [1, EW]])
        dst_w = bass.AP(a["dst_pad"].tensor, PADE - HALO, [[EC, P], [1, EW]])
        load(esrc_i, src_w, "edges_loaded")
        load(edst_i, dst_w, "edges_loaded")
        load(x_rows, a["x"].rearrange("(p t) d -> p t d", t=T), "x_loaded")
        load(wq, a["wq"].rearrange("(k p) n -> p k n", p=128), "mixw_loaded")
        load(wres, a["wres"].rearrange("(k p) n -> p k n", p=128), "mixw_loaded")
        load(bresr, bass.AP(a["bres"].tensor, 0, [[0, P], [1, D]]), "mixw_loaded")
        load(bng, a["bng"], "mixw_loaded")
        load(bnb, a["bnb"], "mixw_loaded")
        load(wdw, a["wdw"], "mixw_loaded")
        sp.wait_ge(sem("blocks_cleared"), 1)
        for b in range(4):
            load(wp[32 * b:32 * b + 32, :, 32 * b:32 * b + 32], a["wpw"][b], "mixw_loaded")
        for dst, name in ((g1c, "g1"), (be1c, "be1"), (fb1c, "fb1"), (g2c, "g2"), (be2c, "be2")):
            load(dst, a[name], "cols_loaded")
        sp.wait_ge(sem("zi_ready"), 2)
        for t in range(T):
            sp.dma_start(counts_dram[t], free(zi, (T - 1 - t) * P, [[1, N]])).then_inc(sem("counts_cleared"), 16)
        load(w1, a["w1"].rearrange("(k p) n -> p k n", p=128), "layerw_loaded")
        load(w3, a["w3"].rearrange("(k p) n -> p k n", p=128), "layerw_loaded")
        sp.wait_ge(sem("flag_ready"), 1)
        far = sp.value_load(flagi[0:1, 0:1], min_val=0, max_val=1)
        with sp.If(far > 0):
            with sp.Fori(1, NWIN) as w:
                for side in (0, 1):
                    sp.wait_ge(sem("window_used"), w * 2 + (side - 2))
                    for dst, name in ((esrc_i, "src_pad"), (edst_i, "dst_pad")):
                        o = PADE - HALO + (w * HALO if side == 0 else w * (-HALO))
                        sp.dma_start(dst, bass.AP(a[name].tensor, o, [[EC, P], [1, EW]])).then_inc(
                            sem("window_loaded"), 16)
        sp.wait_ge(sem("counts_cleared"), 16 * T)
        load(w2, a["w2"].rearrange("(k p) n -> p k n", p=128), "layerw_loaded")
        xd = a["x"].rearrange("(p t) d -> p t d", t=T)
        with sp.Fori(0, NC) as i:
            sp.wait_ge(sem("fx_done"), i * G)
            sp.dma_start(xbuf, xd[:, bass.ds(i * G, G), :]).then_inc(sem("xbuf_loaded"), 16)
        sp.wait_ge(sem("fx_done"), T)
        sp.wait_ge(sem("res_done"), T)
        for dst, name, n in ((b1r, "b1", D1), (b2r, "b2", D2), (b3r, "b3", D3), (g3r, "g3", D3),
                             (be3r, "be3", D3), (fb2r, "fb2", D), (wrr, "wr", D)):
            load(dst, bass.AP(a[name].tensor, 0, [[0, P], [1, n]]), "rowb_loaded")
        load(brc[:, 0:1], bass.AP(a["br"].tensor, 0, [[0, P], [1, 1]]), "rowb_loaded")
        sp.wait_ge(sem("scattered"), 16 * EC)
        sp.wait_ge(sem("rows1_ready"), T)
        for layer in range(3):
            base = layer * T
            def fetch(t, s):
                sp.dma_start(ring[s], counts_dram[t].rearrange("p (t q) -> p t q", t=T)).then_inc(
                    sem(f"ring_loaded{s}"), 16)
            for s in range(RING):
                if layer:
                    sp.wait_ge(sem("agg_done"), base)
                fetch(s, s)
            with sp.Fori(0, 5) as i:
                for s in range(RING):
                    sp.wait_ge(sem("agg_done"), i * RING + (base + s + 1))
                    fetch(i * RING + (RING + s), s)
            sp.wait_ge(sem("agg_done"), base + T - RING)
            fetch(T - 1, 0)
            if layer == 1:
                sp.wait_ge(sem("h2_done"), T)
                load(f1, a["f1"].rearrange("(k p) n -> p k n", p=128), "ffnw_loaded")
                load(f2, a["f2"].rearrange("(k p) n -> p k n", p=128), "ffnw_loaded")
        sp.wait_ge(sem("w_done"), T)
        sp.wait_ge(sem("agg_done"), 3 * T)
        sp.dma_start(w_dram.rearrange("(p t) -> p t", t=T), wv).then_inc(sem("w_stored"), 16)
        sp.wait_ge(sem("w_stored"), 16)
        sp.dma_start(wall, bass.AP(w_dram.tensor, 0, [[0, P], [1, N]])).then_inc(sem("wall_loaded"), 16)
        od = out.rearrange("(p t) d -> p t d", t=T)
        with sp.Fori(0, NC) as i:
            sp.wait_ge(sem("final_done"), i * G + G)
            sp.dma_start(od[:, bass.ds(i * G, G), :], accv[:, bass.ds(i * G, G), :]).then_inc(sem("stored"), 16)
        sp.wait_ge(sem("stored"), 16 * NC)

    @block.gpsimd
    def _(pool):
        done = Steps(pool, sem("pool_steps"))
        pool.memset(wb[:P, 0:3072], 0.0).then_inc(sem("zi_ready"), 1)
        pool.memset(eps, EPS).then_inc(sem("eps_ready"), 1)
        done.did(pool.memset(pool_pause, 0.0))
        pool.memset(wp[:, :, :], 0.0).then_inc(sem("blocks_cleared"), 1)
        done.did(pool.memset(ident[:, :], 0.0))
        done.did(pool.memset(ones[:, :], 1.0))
        done.did(pool.memset(kones[:, :], 0.0))
        done.settle()
        pool.affine_select(out=ident[:, :], in_=ident[:, :], compare_op=ALU.not_equal, fill=1.0, base=0,
                           pattern=[[-1, 128]], channel_multiplier=1).then_inc(sem("ident_ready"), 1)
        pool.wait_ge(sem("ident_ready"), 1)
        for b in range(4):
            done.did(pool.memset(kones[32 * b:32 * b + 32, 32 * b:32 * b + 32], 1.0))
            done.settle()
        pool.iota(iop[:, 0:P], pattern=[[1, P]], base=0, channel_multiplier=0,
                  allow_small_or_imprecise_dtypes=True).then_inc(sem("ident_ready"), 1)
        pool.wait_ge(sem("ident_ready"), 2)
        pool.memset(free(zT, P * G, [[NC * CW, 2], [CW, NC], [1, 1]]), 0.0).then_inc(sem("ident_ready"), 1)
        pool.wait_ge(sem("ident_ready"), 3)
        pool.wait_ge(sem("zi_ready"), 1)
        pool.tensor_copy(zi[:, (T - 1) * P:T * P], ident[:P, 0:P]).then_inc(sem("zi_ready"), 1)
        pool.wait_ge(sem("counts_cleared"), 16 * T)
        pool.wait_ge(sem("edges_ready"), 1)
        cells = counts_dram.rearrange("t p (n o) -> (t p n) o", o=1)
        with pool.Fori(0, EC // SB) as i:
            at_j = pool.snap(i * SB)
            done.enter(i, 2)
            pool.wait_ge(sem("scattered"), i * (16 * SB))
            done.settle()
            done.did(pool.tensor_tensor(pool_pause, pool_pause, pool_pause, ALU.add))
            pool.tensor_copy(sidx, eidx[:, bass.ds(at_j, SB)]).then_inc(sem("staged"), 1)
            pool.tensor_copy(svalue[:, 0:SB], evalue[:, bass.ds(at_j, SB)]).then_inc(sem("staged"), 1)
            pool.wait_ge(sem("staged"), i * 2 + 2)
            done.settle()
            done.did(pool.tensor_tensor(pool_pause, pool_pause, pool_pause, ALU.add))
            for j in range(SB):
                pool.indirect_dma_start(cells, bass.IndirectOffsetOnAxis(ap=sidx[:, j:j + 1], axis=0),
                                        svalue[:, j:j + 1], None, bounds_check=N * N - 1,
                                        oob_is_err=False).then_inc(sem("scattered"), 16)
            done.leave(EC // SB)
        pool.wait_ge(sem("k_done"), 4 * NC)
        pool.memset(tri[:, :], 0.0).then_inc(sem("tri"), 1)
        pool.wait_ge(sem("tri"), 1)
        pool.affine_select(out=tri[:, :], in_=tri[:, :], compare_op=ALU.is_ge, fill=1.0, base=0,
                           pattern=[[-1, 128]], channel_multiplier=1).then_inc(sem("tri"), 1)
        pool.wait_ge(sem("rows1_ready"), T)
        pool.wait_ge(sem("scattered"), 16 * EC)
        pool.memset(free(nT, P * G, [[CW, 2], [1, 1]]), 0.0).then_inc(sem("npad_done"), 1)
        with pool.Fori(0, NC) as i:
            first = pool.snap(i * G)
            pool.wait_ge(sem("xn2_done"), i * G + G)
            pool.wait_ge(sem("trn_done"), i)
            done.enter(i, 1)
            done.settle()
            done.did(pool.tensor_tensor(pool_pause, pool_pause, pool_pause, ALU.add))
            pool.tensor_copy(stage, xn2[:, bass.ds(first, G), :]).then_inc(sem("stage_done"), 1)
            done.leave(NC)

    def edge_keys(dve, done, key, keep):
        done.did(dve.tensor_copy(esrc if keep else key, esrc_i))
        done.did(dve.tensor_copy(edt, edst_i))
        done.settle()
        done.did(dve.tensor_scalar(edp, edt, 1.0 / T, -0.48, ALU.mult, ALU.add))
        done.settle()
        done.did(dve.tensor_scalar(edp, edp, ROUND, ROUND, ALU.add, ALU.subtract))
        done.settle()
        done.did(dve.scalar_tensor_tensor(out=edt, in0=edp, scalar=-float(T), in1=edt, op0=ALU.mult, op1=ALU.add))
        done.settle()
        done.did(dve.scalar_tensor_tensor(out=key, in0=esrc if keep else key, scalar=float(P), in1=edp,
                                          op0=ALU.mult, op1=ALU.add))
        done.settle()
        done.did(dve.scalar_tensor_tensor(out=key, in0=edt, scalar=float(P * N), in1=key,
                                          op0=ALU.mult, op1=ALU.add))
        done.settle()

    KEY_STEPS = 7

    def count_equal(dve, done, other, shift, into, lo, tmp):
        mine = free(ekey, HALO + lo, [[1, EB], [0, HALO]])
        theirs = free(other, HALO + lo + shift, [[1, EB], [1, HALO]])
        done.did(dve.tensor_tensor(eq, mine, theirs, ALU.is_equal))
        done.settle()
        done.did(dve.tensor_reduce(tmp, eq, AX, ALU.add))
        done.settle()

    @block.vector
    def _(dve):
        done = Steps(dve, sem("dve_steps"))

        def layernorm_stats(src, width, n, t):
            parts = max(1, width // 512)
            for h in range(parts):
                done.did(dve.bn_stats(st2[:, h, :], src[:, h * 512:(h + 1) * 512] if parts > 1 else src))
            done.settle()
            done.did(dve.memset(pause, 0.0))
            dve.bn_aggr(mv2, st2[:, 0:parts, :]).then_inc(sem(f"var{n}_done"), 1)
            dve.wait_ge(sem(f"root{n}_done"), t + 1)
            done.did(dve.reciprocal(rs2, root2))
            done.settle()

        dve.wait_ge(sem("edges_loaded"), 32)
        edge_keys(dve, done, ekey, True)
        dstf = wkey
        done.did(dve.tensor_copy(dstf, edst_i))
        done.settle()
        mid, nxt, far_ = (free(dstf, HALO + s, [[1, EC]]) for s in (0, 1, HALO))
        done.did(dve.tensor_tensor(fwd, mid, nxt, ALU.is_gt))
        done.did(dve.tensor_tensor(bwd, mid, far_, ALU.is_equal))
        done.settle()
        done.did(dve.tensor_tensor(fwd, fwd, bwd, ALU.max))
        done.settle()
        dve.tensor_reduce(flagf[:P], fwd, AX, ALU.max).then_inc(sem("flag_part"), 1)
        dve.wait_ge(sem("flag_sum"), 1)
        done.did(dve.tensor_scalar(flagf[0:1], bank(7, 1, 1), 1.0, None, ALU.min))
        done.settle()
        dve.tensor_copy(flagi[0:1, 0:1], flagf[0:1]).then_inc(sem("flag_ready"), 1)
        def near(b):
            count_equal(dve, done, ekey, 1, fwd, b, free(fwd, b, [[1, EB]]))
            count_equal(dve, done, ekey, -HALO, bwd, b, free(bwd, b, [[1, EB]]))
        with dve.Fori(0, EC // EB) as i:
            done.enter(i, 4)
            near(i * EB)
            done.leave(EC // EB)
        dve.wait_ge(sem("ident_ready"), 3)
        with dve.Fori(0, EC // EB) as i:
            dve.wait_ge(sem("degree_used"), i)
            dve.tensor_tensor(ohp, free(edp, HALO + i * EB, [[1, EB], [0, P]]), free(iop, 0, [[0, EB], [1, P]]),
                              ALU.is_equal)
            dve.tensor_tensor(oht, free(edt, HALO + i * EB, [[1, EB], [0, T]]), free(iop, 0, [[0, EB], [1, T]]),
                              ALU.is_equal).then_inc(sem("onehot_done"), 1)
        dve.wait_ge(sem("onehot_done"), EC // EB)
        done.did(dve.scalar_tensor_tensor(out=edt, in0=edp, scalar=float(T), in1=edt, op0=ALU.mult, op1=ALU.add))
        done.settle()
        done.did(dve.tensor_tensor(edp, edt, esrc, ALU.is_equal))
        done.settle()
        dve.wait_ge(sem("flag_ready"), 1)
        far = dve.value_load(flagi[0:1, 0:1], min_val=0, max_val=1)
        self_ = evalue[:, 0:EC]
        done.did(dve.tensor_copy(self_, free(edp, HALO, [[1, EC]])))
        done.settle()
        with dve.If(far > 0):
            with dve.Fori(1, NWIN) as w:
                for side in (0, 1):
                    fs = sem("far_steps")
                    per = KEY_STEPS + 3 * (EC // EB)
                    inner = Steps(dve, fs)
                    inner.base = w * (2 * per) + (side - 2) * per
                    dve.wait_ge(sem("window_loaded"), w * 64 + (32 * side - 32))
                    edge_keys(dve, inner, wkey, False)
                    into = fwd if side == 0 else bwd
                    for b in range(0, EC, EB):
                        part = sqjunk[:, 0:EB]
                        count_equal(dve, inner, wkey, 1 if side == 0 else -HALO, None, b, part)
                        inner.did(dve.tensor_tensor(free(into, b, [[1, EB]]), free(into, b, [[1, EB]]), part,
                                                    ALU.add))
                        inner.settle()
                    assert inner.k == per
                    dve.memset(sqjunk[:, 0:1], 0.0).then_inc(sem("window_used"), 1)
        done.did(dve.scalar_tensor_tensor(out=bwd, in0=bwd, scalar=2.0e7, in1=free(ekey, HALO, [[1, EC]]),
                                          op0=ALU.mult, op1=ALU.add))
        done.did(dve.tensor_scalar(fwd, fwd, 1.0, None, ALU.add))
        done.settle()
        done.did(dve.tensor_scalar(bwd, bwd, 2.0e7, None, ALU.min))
        done.did(dve.tensor_tensor(evalue[:, 0:EC], fwd, self_, ALU.add))
        done.settle()
        dve.tensor_copy(eidx, bwd).then_inc(sem("edges_ready"), 1)
        dve.wait_ge(sem("x_loaded"), 16)
        for t in range(T):
            done.did(dve.bn_stats(stats[:, t, :], x_rows[:, t, :]))
        done.settle()
        for t in range(T):
            done.did(dve.bn_aggr(mv[:, t, :], stats[:, t:t + 1, :]))
        done.settle()
        var = mv[:, :, 1:2].rearrange("p t o -> p (t o)")
        dve.tensor_scalar(ca, var, EPS, None, ALU.add).then_inc(sem("xvar_done"), 1)
        dve.wait_ge(sem("xroot_done"), 1)
        done.did(dve.reciprocal(rstd, rstd))
        dve.wait_ge(sem("xvar_done"), 1)
        done.did(dve.reciprocal(cb, ca))
        done.settle()
        dve.tensor_tensor(cb, var, cb, ALU.mult).then_inc(sem("ratio2_done"), 1)
        for t in range(T):
            done.did(dve.tensor_scalar(x_rows[:, t, :], x_rows[:, t, :], mv[:, t, 0:1], rstd[:, t:t + 1],
                                       ALU.subtract, ALU.mult))
        dve.wait_ge(sem("norm_done"), 1)
        done.did(dve.tensor_scalar(ca, cb, BALL, None, ALU.min))
        done.did(dve.tensor_scalar(cb, cb, 1e-15, None, ALU.max))
        done.settle()
        done.did(dve.tensor_scalar(cc, ca, 1.0, None, ALU.add))
        done.did(dve.tensor_scalar(cd, ca, -1.0, 1.0, ALU.mult, ALU.add))
        done.settle()
        done.did(dve.reciprocal(cd, cd))
        done.settle()
        dve.tensor_tensor(cc, cc, cd, ALU.mult).then_inc(sem("ratio_done"), 1)
        done.did(dve.tensor_tensor(dx, ca, ca, ALU.mult))
        done.settle()
        done.did(dve.tensor_scalar(rstd, dx, 1.0 / 9.0, 1.0 / 7.0, ALU.mult, ALU.add))
        done.settle()
        for c in (1.0 / 5.0, 1.0 / 3.0, 1.0):
            done.did(dve.tensor_tensor(rstd, rstd, dx, ALU.mult))
            done.settle()
            done.did(dve.tensor_scalar(rstd, rstd, c, None, ALU.add))
            done.settle()
        dve.wait_ge(sem("log_done"), 1)
        done.did(dve.tensor_scalar(cd, cd, 0.5, None, ALU.mult))
        done.did(dve.reciprocal(cb, cb))
        done.settle()
        done.did(dve.tensor_tensor(cd, cd, cb, ALU.mult))
        done.did(dve.tensor_scalar(cc, ca, 0.1, None, ALU.is_lt))
        done.settle()
        done.did(dve.tensor_tensor(rstd, rstd, cd, ALU.subtract))
        done.settle()
        done.did(dve.tensor_tensor(rstd, rstd, cc, ALU.mult))
        done.settle()
        done.did(dve.tensor_tensor(cd, rstd, cd, ALU.add))
        done.settle()
        for t in range(T):
            dve.tensor_scalar(zv[:, t, :], x_rows[:, t, :], cd[:, t:t + 1], None, ALU.mult).then_inc(
                sem("z_done"), 1)
        dve.wait_ge(sem("degree_done"), 1)
        dve.tensor_scalar(dinv, bank(7, P, T), 1.0, None, ALU.add).then_inc(sem("dinv_read"), 1)
        dve.wait_ge(sem("droot_done"), 1)
        done.did(dve.reciprocal(dinv, dinv))
        done.settle()
        dve.wait_ge(sem("zrow_done"), 1)
        dve.tensor_scalar(nzrow, zrow, -1.0 / N, None, ALU.mult).then_inc(sem("nzrow_done"), 1)
        dve.wait_ge(sem("gram_done"), 1)
        done.did(dve.tensor_copy(zcol, bank(2, 128, 2)))
        dve.tensor_copy(gram, psum[:, 0:2, 0:D]).then_inc(sem("gram_copied"), 1)
        done.settle()
        dve.wait_ge(sem("mixw_loaded"), 16 * 10)
        dve.wait_ge(sem("gw_done"), 1)
        for k in range(2):
            done.did(dve.tensor_tensor(gw[:, k, 0:512], bank(4 + 2 * k, 128, 512), wq[:, k, 0:512], ALU.mult))
            last = dve.tensor_tensor(gw[:, k, 512:768], bank(5 + 2 * k, 128, 256), wq[:, k, 512:768], ALU.mult)
            last.then_inc(sem("wgw_done"), 1)
        for m in range(NT):
            last = dve.tensor_scalar(wp[:, m, :], wp[:, m, :], wdw[:, m:m + 1], None, ALU.mult)
        last.then_inc(sem("wp_done"), 1)
        dve.wait_ge(sem("bnsum_done"), 1)
        dve.tensor_scalar(tmp6, bank(3, 128, NT), 1.0 / N, None, ALU.mult).then_inc(sem("bnvar_done"), 1)
        done.did(dve.tensor_scalar(bnt, bank(3, 128, NT, 16), 1.0 / N, None, ALU.mult))
        done.settle()
        dve.wait_ge(sem("bnroot_done"), 1)
        done.did(dve.reciprocal(tmp6, tmp6))
        done.settle()
        done.did(dve.tensor_tensor(bns, tmp6, bng, ALU.mult))
        done.settle()
        done.did(dve.tensor_tensor(bnt, bnt, bns, ALU.mult))
        done.settle()
        dve.tensor_tensor(bnt, bnb, bnt, ALU.subtract).then_inc(sem("bn_done"), 1)
        done.did(dve.tensor_scalar(dx, dinv, X_SCALE, None, ALU.mult))
        done.did(dve.tensor_scalar(ca, dinv, 1.0 / X_SCALE, None, ALU.mult))
        done.settle()
        dve.wait_ge(sem("bounds_read"), 1)
        for L, width in ((0, D1), (1, D2)):
            o = 3 * L
            done.did(dve.tensor_tensor(bound[:, o:o + 1], bound[:, o:o + 1], bound[:, o + 2:o + 3], ALU.mult))
            done.settle()
            done.did(dve.scalar_tensor_tensor(out=bound[:, o:o + 1], in0=bound[:, o + 1:o + 2],
                                              scalar=float(width) ** 0.5, in1=bound[:, o:o + 1],
                                              op0=ALU.mult, op1=ALU.add))
            done.settle()
            done.did(dve.tensor_scalar(bound[:, o:o + 1], bound[:, o:o + 1], 1e-20, 1.0 / F16_TOP,
                                       ALU.max, ALU.mult))
            done.settle()
            done.did(dve.reciprocal(bound[:, 6 + L:7 + L], bound[:, o:o + 1]))
            done.settle()
            di, do = (d2in, d2out) if L == 0 else (d3in, d3out)
            done.did(dve.tensor_scalar(di, dinv, bound[:P, 6 + L:7 + L], None, ALU.mult))
            done.did(dve.tensor_scalar(do, dinv, bound[:P, o:o + 1], None, ALU.mult))
            done.settle()
        MIX = 14
        with dve.Fori(0, NC) as i:
            done.enter(i, MIX)
            for m in range(NT):
                dve.wait_ge(sem("s_done"), i * NT + (m + 1))
                if m == 0:
                    dve.wait_ge(sem("res_done"), i * G)
                if m < 4:
                    dve.tensor_scalar(halves(sT[:, m, :]), pair(m % 2), 0.0, None, ALU.max).then_inc(
                        sem("s_evac"), 1)
                else:
                    dve.tensor_copy(halves(sT[:, m, :]), pair(m % 2)).then_inc(sem("s_evac"), 1)
            dve.wait_ge(sem("nc_done"), i * 12 + 12)
            dve.tensor_scalar(halves(umax), pair(2), 1.0 / RMAX ** 2, 1.0, ALU.mult, ALU.max).then_inc(
                sem("u_done"), 1)
            dve.wait_ge(sem("veps_done"), i + 1)
            for n in range(4):
                src, half = (hT, n) if n < 2 else (sT, n - 2)
                q, v = src[:, half, :], src[:, 4 + half, :]
                dve.wait_ge(sem("k_done"), i * 4 + (n + 1))
                dve.tensor_tensor(halves(q), pair(3), halves(q), ALU.mult).then_inc(sem("qk_done"), 1)
                done.did(dve.tensor_tensor(tdiv, v, veps, ALU.add))
                done.settle()
                done.did(dve.reciprocal(tdiv, tdiv))
                done.settle()
                done.did(dve.tensor_tensor(tdiv, tdiv, v, ALU.mult))
                done.settle()
                dve.wait_ge(sem("qk_done"), i * 4 + (n + 1))
                dve.tensor_tensor(q, q, tdiv, ALU.mult).then_inc(sem("o_done"), 1)
                dve.wait_ge(sem("o_done"), i * 4 + (n + 1))
            dve.wait_ge(sem("ocol_read"), i + 1)
            dve.tensor_copy(ucol, bank(6, P, G)).then_inc(sem("ucol_read"), 1)
            dve.wait_ge(sem("ucol_read"), i + 1)
            done.did(dve.tensor_tensor(ocol, ocol, ucol, ALU.max))
            done.settle()
            done.did(dve.reciprocal(ocol, ocol))
            done.settle()
            for j in range(G):
                t = i * G + j
                dve.wait_ge(sem("res_done"), t + 1)
                dve.scalar_tensor_tensor(out=accv[:, t, :], in0=bank(4 + j % 2, P, D), scalar=ocol[:, j:j + 1],
                                         in1=bresr, op0=ALU.mult, op1=ALU.add).then_inc(sem("ft_done"), 1)
            done.leave(NC)
        dve.wait_ge(sem("n4root_done"), 1)
        dve.tensor_scalar(n4, n4, 1e-15, None, ALU.max).then_inc(sem("n4_ready"), 1)
        dve.wait_ge(sem("tanh_done"), 1)
        done.did(dve.tensor_scalar(f4, f4, BALL, None, ALU.min))
        done.did(dve.reciprocal(n4, n4))
        done.settle()
        done.did(dve.tensor_tensor(f4, f4, n4, ALU.mult))
        done.settle()
        with dve.Fori(0, NC) as i:
            dve.wait_ge(sem("xbuf_loaded"), i * 16 + 16)
            for j in range(G):
                t = i * G + j
                dve.scalar_tensor_tensor(out=accv[:, t, :], in0=accv[:, t, :], scalar=f4[:, bass.ds(t, 1)],
                                         in1=xbuf[:, j, :], op0=ALU.mult, op1=ALU.add).then_inc(
                    sem("fx_done"), 1)
        dve.wait_ge(sem("fx_done"), T)
        for t in range(T):
            if t >= G:
                dve.wait_ge(sem("rows1_ready"), t - G + 1)
            done.did(dve.tensor_scalar(xbuf[:, t % G, :], x_rows[:, t, :], dx[:, t:t + 1], None, ALU.mult))
            done.settle()
            done.did(dve.tensor_copy(x2[:, t, 0, :], xbuf[:, t % G, :]))
            done.settle()
            dve.tensor_tensor(x2[:, t, 1, :], xbuf[:, t % G, :], x2[:, t, 0, :], ALU.subtract).then_inc(
                sem("rows1_ready"), 1)

        dve.wait_ge(sem("rowb_loaded"), 16 * 8)
        dve.wait_ge(sem("scattered"), 16 * EC)

        def rows_out(t, width, tile, scale, layer):
            dve.wait_ge(sem(f"h{layer}_done"), t + 1)
            dve.wait_ge(sem(f"lo{layer}_done"), t)
            dve.tensor_scalar(hbuf[:, 0:width], bank(7, P, width), scale[:, bass.ds(t, 1)], None,
                              ALU.mult).then_inc(sem(f"hbuf{layer}_done"), 1)
            dve.wait_ge(sem(f"hi{layer}_done"), t + 1)
            dve.tensor_tensor(tile[:, t, 1, :], hbuf[:, 0:width], tile[:, t, 0, :], ALU.subtract).then_inc(
                sem(f"lo{layer}_done"), 1)

        def normalise(t, buf, width, relu, xhat):
            dve.wait_ge(sem(relu), t + 1)
            layernorm_stats(buf, width, 1 if width == D1 else 2, t)
            dve.tensor_scalar(buf, buf, mv2[:, 0:1], rs2, ALU.subtract, ALU.mult).then_inc(sem(xhat), 1)

        def step1(t, b, first=False, last=False):
            if not last:
                dve.wait_ge(sem("yhi_done"), t + 1)
                dve.tensor_tensor(ysum, bank(b, P, D, D), yhi, ALU.add).then_inc(sem("y_done"), 1)
                dve.wait_ge(sem("p1_done"), t + 1)
                dve.scalar_tensor_tensor(out=pre[b].rearrange("p (h n) -> p h n", h=2), in0=psum[:P, 3:5, :],
                                         scalar=ca[:, bass.ds(t, 1)],
                                         in1=b1r.rearrange("p (h n) -> p h n", h=2), op0=ALU.mult,
                                         op1=ALU.add).then_inc(sem("pre1_done"), 1)
                normalise(t, pre[b], D1, "relu1_done", "xhat1_done")
            if not first:
                rows_out(t - 1, D2, h2in, d2in, 2)

        step1(0, 0, first=True)
        with dve.Fori(0, 6) as i:
            done.enter(i, 4 * 4)
            for k in range(1, 5):
                step1(i * 4 + k, k % 2)
            done.leave(6)
        step1(T, T % 2, last=True)

        def step2(t, b, first=False, last=False):
            if not last:
                dve.wait_ge(sem("agg_done"), t + (T + 1))
                dve.scalar_tensor_tensor(out=pre[b][:, 0:D2], in0=bank(b, P, D2), scalar=d2out[:, bass.ds(t, 1)],
                                         in1=b2r, op0=ALU.mult, op1=ALU.add).then_inc(sem("pre2_done"), 1)
                normalise(t, pre[b][:, 0:D2], D2, "relu2_done", "xhat2_done")
            if not first:
                rows_out(t - 1, D3, x2, d3in, 3)

        step2(0, 0, first=True)
        with dve.Fori(0, 6) as i:
            done.enter(i, 3 * 4)
            for k in range(1, 5):
                step2(i * 4 + k, k % 2)
            done.leave(6)
        step2(T, T % 2, last=True)

        def step3(t, b):
            buf = pre[0][:, 0:D]
            dve.wait_ge(sem("agg_done"), t + (2 * T + 1))
            s = d3out[:, bass.ds(t, 1)]
            done.did(dve.scalar_tensor_tensor(out=buf, in0=bank(b, P, D), scalar=s, in1=b3r, op0=ALU.mult,
                                              op1=ALU.add))
            done.settle()
            dve.scalar_tensor_tensor(out=buf, in0=bank(b, P, D, D), scalar=s, in1=buf, op0=ALU.mult,
                                     op1=ALU.add).then_inc(sem("pre3_done"), 1)
            dve.wait_ge(sem("pre3_done"), t + 1)
            done.did(dve.tensor_scalar(buf, buf, 0.0, None, ALU.max))
            done.settle()
            layernorm_stats(buf, D, 3, t)
            done.did(dve.tensor_scalar(buf, buf, mv2[:, 0:1], rs2, ALU.subtract, ALU.mult))
            done.settle()
            done.did(dve.tensor_tensor(buf, buf, g3r, ALU.mult))
            done.settle()
            done.did(dve.tensor_tensor(buf, buf, be3r, ALU.add))
            done.settle()
            summed = pre[1][:, 0:D]
            done.did(dve.tensor_tensor(summed, accv[:, t, :], buf, ALU.add))
            done.settle()
            dve.tensor_scalar(accv[:, t, :], summed, 1.0, None, ALU.mult).then_inc(sem("sum_done"), 1)
            layernorm_stats(summed, D, 4, t)
            dve.tensor_scalar(xn2[:, t, :], summed, mv2[:, 0:1], rs2, ALU.subtract, ALU.mult).then_inc(
                sem("xn2_done"), 1)
            dve.wait_ge(sem("xn2_done"), t + 1)
            done.did(dve.tensor_tensor(post, xn2[:, t, :], wrr, ALU.mult))
            done.settle()
            dve.tensor_reduce(wv[:, bass.ds(t, 1)], post, AX, ALU.add).then_inc(sem("wdot_done"), 1)
            dve.wait_ge(sem("wdot_done"), t + 1)
            dve.tensor_scalar(wv[:, bass.ds(t, 1)], wv[:, bass.ds(t, 1)], brc[:, 0:1], None, ALU.add).then_inc(
                sem("w_done"), 1)

        STEP3 = 13
        step3(0, 0)
        with dve.Fori(0, 6) as i:
            done.enter(i, STEP3 * 4)
            for k in range(1, 5):
                step3(i * 4 + k, k % 2)
            done.leave(6)
        dve.wait_ge(sem("w_done"), T)
        dve.tensor_scalar(pref, wv, -1.0, None, ALU.mult).then_inc(sem("negw_done"), 1)
        dve.wait_ge(sem("wall_loaded"), 16)
        with dve.Fori(0, NC) as i:
            done.enter(i, G)
            for j in range(G):
                t = i * G + j
                done.settle()
                done.did(dve.tensor_scalar(gtjunk, wall, wv[:, bass.ds(t, 1)], 0.0, ALU.is_gt, ALU.add,
                                           accum_out=gt[:, bass.ds(t, 1)]))
            for j in range(G):
                t = i * G + j
                dve.wait_ge(sem("yffn_done"), t + 1)
                dve.tensor_tensor(x_rows[:, t, :], bank(3 - j % 2, P, D), fb2r, ALU.add).then_inc(
                    sem("yffn_evac"), 1)
            done.leave(NC)
        done.settle()
        dve.wait_ge(sem("sign_done"), T)
        done.did(dve.tensor_tensor(sg, sg, gt, ALU.subtract))
        done.did(dve.tensor_scalar(cc, gt, float(KSEL), None, ALU.is_lt))
        done.settle()
        done.did(dve.tensor_scalar(sg, sg, float(N), float(KSEL), ALU.add, ALU.is_gt))
        done.settle()
        done.did(dve.tensor_tensor(bnd, sg, cc, ALU.mult))
        done.did(dve.memset(cd, 0.0))
        done.settle()
        dve.tensor_tensor_scan(pref, bnd, cd, 0.0, ALU.add, ALU.add).then_inc(sem("prefix_done"), 1)
        dve.wait_ge(sem("before_done"), 1)
        done.did(dve.tensor_tensor(pref, pref, bnd, ALU.subtract))
        done.did(dve.tensor_copy(n4[:, 0:1], bank(0, P, 1)))
        done.settle()
        done.did(dve.tensor_scalar(pref, pref, n4[:, 0:1], None, ALU.add))
        done.settle()
        done.did(dve.tensor_tensor(pref, pref, gt, ALU.add))
        done.settle()
        done.did(dve.tensor_scalar(pref, pref, float(KSEL), None, ALU.is_lt))
        done.did(dve.tensor_scalar(cd, bnd, -1.0, 1.0, ALU.mult, ALU.add))
        done.settle()
        done.did(dve.tensor_tensor(pref, pref, bnd, ALU.mult))
        done.did(dve.tensor_tensor(cd, cd, cc, ALU.mult))
        done.settle()
        done.did(dve.tensor_tensor(pref, pref, cd, ALU.add))
        done.settle()
        done.did(dve.tensor_tensor(wsel, pref, wv, ALU.mult))
        done.settle()
        dve.wait_ge(sem("yffn_evac"), T)
        for t in range(T):
            done.did(dve.scalar_tensor_tensor(out=x_rows[:, t, :], in0=x_rows[:, t, :], scalar=wsel[:, t:t + 1],
                                              in1=xn2[:, t, :], op0=ALU.mult, op1=ALU.add))
            done.settle()
            dve.tensor_tensor(accv[:, t, :], accv[:, t, :], x_rows[:, t, :], ALU.add).then_inc(
                sem("final_done"), 1)

    @block.scalar
    def _(act):
        done = Steps(act, sem("act_steps"))
        act.wait_ge(sem("eps_ready"), 1)
        act.wait_ge(sem("xvar_done"), 1)
        act.activation(rstd, ca, ACT.Sqrt).then_inc(sem("xroot_done"), 1)
        act.wait_ge(sem("ratio2_done"), 1)
        act.activation(cb, cb, ACT.Sqrt, scale=float(D)).then_inc(sem("norm_done"), 1)
        act.wait_ge(sem("ratio_done"), 1)
        act.activation(cd, cc, ACT.Ln).then_inc(sem("log_done"), 1)
        act.wait_ge(sem("dinv_read"), 1)
        act.activation(dinv, dinv, ACT.Sqrt).then_inc(sem("droot_done"), 1)
        act.wait_ge(sem("ident_ready"), 3)
        for c in range(NC):
            for k in range(2):
                act.wait_ge(sem("trz_done"), 3 * c + k + 1)
                act.copy(zT[:, k, c * CW:c * CW + 4 * P], bank(4 + k, 128, 4 * P)).then_inc(sem("zT_done"), 1)
            act.wait_ge(sem("trz_done"), 3 * c + 3)
            act.copy(zT[:, :, c * CW + 4 * P:c * CW + 5 * P],
                     bank(6, 128, 2 * P).rearrange("p (k q) -> p k q", k=2)).then_inc(sem("zT_done"), 1)
        act.wait_ge(sem("zsum_done"), 1)
        act.copy(zrow, bank(3, 1, D)).then_inc(sem("zrow_done"), 1)
        act.wait_ge(sem("layerw_loaded"), 48)
        act.wait_ge(sem("cols_loaded"), 80)
        junk = sqw
        for L, (w, nk, width, g, be) in enumerate(((w2, 8, D2, g1c, be1c), (w3, 4, D3, g2c, be2c))):
            o = 8 * L
            for k in range(nk):
                done.settle()
                done.did(act.activation(junk[:, 0:width], w[:, k, :], ACT.Square,
                                        accum_out=ssw[:, o + k:o + k + 1]))
                done.settle()
                done.did(act.activation(junk[:, 0:width], w[:, k, :], ACT.Square, scale=g[:, k:k + 1],
                                        accum_out=ssg[:, o + k:o + k + 1]))
            done.settle()
            last = act.activation(ssb[:, o:o + nk], be, ACT.Square)
            last.then_inc(sem("squares_done"), 1)

        act.wait_ge(sem("bnvar_done"), 1)
        act.activation(tmp6, tmp6, ACT.Sqrt, bias=eps).then_inc(sem("bnroot_done"), 1)
        act.wait_ge(sem("bounds_done"), 1)
        act.activation(bound[:, 0:6], bank(6, 128, 6, 16), ACT.Sqrt).then_inc(sem("bounds_read"), 1)
        act.wait_ge(sem("bn_done"), 1)
        act.preload_act_table(ACT.Sqrt)
        with act.Fori(0, NC) as i:
            def square(dst_slot, src, name, n, c):
                act.wait_ge(sem("nc_done"), i * 12 + c - 2 if c >= 2 else i * 12)
                act.activation(dst_slot, src, ACT.Square).then_inc(sem("sq_done"), 1)
            for m in range(NT):
                act.wait_ge(sem("qkv_done"), i * NT + (m + 1))
                if m == 0:
                    act.wait_ge(sem("res_done"), i * G)
                act.activation(halves(hT[:, m, :]), pair(m % 2), ACT.Relu, scale=bns[:, m:m + 1],
                               bias=bnt[:, m:m + 1]).then_inc(sem("h_done"), 1)
                act.wait_ge(sem("h_done"), i * NT + (m + 1))
                square(sq[:, m % 3, :], hT[:, m, :], "h", m, m)
            for m in range(NT):
                act.wait_ge(sem("s_evac"), i * NT + (m + 1))
                square(halves(sq[:, m % 3, :]), pair(m % 2), "s", m, NT + m)
            act.wait_ge(sem("u_done"), i + 1)
            act.activation(veps, umax, ACT.Sqrt, scale=1e-30).then_inc(sem("veps_done"), 1)
            for n in range(4):
                act.wait_ge(sem("o_done"), i * 4 + (n + 1))
                src, half = (hT, n) if n < 2 else (sT, n - 2)
                act.activation(src[:, 2 + half, :], src[:, half, :], ACT.Square).then_inc(sem("osq_done"), 1)
            act.wait_ge(sem("cols_done"), i + 1)
            act.activation(ocol, bank(6, P, G, 16), ACT.Sqrt, scale=1.0 / RMAX ** 2).then_inc(sem("ocol_read"), 1)
            for j in range(G):
                t = i * G + j
                act.wait_ge(sem("ft_done"), t + 1)
                act.wait_ge(sem("n4_done"), t)
                act.activation(sqjunk, accv[:, t, :], ACT.Square, accum_out=n4[:, bass.ds(t, 1)]).then_inc(
                    sem("n4_done"), 1)
        act.wait_ge(sem("n4_done"), T)
        act.activation(n4, n4, ACT.Sqrt).then_inc(sem("n4root_done"), 1)
        act.wait_ge(sem("n4_ready"), 1)
        act.activation(f4, n4, ACT.Tanh).then_inc(sem("tanh_done"), 1)
        act.preload_act_table(ACT.Sqrt)

        def turn_in(t, k_tiles, g, be, layer):
            act.wait_ge(sem(f"trx{layer}_done"), t + 1)
            act.wait_ge(sem(f"h{layer}_done"), t)
            for k in range(k_tiles):
                last = act.activation(xT[:, k, :], bank(5 + k // 4, 128, P, (k % 4) * P), ACT.Identity,
                                      scale=g[:, k:k + 1], bias=be[:, k:k + 1])
            last.then_inc(sem(f"xT{layer}_done"), 1)

        def root(t, n):
            act.wait_ge(sem(f"var{n}_done"), t + 1)
            act.activation(root2, mv2[:, 1:2], ACT.Sqrt, bias=eps[:P]).then_inc(sem(f"root{n}_done"), 1)

        def high(t, width, tile, layer):
            act.wait_ge(sem(f"hbuf{layer}_done"), t + 1)
            act.copy(tile[:, t, 0, :], hbuf[:, 0:width]).then_inc(sem(f"hi{layer}_done"), 1)

        def step1(t, b, first=False, last=False):
            if not last:
                act.wait_ge(sem("agg_done"), t + 1)
                act.wait_ge(sem("y_done"), t)
                act.copy(yhi, bank(b, P, D)).then_inc(sem("yhi_done"), 1)
                act.wait_ge(sem("try_done"), t + 1)
                act.wait_ge(sem("p1_done"), t)
                act.copy(yT, bank(2, 128, 2 * P).rearrange("p (k q) -> p k q", k=2)).then_inc(sem("yT_done"), 1)
            if not first:
                turn_in(t - 1, 8, g1c, be1c, 2)
            if not last:
                act.wait_ge(sem("pre1_done"), t + 1)
                act.activation(pre[b], pre[b], ACT.Relu).then_inc(sem("relu1_done"), 1)
                root(t, 1)
            if not first:
                high(t - 1, D2, h2in, 2)

        act.wait_ge(sem("rows1_ready"), T)
        step1(0, 0, first=True)
        with act.Fori(0, 6) as i:
            for k in range(1, 5):
                step1(i * 4 + k, k % 2)
        step1(T, 1, last=True)

        def step2(t, b, first=False, last=False):
            if not last:
                act.wait_ge(sem("pre2_done"), t + 1)
                act.activation(pre[b][:, 0:D2], pre[b][:, 0:D2], ACT.Relu).then_inc(sem("relu2_done"), 1)
                root(t, 2)
            if not first:
                turn_in(t - 1, 4, g2c, be2c, 3)
                high(t - 1, D3, x2, 3)

        step2(0, 0, first=True)
        with act.Fori(0, 6) as i:
            for k in range(1, 5):
                step2(i * 4 + k, k % 2)
        step2(T, 1, last=True)

        with act.Fori(0, T) as t:
            root(t, 3)
            root(t, 4)

        act.wait_ge(sem("negw_done"), 1)
        act.wait_ge(sem("wall_loaded"), 16)
        act.preload_act_table(ACT.Gelu_apprx_tanh)
        with act.Fori(0, NC) as i:
            for k in range(2):
                act.wait_ge(sem("trn_done"), i + 1)
                act.wait_ge(sem("hid_done"), i * 8)
                act.copy(nT[:, k, 0:4 * P], bank(k, 128, 4 * P)).then_inc(sem("nT_done"), 1)
            act.copy(nT[:, :, 4 * P:5 * P], bank(2, 128, 2 * P).rearrange("p (k q) -> p k q", k=2)).then_inc(
                sem("nT_done"), 1)
            for m in range(8):
                act.wait_ge(sem("hid_done"), i * 8 + (m + 1))
                if m == 0:
                    act.wait_ge(sem("yffn_done"), i * G)
                act.activation(halves(gT[:, m, :]), pair(2 + m % 2), ACT.Gelu_apprx_tanh,
                               bias=fb1c[:, m:m + 1]).then_inc(sem("gelu_done"), 1)
            for j in range(G):
                t = i * G + j
                act.wait_ge(sem("sign_done"), t)
                act.activation(sgjunk, wall, ACT.Sign, bias=pref[:, bass.ds(t, 1)],
                               accum_out=sg[:, bass.ds(t, 1)]).then_inc(sem("sign_done"), 1)

    @block.tensor
    def _(pe):
        def mm(o, l, r, start, stop):
            return pe.matmul(o, l, r, start=start, stop=stop)

        pe.wait_ge(sem("ident_ready"), 3)
        pe.wait_ge(sem("flag_part"), 1)
        mm(bank(7, 1, 1), ones[:P, 0:1], flagf[:P], True, True).then_inc(sem("flag_sum"), 1)

        pe.wait_ge(sem("flag_ready"), 1)

        def degree(i, first=False):
            pe.wait_ge(sem("onehot_done"), i + 1)
            for j in range(EB):
                last = mm(bank(7, P, T), ohp[:, j, :], oht[:, j, :], first and j == 0, False)
            last.then_inc(sem("degree_used"), 1)
        degree(0, True)
        with pe.Fori(1, EC // EB - 1) as i:
            degree(i)
        pe.wait_ge(sem("onehot_done"), EC // EB)
        for j in range(EB):
            last = mm(bank(7, P, T), ohp[:, j, :], oht[:, j, :], False, j == EB - 1)
        last.then_inc(sem("degree_done"), 1)

        for c in range(NC):
            for k in range(2):
                pe.wait_ge(sem("z_done"), G * c + 4)
                pe.wait_ge(sem("zT_done"), 3 * c - 3 + k + 1 if c else 0)
                for j in range(4):
                    last = pe.transpose(bank(4 + k, 128, P, j * P), zv[:, G * c + j, k * 128:(k + 1) * 128],
                                        ident[:P, 0:P])
                last.then_inc(sem("trz_done"), 1)
            pe.wait_ge(sem("z_done"), G * c + 5)
            pe.wait_ge(sem("zT_done"), 3 * c)
            for k in range(2):
                last = pe.transpose(bank(6, 128, P, k * P), zv[:, G * c + 4, k * 128:(k + 1) * 128], ident[:P, 0:P])
            last.then_inc(sem("trz_done"), 1)
        for t in range(T):
            for m in range(2):
                mm(bank(m, 128, D), zv[:, t, m * 128:(m + 1) * 128], zv[:, t, :], t == 0, False)
            last = mm(bank(3, 1, D), ones[:P, 0:1], zv[:, t, :], t == 0, t == T - 1)
        last.then_inc(sem("zsum_done"), 1)
        pe.wait_ge(sem("nzrow_done"), 1)
        for m in range(2):
            mm(bank(m, 128, D), nzrow[:, m * 128:(m + 1) * 128], zrow, False, True)
        for k in range(2):
            last = mm(bank(2, 128, 1, k), zrow[:, k * 128:(k + 1) * 128], ones[0:1, 0:1], True, True)
        last.then_inc(sem("gram_done"), 1)
        pe.wait_ge(sem("gram_copied"), 1)
        pe.wait_ge(sem("mixw_loaded"), 16 * 10)
        pe.wait_ge(sem("zT_done"), 3 * NC)
        pe.wait_ge(sem("dinv_read"), 1)
        for m in range(2):
            for n0, n1, b in ((0, 512, 4 + 2 * m), (512, 768, 5 + 2 * m)):
                for k in range(2):
                    last = mm(bank(b, 128, n1 - n0), gram[:, k, m * 128:(m + 1) * 128], wq[:, k, n0:n1],
                              k == 0, k == 1)
        last.then_inc(sem("gw_done"), 1)
        pe.wait_ge(sem("wgw_done"), 2)
        pe.wait_ge(sem("zrow_done"), 1)
        for m in range(NT):
            for k in range(2):
                mm(bank(3, 128, 1, m), gw[:, k, m * 128:(m + 1) * 128], ones[:, 0:1], k == 0, k == 1)
            for k in range(2):
                last = mm(bank(3, 128, 1, 16 + m), wq[:, k, m * 128:(m + 1) * 128], zcol[:, k:k + 1],
                          k == 0, k == 1)
        last.then_inc(sem("bnsum_done"), 1)
        pe.wait_ge(sem("squares_done"), 2)
        n = 0
        for L, nk in ((0, 8), (1, 4)):
            for s in (ssw, ssg, ssb):
                for k in range(nk):
                    last = mm(bank(6, 128, 1, 16 + n), ones[:, :], s[:, 8 * L + k:8 * L + k + 1], k == 0, k == nk - 1)
                n += 1
        last.then_inc(sem("bounds_done"), 1)

        pe.wait_ge(sem("bn_done"), 1)
        pe.wait_ge(sem("wp_done"), 1)
        pe.wait_ge(sem("bounds_read"), 1)
        with pe.Fori(0, NC) as i:
            def norm2(c):
                pe.wait_ge(sem("sq_done"), i * 12 + (c + 1))
                for h in range(2):
                    last = mm(bank(4 + h, 128, CH), ones[:, :], sq[:, c % 3, h * CH:(h + 1) * CH], c == 0, c == 11)
                last.then_inc(sem("nc_done"), 1)

            for m in range(NT):
                if m < 2:
                    pe.wait_ge(sem("s_evac"), i * NT)
                    pe.wait_ge(sem("sq_done"), i * 12)
                else:
                    pe.wait_ge(sem("h_done"), i * NT + (m - 1))
                for k in range(2):
                    for h in range(2):
                        last = mm(bank(2 * (m % 2) + h, 128, CH), wq[:, k, m * 128:(m + 1) * 128],
                                  zT[:, k, bass.ds(i * CW + h * CH, CH)], k == 0, k == 1)
                last.then_inc(sem("qkv_done"), 1)
                if m == 2:
                    pe.wait_ge(sem("ft_done"), i * G)
                if m >= 2:
                    norm2(m - 2)
            for m in range(NT):
                if m < 2:
                    pe.wait_ge(sem("h_done"), i * NT + (m + 5))
                else:
                    pe.wait_ge(sem("s_evac"), i * NT + (m - 1))
                    pe.wait_ge(sem("sq_done"), i * 12 + (NT + m - 1))
                pe.wait_ge(sem("h_done"), i * NT + (m + 1))
                for h in range(2):
                    last = mm(bank(2 * (m % 2) + h, 128, CH), wp[:, m, :], hT[:, m, h * CH:(h + 1) * CH], True, True)
                last.then_inc(sem("s_done"), 1)
                norm2(m + 4)
            norm2(10)
            norm2(11)
            for n in range(4):
                src, half = (hT, n) if n < 2 else (sT, n - 2)
                pe.wait_ge(sem("qk_done"), i * 4 + n)
                if n == 0:
                    pe.wait_ge(sem("ucol_read"), i)
                    pe.wait_ge(sem("ocol_read"), i)
                if n == 2:
                    pe.wait_ge(sem("s_evac"), i * NT + 4)
                for h in range(2):
                    last = mm(bank(6 + h, 128, CH), kones[:, :], src[:, 2 + half, h * CH:(h + 1) * CH], True, True)
                last.then_inc(sem("k_done"), 1)
            pe.wait_ge(sem("u_done"), i + 1)
            pe.wait_ge(sem("qk_done"), i * 4 + 4)
            for j in range(G):
                mm(bank(6, P, 1, j), umax[0:1, j * P:(j + 1) * P], ones[0:1, 0:1], True, True)
            pe.wait_ge(sem("osq_done"), i * 4 + 4)
            for j in range(G):
                for n in range(4):
                    src, half = (hT, n) if n < 2 else (sT, n - 2)
                    last = mm(bank(6, P, 1, 16 + j), src[:, 2 + half, j * P:(j + 1) * P], ones[:, 0:1], n == 0, n == 3)
            last.then_inc(sem("cols_done"), 1)
            for j in range(G):
                if j >= 2:
                    pe.wait_ge(sem("ft_done"), i * G + (j - 1))
                for n in range(4):
                    src, half = (hT, n) if n < 2 else (sT, n - 2)
                    last = mm(bank(4 + j % 2, P, D), src[:, half, j * P:(j + 1) * P], wres[:, n, :], n == 0, n == 3)
                last.then_inc(sem("res_done"), 1)

        def aggregate(layer, t, slot, b, parts, visit, free_sem, free_at):
            pe.wait_ge(sem(f"ring_loaded{slot}"), visit)
            if free_at is not None:
                pe.wait_ge(sem(free_sem), free_at)
            for s in range(T):
                for h in range(len(parts)):
                    last = mm(bank(b, P, 512), ring[slot][:, s, :], parts[h](s), s == 0 and h == 0,
                              s == T - 1 and h == len(parts) - 1)
            last.then_inc(sem("agg_done"), 1)

        both = [lambda s: x2[:, s, :, :].rearrange("p h d -> p (h d)")]
        wide = [lambda s: h2in[:, s, 0, :], lambda s: h2in[:, s, 1, :]]
        SLOT0 = (T + RING - 1) // RING

        def visits(layer, slot):
            return layer * (SLOT0 if slot == 0 else SLOT0 - 1)

        def turn(t, b, k_tiles, layer):
            pe.wait_ge(sem(f"xhat{layer - 1}_done"), t + 1)
            pe.wait_ge(sem(f"xT{layer}_done"), t)
            for k in range(k_tiles):
                last = pe.transpose(bank(5 + k // 4, 128, P, (k % 4) * P), pre[b][:, k * 128:(k + 1) * 128],
                                    ident[:P, 0:P])
            last.then_inc(sem(f"trx{layer}_done"), 1)

        def product(t, k_tiles, w, width, layer):
            pe.wait_ge(sem(f"xT{layer}_done"), t + 1)
            pe.wait_ge(sem(f"hbuf{layer}_done"), t)
            for k in range(k_tiles):
                last = mm(bank(7, P, width), xT[:, k, :], w[:, k, :], k == 0, k == k_tiles - 1)
            last.then_inc(sem(f"h{layer}_done"), 1)

        def step1(t, k, i, first=False, last=False):
            b, slot = k % 2, k % RING
            if not last:
                it = 1 if i is None else (i * 16 + (32 if slot == 0 else 16))
                aggregate(0, t, slot, b, both, 16 if i is None else it, "y_done", t - 1 if i is not None else None)
            if not first:
                turn(t - 1, (k - 1) % 2, 8, 2)
            if not last:
                pe.wait_ge(sem("y_done"), t + 1)
                pe.wait_ge(sem("yT_done"), t)
                for c in range(2):
                    z = pe.transpose(bank(2, 128, P, c * P), ysum[:, c * 128:(c + 1) * 128], ident[:P, 0:P])
                z.then_inc(sem("try_done"), 1)
                pe.wait_ge(sem("yT_done"), t + 1)
                pe.wait_ge(sem("pre1_done"), t)
                for h in range(2):
                    for c in range(2):
                        z = mm(bank(3 + h, P, 512), yT[:, c, :], w1[:, c, h * 512:(h + 1) * 512], c == 0, c == 1)
                z.then_inc(sem("p1_done"), 1)
            if not first:
                product(t - 1, 8, w2, D2, 2)

        pe.wait_ge(sem("rows1_ready"), T)
        pe.wait_ge(sem("ft_done"), T)
        step1(0, 0, None, first=True)
        with pe.Fori(0, 6) as i:
            for k in range(1, 5):
                step1(i * 4 + k, k, i)
        step1(T, T, 0, last=True)

        def step2(t, k, i, first=False, last=False):
            b, slot = k % 2, k % RING
            if not last:
                v = 16 * visits(1, slot)
                it = v + 16 if i is None else i * 16 + (v + (32 if slot == 0 else 16))
                if i is None:
                    aggregate(1, t, slot, b, wide, it, None, None)
                else:
                    aggregate(1, t, slot, b, wide, it, "pre2_done", t - 1)
            if not first:
                turn(t - 1, (k - 1) % 2, 4, 3)
                product(t - 1, 4, w3, D3, 3)

        pe.wait_ge(sem("lo2_done"), T)
        step2(0, 0, None, first=True)
        with pe.Fori(0, 6) as i:
            for k in range(1, 5):
                step2(i * 4 + k, k, i)
        step2(T, T, 0, last=True)

        pe.wait_ge(sem("lo3_done"), T)
        def step3(t, k, i):
            b, slot = k % 2, k % RING
            v = 16 * visits(2, slot)
            it = v + 16 if i is None else i * 16 + (v + (32 if slot == 0 else 16))
            if i is None:
                aggregate(2, t, slot, b, both, it, None, None)
            else:
                aggregate(2, t, slot, b, both, it, "pre3_done", t - 1)
        step3(0, 0, None)
        with pe.Fori(0, 6) as i:
            for k in range(1, 5):
                step3(i * 4 + k, k, i)

        pe.wait_ge(sem("ffnw_loaded"), 32)
        pe.wait_ge(sem("pre3_done"), T)
        pe.wait_ge(sem("npad_done"), 1)
        with pe.Fori(0, NC) as i:
            pe.wait_ge(sem("stage_done"), i + 1)
            pe.wait_ge(sem("nT_done"), i * 3)
            pe.wait_ge(sem("yffn_evac"), i * G)
            for k in range(2):
                for j in range(4):
                    pe.transpose(bank(k, 128, P, j * P), stage[:, j, k * 128:(k + 1) * 128], ident[:P, 0:P])
                last = pe.transpose(bank(2, 128, P, k * P), stage[:, 4, k * 128:(k + 1) * 128], ident[:P, 0:P])
            last.then_inc(sem("trn_done"), 1)
            pe.wait_ge(sem("nT_done"), i * 3 + 3)
            for m in range(8):
                pe.wait_ge(sem("gelu_done"), i * 8 + (m - 1 if m >= 2 else 0))
                for k in range(2):
                    for h in range(2):
                        last = mm(bank(4 + 2 * (m % 2) + h, 128, CH), f1[:, k, m * 128:(m + 1) * 128],
                                  nT[:, k, h * CH:(h + 1) * CH], k == 0, k == 1)
                last.then_inc(sem("hid_done"), 1)
            pe.wait_ge(sem("gelu_done"), i * 8 + 8)
            for j in range(G):
                pe.wait_ge(sem("yffn_evac"), i * G + (j - 1 if j >= 2 else 0))
                for m in range(8):
                    last = mm(bank(3 - j % 2, P, D), gT[:, m, j * P:(j + 1) * P], f2[:, m, :], m == 0, m == 7)
                last.then_inc(sem("yffn_done"), 1)
        pe.wait_ge(sem("tri"), 2)
        pe.wait_ge(sem("prefix_done"), 1)
        mm(bank(0, P, 1), tri[:P, 0:P], pref[:, T - 1:T], True, True).then_inc(sem("before_done"), 1)


def _plan(v):
    pad = lambda e, fill: np.concatenate([np.full(PADE, fill, e.dtype), e, np.full(PADE, fill, e.dtype)])
    order = np.concatenate([np.arange(32 * g, 32 * g + 32) for k in range(3) for g in range(k, 24, 3)])
    tiles = lambda x: np.ascontiguousarray(x.reshape(-1, 128).T)
    wpw = v["L0_mix_w_pw"][order, :, 0].reshape(NT, 4, 32, 32).transpose(1, 3, 0, 2)
    return {
        "x": v["x"], "src_pad": pad(v["src"], 100000), "dst_pad": pad(v["dst"], 75000),
        "w1": v["L0_gnn_W1"], "w2": v["L0_gnn_W2"], "w3": v["L0_gnn_W3"],
        "b1": v["L0_gnn_b1"], "b2": v["L0_gnn_b2"], "b3": v["L0_gnn_b3"],
        "g1": tiles(v["L0_gnn_g1"]), "be1": tiles(v["L0_gnn_beta1"]),
        "g2": tiles(v["L0_gnn_g2"]), "be2": tiles(v["L0_gnn_beta2"]),
        "g3": v["L0_gnn_g3"], "be3": v["L0_gnn_beta3"],
        "wq": np.ascontiguousarray(v["L0_mix_w_qkv"][order, :, 2].T),
        "bng": tiles(v["L0_mix_bn_gamma"][order]), "bnb": tiles(v["L0_mix_bn_beta"][order]),
        "wdw": tiles(v["L0_mix_w_dw"][order, 0, 2]), "wpw": np.ascontiguousarray(wpw),
        "wres": np.ascontiguousarray(v["L0_mix_w_res"][:, :, 0].T), "bres": v["L0_mix_b_res"],
        "wr": v["L0_ffn_wr"][:, 0], "br": v["L0_ffn_br"], "f1": v["L0_ffn_w1"],
        "fb1": tiles(v["L0_ffn_b1"]), "f2": v["L0_ffn_w2"], "fb2": v["L0_ffn_b2"],
    }


def kernel(**inputs):
    import concourse.bacc as bacc
    from concourse.bass_utils import run_bass_kernel_spmd

    nc = bacc.Bacc("TRN2", target_bir_lowering=False, num_devices=1)
    arrays, aps = {}, {}
    for name, x in _plan({k: np.asarray(x) for k, x in inputs.items()}).items():
        x = np.ascontiguousarray(x)
        arrays[f"in_{name}"] = x
        aps[name] = nc.dram_tensor(f"in_{name}", x.shape, mybir.dt.from_np(x.dtype), kind="ExternalInput").ap()
    out = nc.dram_tensor("out", (N, D), F32, kind="ExternalOutput").ap()
    scratch = {"counts": nc.dram_tensor("counts", (T, P, N), F16).ap(), "w": nc.dram_tensor("w_nodes", (N,), F32).ap()}
    build(nc, aps, out, scratch)
    return run_bass_kernel_spmd(nc, [arrays], core_ids=[0]).results[0]["out"]
```

```python
from contextlib import ExitStack

import numpy as np
import concourse.bass as bass
from concourse import mybir

F32 = mybir.dt.float32
F16 = mybir.dt.float16
BF16 = mybir.dt.bfloat16
I32 = mybir.dt.int32
ALU = mybir.AluOpType
ACT = mybir.ActivationFunctionType
AX = mybir.AxisListType.X

N = 3125
E = 53125
P = 125
T = N // P
G = 5
D = 256
D1, D2, D3 = 1024, 512, 256
CW = G * P + 1
CH = CW // 2
NC = T // G
EC = E // P
HALO = 40
EW = EC + 2 * HALO
NWIN = -(-E // HALO)
EB = 25
PADE = NWIN * HALO + HALO
SB = EC // 5
KSEL = N // 2 - 1
EPS = 1e-5
F16_TOP = 32000.0
X_SCALE = 2048.0
BALL = float(np.float32(1.0 - 1e-5))
RMAX = float(np.arctanh(np.float64(np.float32(1.0 - 1e-5))))
ROUND = 1.5 * 2 ** 23
NT = 6
COUNTED = 3
PB = 10
RING = 4


class Steps:

    def __init__(self, eng, sem):
        self.eng, self.sem, self.base, self.k = eng, sem, 0, 0

    def did(self, ins):
        ins.then_inc(self.sem, 1)
        self.k += 1

    def settle(self):
        self.eng.wait_ge(self.sem, self.base + self.k)

    def enter(self, i, per):
        self.outer, self.per = self.k, per
        self.base, self.k = i * per + self.outer, 0

    def leave(self, times):
        assert self.k == self.per, (self.k, self.per)
        self.base, self.k = 0, self.outer + times * self.per


def free(ap, offset, dims):
    return bass.AP(ap.tensor, ap.offset + offset, [list(ap.ap[0])] + [list(d) for d in dims])


def build(nc, a, out, scratch):
    with ExitStack() as ctx:
        _build(ctx, nc, a, out, scratch)


def _build(ctx, nc, a, out, scratch):
    counts_dram, w_dram = scratch["counts"], scratch["w"]

    def sb(name, shape, dt):
        return ctx.enter_context(nc.sbuf_tensor(name, shape, dt))

    sems = {}

    def sem(name):
        if name not in sems:
            sems[name] = ctx.enter_context(nc.semaphore(name))
        return sems[name]

    psum = ctx.enter_context(nc.psum_tensor("psum", [128, 8, 512], F32))
    rows = sb("rows", [128, T * D], F32)
    acc = sb("acc", [128, T * D], F32)
    big = sb("big", [128, 12800], F32)
    wa = sb("wa", [128, 2048], F32)
    wb = sb("wb", [128, 4096], F32)
    wc = sb("wc", [128, 1024], F32)
    wm = sb("wm", [128, 3328], F32)
    scr = sb("scr", [128, 15600], F32)
    ident = sb("ident", [128, 128], F32)
    ones = sb("ones", [128, 128], F32)
    kones = sb("kones", [128, 128], F32)
    col = sb("col", [128, 900], F32)

    at = {"scr": 0, "col": 0, "wm": 0, "big": 0}

    def take(region, n):
        t = {"scr": scr, "col": col, "wm": wm, "big": big}[region]
        o = at[region]
        at[region] = o + n
        assert at[region] <= t.shape[1], (region, at[region])
        return t[:, o:o + n]

    x_rows = rows[:P, :].rearrange("p (t d) -> p t d", t=T)
    x2 = rows[:P, :].bitcast(F16).rearrange("p (t h d) -> p t h d", t=T, h=2)
    accv = acc[:P, :].rearrange("p (t d) -> p t d", t=T)
    zv = accv
    zT = take("big", 2 * NC * CW).rearrange("p (k c) -> p k c", k=2)
    hT = take("big", NT * CW).rearrange("p (m c) -> p m c", m=NT)
    sq = take("big", 3 * CW).rearrange("p (m c) -> p m c", m=3)
    umax = take("big", CW)
    h2in = big[:P, :].bitcast(F16).rearrange("p (t h d) -> p t h d", t=T, h=2)
    xn2 = big[:P, 0:6400].rearrange("p (t d) -> p t d", t=T)
    gT = big[:, 6400:6400 + 8 * CW].rearrange("p (m c) -> p m c", m=8)
    w1 = wa[:, :].rearrange("p (k n) -> p k n", k=2)
    w2 = wb[:, :].rearrange("p (k n) -> p k n", k=8)
    w3 = wc[:, :].rearrange("p (k n) -> p k n", k=4)
    f1 = wa[:, :].rearrange("p (k n) -> p k n", k=2)
    f2 = wb[:, 0:2048].rearrange("p (k n) -> p k n", k=8)
    zi = wb[:P, 0:3072].bitcast(F16)
    wq = take("wm", 2 * 768).rearrange("p (k n) -> p k n", k=2)
    wp = take("wm", NT * 128).rearrange("p (m n) -> p m n", m=NT)
    wres = take("wm", 4 * D).rearrange("p (k n) -> p k n", k=4)
    b1r, b2r, b3r = wm[:P, 0:1024], wm[:P, 1024:1536], wm[:P, 1536:1792]
    g3r, be3r = wm[:P, 1792:2048], wm[:P, 2048:2304]
    fb2r, wrr = wm[:P, 2304:2560], wm[:P, 2560:2816]
    sT = take("scr", NT * CW).rearrange("p (m c) -> p m c", m=NT)
    veps = take("scr", CW)
    tdiv = take("scr", CW)
    xbuf = take("scr", G * D)[:P].rearrange("p (t d) -> p t d", t=G)
    gram = take("scr", 512).rearrange("p (k n) -> p k n", k=2)
    bresr = take("scr", 256)[:P]
    sqjunk = take("scr", 256)[:P]
    wdp, wdt = scr[:P, 0:EW], scr[:P, EW:2 * EW]
    gw = scr[:, 0:2 * 768].rearrange("p (k n) -> p k n", k=2)
    sqw = scr[:, NT * CW:NT * CW + 512]
    esrc_i = take("scr", EW)[:P].bitcast(I32)
    edst_i = take("scr", EW)[:P].bitcast(I32)
    esrc = take("scr", EW)[:P]
    ekey = take("scr", EW)[:P]
    edp = take("scr", EW)[:P]
    edt = take("scr", EW)[:P]
    fwd = take("scr", EC)[:P]
    bwd = take("scr", EC)[:P]
    eidx = take("scr", EC)[:P].bitcast(I32)
    evalue = take("scr", EC // 2 + 1)[:P].bitcast(F16)
    equal = acc[:P, :].bitcast(BF16)
    OW = EB * (P + T)
    onehot = []
    for s in range(2):
        o = 2 * NC * CW + s * OW // 2
        oh = big[:P, o:o + OW // 2].bitcast(BF16)
        onehot.append((oh, oh[:, 0:EB * P].rearrange("p (j q) -> p j q", j=EB),
                       oh[:, EB * P:OW].rearrange("p (j q) -> p j q", j=EB)))
    sidx = take("scr", SB)[:P].bitcast(I32)
    svalue = take("scr", (SB + 1) // 2)[:P].bitcast(F16)
    iop = take("scr", (P + 1) // 2)[:P].bitcast(BF16)
    wkey = take("scr", EW)[:P]
    at["scr"] = 0
    ring = take("scr", RING * 1563)[:P].bitcast(F16)
    ring = [ring[:, s * 3126:s * 3126 + N].rearrange("p (t q) -> p t q", t=T) for s in range(RING)]
    pre = [take("scr", 1024)[:P] for _ in range(2)]
    xT = take("scr", 8 * P).rearrange("p (k q) -> p k q", k=8)
    ysum, yhi = take("scr", D)[:P], take("scr", D)[:P]
    yT = take("scr", 2 * P).rearrange("p (k q) -> p k q", k=2)
    hbuf = take("scr", 512)[:P]
    post = take("scr", D)[:P]
    xslot = [take("scr", D)[:P] for _ in range(RING)]
    stage = take("scr", G * D)[:P].rearrange("p (t d) -> p t d", t=G)
    nT = take("scr", 2 * CW).rearrange("p (k c) -> p k c", k=2)
    wall = scr[:P, 0:N]
    gtjunk = scr[:P, N + 1:N + 1 + 1563].bitcast(BF16)[:, 0:N]
    sgjunk = scr[:P, N + 1 + 1563:N + 1 + 2 * 1563].bitcast(BF16)[:, 0:N]
    def c_(n):
        return take("col", n)
    stats = c_(T * 6)[:P].rearrange("p (t s) -> p t s", t=T)
    mv = c_(T * 2)[:P].rearrange("p (t s) -> p t s", t=T)
    rstd, dinv, ca, cb, cc, cd = (c_(T)[:P] for _ in range(6))
    dx, d2in, d2out, d3in, d3out = (c_(T)[:P] for _ in range(5))
    st2 = c_(12)[:P].rearrange("p (a s) -> p a s", a=2)
    st3, st4, mv3, mv4 = c_(6)[:P], c_(6)[:P], c_(2)[:P], c_(2)[:P]
    rs3, rs4, root3, root4 = (c_(1)[:P] for _ in range(4))
    mv2, rs2, root2 = c_(2)[:P], c_(1)[:P], c_(1)[:P]
    eps = c_(1)
    bng, bnb, bns, bnt, wdw, tmp6 = (c_(NT) for _ in range(6))
    zcol = c_(2)
    zrow = big[0:1, 10016:10016 + 256]
    nzrow = big[0:1, 10016 + 256:10016 + 512]
    g1c, be1c, fb1c, g2c, be2c = c_(8), c_(8), c_(8), c_(4), c_(4)
    ssw, ssg = c_(12), c_(12)
    ssb = c_(12)
    bound = c_(8)
    ucol, ocol = (c_(G)[:P] for _ in range(2))
    n4, f4 = (c_(T)[:P] for _ in range(2))
    flagf, flagi = c_(1), c_(1).bitcast(I32)
    wv, wsel, gt, sg, bnd, pref, brc = (c_(T)[:P] for _ in range(7))
    tri = kones
    pause, pool_pause = c_(1)[:P], c_(1)[:P]

    def bank(b, p, n, o=0):
        return psum[:p, b, o:o + n]

    def pair(i, p=128):
        return psum[:p, 2 * i:2 * i + 2, 0:CH]

    def halves(ap):
        return ap.rearrange("p (h c) -> p h c", h=2)

    block = ctx.enter_context(nc.Block())

    @block.sync
    def _(sp):
        def load(dst, src, name):
            sp.dma_start(dst, src).then_inc(sem(name), 16)

        src_w = bass.AP(a["src_pad"].tensor, PADE - HALO, [[EC, P], [1, EW]])
        dst_w = bass.AP(a["dst_pad"].tensor, PADE - HALO, [[EC, P], [1, EW]])
        load(esrc_i, src_w, "edges_loaded")
        load(edst_i, dst_w, "edges_loaded")
        load(x_rows, a["x"].rearrange("(p t) d -> p t d", t=T), "x_loaded")
        load(wq, a["wq"].rearrange("(k p) n -> p k n", p=128), "mixw_loaded")
        load(wres, a["wres"].rearrange("(k p) n -> p k n", p=128), "mixw_loaded")
        load(bresr, bass.AP(a["bres"].tensor, 0, [[0, P], [1, D]]), "mixw_loaded")
        load(bng, a["bng"], "mixw_loaded")
        load(bnb, a["bnb"], "mixw_loaded")
        load(wdw, a["wdw"], "mixw_loaded")
        sp.wait_ge(sem("blocks_cleared"), 1)
        for b in range(4):
            load(wp[32 * b:32 * b + 32, :, 32 * b:32 * b + 32], a["wpw"][b], "mixw_loaded")
        for dst, name in ((g1c, "g1"), (be1c, "be1"), (fb1c, "fb1"), (g2c, "g2"), (be2c, "be2")):
            load(dst, a[name], "cols_loaded")
        sp.wait_ge(sem("zi_ready"), 2)
        for t in range(T):
            sp.dma_start(counts_dram[t], free(zi, (T - 1 - t) * P, [[1, N]])).then_inc(sem("counts_cleared"), 16)
        load(w1, a["w1"].rearrange("(k p) n -> p k n", p=128), "layerw_loaded")
        load(w3, a["w3"].rearrange("(k p) n -> p k n", p=128), "layerw_loaded")
        sp.wait_ge(sem("flag_ready"), 1)
        far = sp.value_load(flagi[0:1, 0:1], min_val=0, max_val=1)
        with sp.If(far > 0):
            with sp.Fori(1, NWIN) as w:
                for side in (0, 1):
                    sp.wait_ge(sem("window_used"), w * 2 + (side - 2))
                    for dst, name in ((esrc_i, "src_pad"), (edst_i, "dst_pad")):
                        o = PADE - HALO + (w * HALO if side == 0 else w * (-HALO))
                        sp.dma_start(dst, bass.AP(a[name].tensor, o, [[EC, P], [1, EW]])).then_inc(
                            sem("window_loaded"), 16)
        sp.wait_ge(sem("counts_cleared"), 16 * T)
        load(w2, a["w2"].rearrange("(k p) n -> p k n", p=128), "layerw_loaded")
        sp.wait_ge(sem("ft_done"), T)
        sp.wait_ge(sem("res_done"), T)
        for dst, name, n in ((b1r, "b1", D1), (b2r, "b2", D2), (b3r, "b3", D3), (g3r, "g3", D3),
                             (be3r, "be3", D3), (fb2r, "fb2", D), (wrr, "wr", D)):
            load(dst, bass.AP(a[name].tensor, 0, [[0, P], [1, n]]), "rowb_loaded")
        load(brc[:, 0:1], bass.AP(a["br"].tensor, 0, [[0, P], [1, 1]]), "rowb_loaded")
        sp.wait_ge(sem("scattered"), 16 * EC)
        sp.wait_ge(sem("rows1_ready"), T)
        xd = a["x"].rearrange("(p t) d -> p t d", t=T)
        for layer in range(3):
            base = layer * T
            def fetch(t, s):
                if layer == 0:
                    sp.dma_start(xslot[s], xd[:, bass.ds(t, 1), :].rearrange("p o d -> p (o d)")).then_inc(
                        sem(f"xslot{s}_loaded"), 16)
                sp.dma_start(ring[s], counts_dram[t].rearrange("p (t q) -> p t q", t=T)).then_inc(
                    sem(f"ring_loaded{s}"), 16)
            for s in range(RING):
                if layer:
                    sp.wait_ge(sem("agg_done"), base)
                fetch(s, s)
            with sp.Fori(0, 5) as i:
                for s in range(RING):
                    sp.wait_ge(sem("agg_done"), i * RING + (base + s + 1))
                    if layer == 0:
                        sp.wait_ge(sem("fx_done"), i * RING + (s + 1))
                    fetch(i * RING + (RING + s), s)
            sp.wait_ge(sem("agg_done"), base + T - RING)
            if layer == 0:
                sp.wait_ge(sem("fx_done"), T - RING)
            fetch(T - 1, 0)
            if layer == 1:
                sp.wait_ge(sem("h2_done"), T)
                load(f1, a["f1"].rearrange("(k p) n -> p k n", p=128), "ffnw_loaded")
                load(f2, a["f2"].rearrange("(k p) n -> p k n", p=128), "ffnw_loaded")
        sp.wait_ge(sem("negw_done"), 1)
        sp.wait_ge(sem("agg_done"), 3 * T)
        sp.dma_start(w_dram.rearrange("(p t) -> p t", t=T), wv).then_inc(sem("w_stored"), 16)
        sp.wait_ge(sem("w_stored"), 16)
        sp.dma_start(wall, bass.AP(w_dram.tensor, 0, [[0, P], [1, N]])).then_inc(sem("wall_loaded"), 16)
        od = out.rearrange("(p t) d -> p t d", t=T)
        with sp.Fori(0, NC) as i:
            sp.wait_ge(sem("final_done"), i * G + G)
            sp.dma_start(od[:, bass.ds(i * G, G), :], accv[:, bass.ds(i * G, G), :]).then_inc(sem("stored"), 16)
        sp.wait_ge(sem("stored"), 16 * NC)

    @block.gpsimd
    def _(pool):
        done = Steps(pool, sem("pool_steps"))
        pool.memset(wb[:P, 0:3072], 0.0).then_inc(sem("zi_ready"), 1)
        pool.memset(eps, EPS).then_inc(sem("eps_ready"), 1)
        done.did(pool.memset(pool_pause, 0.0))
        pool.memset(wp[:, :, :], 0.0).then_inc(sem("blocks_cleared"), 1)
        done.did(pool.memset(ident[:, :], 0.0))
        done.did(pool.memset(ones[:, :], 1.0))
        done.did(pool.memset(kones[:, :], 0.0))
        done.settle()
        pool.affine_select(out=ident[:, :], in_=ident[:, :], compare_op=ALU.not_equal, fill=1.0, base=0,
                           pattern=[[-1, 128]], channel_multiplier=1).then_inc(sem("ident_ready"), 1)
        pool.wait_ge(sem("ident_ready"), 1)
        for b in range(4):
            done.did(pool.memset(kones[32 * b:32 * b + 32, 32 * b:32 * b + 32], 1.0))
            done.settle()
        pool.iota(iop[:, 0:P], pattern=[[1, P]], base=0, channel_multiplier=0,
                  allow_small_or_imprecise_dtypes=True).then_inc(sem("ident_ready"), 1)
        pool.wait_ge(sem("ident_ready"), 2)
        pool.memset(free(zT, P * G, [[NC * CW, 2], [CW, NC], [1, 1]]), 0.0).then_inc(sem("ident_ready"), 1)
        pool.wait_ge(sem("ident_ready"), 3)
        pool.wait_ge(sem("zi_ready"), 1)
        pool.tensor_copy(zi[:, (T - 1) * P:T * P], ident[:P, 0:P]).then_inc(sem("zi_ready"), 1)
        pool.wait_ge(sem("keys_ready"), 1)
        for b in range(PB):
            both_oh, ohp, oht = onehot[b % 2]
            if b >= 2:
                pool.wait_ge(sem("degree_used"), b - 1)
            pool.tensor_tensor(ohp, free(edp, HALO + b * EB, [[1, EB], [0, P]]), free(iop, 0, [[0, EB], [1, P]]),
                               ALU.subtract).then_inc(sem("offset_done"), 1)
            pool.tensor_tensor(oht, free(edt, HALO + b * EB, [[1, EB], [0, T]]), free(iop, 0, [[0, EB], [1, T]]),
                               ALU.subtract).then_inc(sem("offset_done"), 1)
        pool.wait_ge(sem("counts_cleared"), 16 * T)
        pool.wait_ge(sem("edges_ready"), 1)
        cells = counts_dram.rearrange("t p (n o) -> (t p n) o", o=1)
        with pool.Fori(0, EC // SB) as i:
            at_j = pool.snap(i * SB)
            done.enter(i, 2)
            pool.wait_ge(sem("scattered"), i * (16 * SB))
            done.settle()
            done.did(pool.tensor_tensor(pool_pause, pool_pause, pool_pause, ALU.add))
            pool.tensor_copy(sidx, eidx[:, bass.ds(at_j, SB)]).then_inc(sem("staged"), 1)
            pool.tensor_copy(svalue[:, 0:SB], evalue[:, bass.ds(at_j, SB)]).then_inc(sem("staged"), 1)
            pool.wait_ge(sem("staged"), i * 2 + 2)
            done.settle()
            done.did(pool.tensor_tensor(pool_pause, pool_pause, pool_pause, ALU.add))
            for j in range(SB):
                pool.indirect_dma_start(cells, bass.IndirectOffsetOnAxis(ap=sidx[:, j:j + 1], axis=0),
                                        svalue[:, j:j + 1], None, bounds_check=N * N - 1,
                                        oob_is_err=False).then_inc(sem("scattered"), 16)
            done.leave(EC // SB)
        pool.wait_ge(sem("k_done"), 4 * NC)
        pool.memset(tri[:, :], 0.0).then_inc(sem("tri"), 1)
        pool.wait_ge(sem("tri"), 1)
        pool.affine_select(out=tri[:, :], in_=tri[:, :], compare_op=ALU.is_ge, fill=1.0, base=0,
                           pattern=[[-1, 128]], channel_multiplier=1).then_inc(sem("tri"), 1)
        pool.wait_ge(sem("rows1_ready"), T)
        pool.wait_ge(sem("scattered"), 16 * EC)
        pool.memset(free(nT, P * G, [[CW, 2], [1, 1]]), 0.0).then_inc(sem("npad_done"), 1)
        pool.wait_ge(sem("rowb_loaded"), 16 * 8)
        pool.wait_ge(sem("fx_done"), T)
        for t in range(T):
            pool.tensor_tensor(accv[:, t, :], accv[:, t, :], be3r, ALU.add).then_inc(sem("be3_added"), 1)
        for i in range(NC):
            pool.wait_ge(sem("xn2_done"), i * G + G)
            pool.wait_ge(sem("trn_done"), i)
            pool.tensor_copy(stage, xn2[:, i * G:i * G + G, :]).then_inc(sem("stage_done"), 1)
            pool.wait_ge(sem("sum_done"), i * G + G)
            chunk = accv[:, i * G:i * G + G, :]
            pool.tensor_tensor(chunk, chunk, xn2[:, i * G:i * G + G, :], ALU.add).then_inc(sem("xn2_added"), 1)

    def edge_keys(dve, done, key, esrc, edp, edt):
        done.did(dve.tensor_copy(esrc, esrc_i))
        done.did(dve.tensor_copy(edt, edst_i))
        done.settle()
        done.did(dve.tensor_scalar(edp, edt, 1.0 / T, -0.48, ALU.mult, ALU.add))
        done.settle()
        done.did(dve.tensor_scalar(edp, edp, ROUND, ROUND, ALU.add, ALU.subtract))
        done.settle()
        done.did(dve.scalar_tensor_tensor(out=edt, in0=edp, scalar=-float(T), in1=edt, op0=ALU.mult, op1=ALU.add))
        done.settle()
        done.did(dve.scalar_tensor_tensor(out=key, in0=esrc, scalar=float(P), in1=edp,
                                          op0=ALU.mult, op1=ALU.add))
        done.settle()
        done.did(dve.scalar_tensor_tensor(out=key, in0=edt, scalar=float(P * N), in1=key,
                                          op0=ALU.mult, op1=ALU.add))
        done.settle()

    KEY_STEPS = 7

    def count_equal(dve, done, other, shift, into, lo, tmp):
        mine = free(ekey, HALO + lo, [[1, EB], [0, HALO]])
        theirs = free(other, HALO + lo + shift, [[1, EB], [1, HALO]])
        pairs = free(equal, 0, [[HALO, EB], [1, HALO]])
        done.did(dve.tensor_tensor(pairs, mine, theirs, ALU.is_equal))
        done.settle()
        done.did(dve.tensor_reduce(tmp, pairs, AX, ALU.add))
        done.settle()

    @block.vector
    def _(dve):
        done = Steps(dve, sem("dve_steps"))

        def layernorm_stats(src, width, n, t):
            parts = max(1, width // 512)
            for h in range(parts):
                done.did(dve.bn_stats(st2[:, h, :], src[:, h * 512:(h + 1) * 512] if parts > 1 else src))
            done.settle()
            done.did(dve.memset(pause, 0.0))
            dve.bn_aggr(mv2, st2[:, 0:parts, :]).then_inc(sem(f"var{n}_done"), 1)
            dve.wait_ge(sem(f"root{n}_done"), t + 1)
            done.did(dve.reciprocal(rs2, root2))
            done.settle()

        dve.wait_ge(sem("edges_loaded"), 32)
        edge_keys(dve, done, ekey, esrc, edp, edt)
        done.settle()
        dve.memset(pause, 0.0).then_inc(sem("keys_ready"), 1)
        dstf = wkey
        done.did(dve.tensor_copy(dstf, edst_i))
        done.settle()
        mid, nxt, far_ = (free(dstf, HALO + s, [[1, EC]]) for s in (0, 1, HALO))
        done.did(dve.tensor_tensor(fwd, mid, nxt, ALU.is_gt))
        done.did(dve.tensor_tensor(bwd, mid, far_, ALU.is_equal))
        done.settle()
        done.did(dve.tensor_tensor(fwd, fwd, bwd, ALU.max))
        done.settle()
        dve.tensor_reduce(flagf[:P], fwd, AX, ALU.max).then_inc(sem("flag_part"), 1)
        dve.wait_ge(sem("flag_sum"), 1)
        done.did(dve.tensor_scalar(flagf[0:1], bank(7, 1, 1), 1.0, None, ALU.min))
        done.settle()
        dve.tensor_copy(flagi[0:1, 0:1], flagf[0:1]).then_inc(sem("flag_ready"), 1)
        done.settle()
        for lo, hi in ((0, EC // 2), (EC // 2, EC)):
            n = hi - lo + HALO
            done.did(dve.tensor_tensor(free(equal, 0, [[HALO, n], [1, HALO]]), free(ekey, lo, [[1, n], [0, HALO]]),
                                       free(ekey, lo + 1, [[1, n], [1, HALO]]), ALU.is_equal))
            done.settle()
            done.did(dve.tensor_reduce(fwd[:, lo:hi], free(equal, HALO * HALO, [[HALO, hi - lo], [1, HALO]]), AX,
                                       ALU.add))
            done.did(dve.tensor_reduce(bwd[:, lo:hi],
                                       free(equal, (HALO - 1) * HALO, [[HALO, hi - lo], [1 - HALO, HALO]]), AX,
                                       ALU.add))
            done.settle()
        self_ = evalue[:, 0:EC]
        done.did(dve.tensor_tensor(self_, free(dstf, HALO, [[1, EC]]), free(esrc, HALO, [[1, EC]]), ALU.is_equal))
        done.settle()
        dve.wait_ge(sem("flag_ready"), 1)
        far = dve.value_load(flagi[0:1, 0:1], min_val=0, max_val=1)
        with dve.If(far > 0):
            with dve.Fori(1, NWIN) as w:
                for side in (0, 1):
                    fs = sem("far_steps")
                    per = KEY_STEPS + 3 * (EC // EB)
                    inner = Steps(dve, fs)
                    inner.base = w * (2 * per) + (side - 2) * per
                    dve.wait_ge(sem("window_loaded"), w * 64 + (32 * side - 32))
                    edge_keys(dve, inner, wkey, wkey, wdp, wdt)
                    into = fwd if side == 0 else bwd
                    for b in range(0, EC, EB):
                        part = sqjunk[:, 0:EB]
                        count_equal(dve, inner, wkey, 1 if side == 0 else -HALO, None, b, part)
                        inner.did(dve.tensor_tensor(free(into, b, [[1, EB]]), free(into, b, [[1, EB]]), part,
                                                    ALU.add))
                        inner.settle()
                    assert inner.k == per
                    dve.memset(sqjunk[:, 0:1], 0.0).then_inc(sem("window_used"), 1)
        done.did(dve.scalar_tensor_tensor(out=bwd, in0=bwd, scalar=2.0e7, in1=free(ekey, HALO, [[1, EC]]),
                                          op0=ALU.mult, op1=ALU.add))
        done.did(dve.tensor_scalar(fwd, fwd, 1.0, None, ALU.add))
        done.settle()
        done.did(dve.tensor_scalar(bwd, bwd, 2.0e7, None, ALU.min))
        done.did(dve.tensor_tensor(evalue[:, 0:EC], fwd, self_, ALU.add))
        done.settle()
        dve.tensor_copy(eidx, bwd).then_inc(sem("edges_ready"), 1)
        dve.wait_ge(sem("x_loaded"), 16)
        for t in range(T):
            done.did(dve.bn_stats(stats[:, t, :], x_rows[:, t, :]))
        done.settle()
        for t in range(T):
            done.did(dve.bn_aggr(mv[:, t, :], stats[:, t:t + 1, :]))
        done.settle()
        var = mv[:, :, 1:2].rearrange("p t o -> p (t o)")
        dve.tensor_scalar(ca, var, EPS, None, ALU.add).then_inc(sem("xvar_done"), 1)
        dve.wait_ge(sem("xroot_done"), 1)
        done.did(dve.reciprocal(rstd, rstd))
        dve.wait_ge(sem("xvar_done"), 1)
        done.did(dve.reciprocal(cb, ca))
        done.settle()
        dve.tensor_tensor(cb, var, cb, ALU.mult).then_inc(sem("ratio2_done"), 1)
        for t in range(T):
            done.did(dve.tensor_scalar(x_rows[:, t, :], x_rows[:, t, :], mv[:, t, 0:1], rstd[:, t:t + 1],
                                       ALU.subtract, ALU.mult))
        dve.wait_ge(sem("norm_done"), 1)
        done.did(dve.tensor_scalar(ca, cb, BALL, None, ALU.min))
        done.did(dve.tensor_scalar(cb, cb, 1e-15, None, ALU.max))
        done.settle()
        done.did(dve.tensor_scalar(cc, ca, 1.0, None, ALU.add))
        done.did(dve.tensor_scalar(cd, ca, -1.0, 1.0, ALU.mult, ALU.add))
        done.settle()
        done.did(dve.reciprocal(cd, cd))
        done.settle()
        dve.tensor_tensor(cc, cc, cd, ALU.mult).then_inc(sem("ratio_done"), 1)
        done.did(dve.tensor_tensor(dx, ca, ca, ALU.mult))
        done.settle()
        done.did(dve.tensor_scalar(rstd, dx, 1.0 / 9.0, 1.0 / 7.0, ALU.mult, ALU.add))
        done.settle()
        for c in (1.0 / 5.0, 1.0 / 3.0, 1.0):
            done.did(dve.tensor_tensor(rstd, rstd, dx, ALU.mult))
            done.settle()
            done.did(dve.tensor_scalar(rstd, rstd, c, None, ALU.add))
            done.settle()
        dve.wait_ge(sem("log_done"), 1)
        done.did(dve.tensor_scalar(cd, cd, 0.5, None, ALU.mult))
        done.did(dve.reciprocal(cb, cb))
        done.settle()
        done.did(dve.tensor_tensor(cd, cd, cb, ALU.mult))
        done.did(dve.tensor_scalar(cc, ca, 0.1, None, ALU.is_lt))
        done.settle()
        done.did(dve.tensor_tensor(rstd, rstd, cd, ALU.subtract))
        done.settle()
        done.did(dve.tensor_tensor(rstd, rstd, cc, ALU.mult))
        done.settle()
        done.did(dve.tensor_tensor(cd, rstd, cd, ALU.add))
        done.settle()
        for t in range(T):
            dve.tensor_scalar(zv[:, t, :], x_rows[:, t, :], cd[:, t:t + 1], None, ALU.mult).then_inc(
                sem("z_done"), 1)
        for b in range(PB, EC // EB):
            both_oh, ohp, oht = onehot[b % 2]
            dve.wait_ge(sem("degree_used"), b - 1)
            done.did(dve.tensor_tensor(ohp, free(edp, HALO + b * EB, [[1, EB], [0, P]]),
                                       free(iop, 0, [[0, EB], [1, P]]), ALU.is_equal))
            dve.tensor_tensor(oht, free(edt, HALO + b * EB, [[1, EB], [0, T]]),
                              free(iop, 0, [[0, EB], [1, T]]), ALU.is_equal).then_inc(sem("onehot_done"), 1)
        dve.wait_ge(sem("degree_used"), EC // EB)
        dve.tensor_scalar(dinv, bank(7, P, T), 1.0, None, ALU.add).then_inc(sem("dinv_read"), 1)
        dve.wait_ge(sem("droot_done"), 1)
        done.did(dve.reciprocal(dinv, dinv))
        done.settle()
        dve.wait_ge(sem("zrow_done"), 1)
        dve.tensor_scalar(nzrow, zrow, -1.0 / N, None, ALU.mult).then_inc(sem("nzrow_done"), 1)
        dve.wait_ge(sem("gram_done"), 1)
        done.did(dve.tensor_copy(zcol, bank(2, 128, 2)))
        dve.tensor_copy(gram, psum[:, 0:2, 0:D]).then_inc(sem("gram_copied"), 1)
        done.settle()
        dve.wait_ge(sem("mixw_loaded"), 16 * 10)
        dve.wait_ge(sem("gw_done"), 1)
        for k in range(2):
            done.did(dve.tensor_tensor(gw[:, k, 0:512], bank(4 + 2 * k, 128, 512), wq[:, k, 0:512], ALU.mult))
            last = dve.tensor_tensor(gw[:, k, 512:768], bank(5 + 2 * k, 128, 256), wq[:, k, 512:768], ALU.mult)
            last.then_inc(sem("wgw_done"), 1)
        for m in range(NT):
            last = dve.tensor_scalar(wp[:, m, :], wp[:, m, :], wdw[:, m:m + 1], None, ALU.mult)
        last.then_inc(sem("wp_done"), 1)
        dve.wait_ge(sem("bnsum_done"), 1)
        dve.tensor_scalar(tmp6, bank(3, 128, NT), 1.0 / N, None, ALU.mult).then_inc(sem("bnvar_done"), 1)
        done.did(dve.tensor_scalar(bnt, bank(3, 128, NT, 16), 1.0 / N, None, ALU.mult))
        done.settle()
        dve.wait_ge(sem("bnroot_done"), 1)
        done.did(dve.reciprocal(tmp6, tmp6))
        done.settle()
        done.did(dve.tensor_tensor(bns, tmp6, bng, ALU.mult))
        done.settle()
        done.did(dve.tensor_tensor(bnt, bnt, bns, ALU.mult))
        done.settle()
        dve.tensor_tensor(bnt, bnb, bnt, ALU.subtract).then_inc(sem("bn_done"), 1)
        done.did(dve.tensor_scalar(dx, dinv, X_SCALE, None, ALU.mult))
        done.did(dve.tensor_scalar(ca, dinv, 1.0 / X_SCALE, None, ALU.mult))
        done.settle()
        dve.wait_ge(sem("bounds_read"), 1)
        for L, width in ((0, D1), (1, D2)):
            o = 3 * L
            done.did(dve.tensor_tensor(bound[:, o:o + 1], bound[:, o:o + 1], bound[:, o + 2:o + 3], ALU.mult))
            done.settle()
            done.did(dve.scalar_tensor_tensor(out=bound[:, o:o + 1], in0=bound[:, o + 1:o + 2],
                                              scalar=float(width) ** 0.5, in1=bound[:, o:o + 1],
                                              op0=ALU.mult, op1=ALU.add))
            done.settle()
            done.did(dve.tensor_scalar(bound[:, o:o + 1], bound[:, o:o + 1], 1e-20, 1.0 / F16_TOP,
                                       ALU.max, ALU.mult))
            done.settle()
            done.did(dve.reciprocal(bound[:, 6 + L:7 + L], bound[:, o:o + 1]))
            done.settle()
            di, do = (d2in, d2out) if L == 0 else (d3in, d3out)
            done.did(dve.tensor_scalar(di, dinv, bound[:P, 6 + L:7 + L], None, ALU.mult))
            done.did(dve.tensor_scalar(do, dinv, bound[:P, o:o + 1], None, ALU.mult))
            done.settle()
        MIX = 14 + 2 * G
        with dve.Fori(0, NC) as i:
            done.enter(i, MIX)
            for j in range(G):
                t = i * G + j
                raw = xbuf[:, j, :]
                dve.wait_ge(sem("rows1_ready"), i * G)
                done.did(dve.tensor_scalar(raw, x_rows[:, t, :], dx[:, bass.ds(t, 1)], None, ALU.mult))
            done.settle()
            for j in range(G):
                done.did(dve.tensor_scalar(x2[:, i * G + j, 0, :], xbuf[:, j, :], 1.0, None, ALU.mult))
            done.settle()
            for j in range(G):
                t = i * G + j
                dve.tensor_tensor(x2[:, t, 1, :], xbuf[:, j, :], x2[:, t, 0, :], ALU.subtract).then_inc(
                    sem("rows1_ready"), 1)
            for m in range(NT):
                dve.wait_ge(sem("s_done"), i * NT + (m + 1))
                if m == 0:
                    dve.wait_ge(sem("res_done"), i * G)
                if m < 4:
                    dve.tensor_scalar(halves(sT[:, m, :]), pair(m % 2), 0.0, None, ALU.max).then_inc(
                        sem("s_evac"), 1)
                else:
                    dve.tensor_copy(halves(sT[:, m, :]), pair(m % 2)).then_inc(sem("s_evac"), 1)
            dve.wait_ge(sem("nc_done"), i * 12 + 12)
            dve.tensor_scalar(halves(umax), pair(2), 1.0 / RMAX ** 2, 1.0, ALU.mult, ALU.max).then_inc(
                sem("u_done"), 1)
            dve.wait_ge(sem("veps_done"), i + 1)
            for n in range(4):
                src, half = (hT, n) if n < 2 else (sT, n - 2)
                q, v = src[:, half, :], src[:, 4 + half, :]
                dve.wait_ge(sem("k_done"), i * 4 + (n + 1))
                dve.tensor_tensor(halves(q), pair(3), halves(q), ALU.mult).then_inc(sem("qk_done"), 1)
                done.did(dve.tensor_tensor(tdiv, v, veps, ALU.add))
                done.settle()
                done.did(dve.reciprocal(tdiv, tdiv))
                done.settle()
                done.did(dve.tensor_tensor(tdiv, tdiv, v, ALU.mult))
                done.settle()
                dve.wait_ge(sem("qk_done"), i * 4 + (n + 1))
                dve.tensor_tensor(q, q, tdiv, ALU.mult).then_inc(sem("o_done"), 1)
                dve.wait_ge(sem("o_done"), i * 4 + (n + 1))
            dve.wait_ge(sem("ocol_read"), i + 1)
            dve.tensor_copy(ucol, bank(6, P, G)).then_inc(sem("ucol_read"), 1)
            dve.wait_ge(sem("ucol_read"), i + 1)
            done.did(dve.tensor_tensor(ocol, ocol, ucol, ALU.max))
            done.settle()
            done.did(dve.reciprocal(ocol, ocol))
            done.settle()
            for j in range(G):
                t = i * G + j
                dve.wait_ge(sem("res_done"), t + 1)
                dve.scalar_tensor_tensor(out=accv[:, t, :], in0=bank(4 + j % 2, P, D), scalar=ocol[:, j:j + 1],
                                         in1=bresr, op0=ALU.mult, op1=ALU.add).then_inc(sem("ft_done"), 1)
            done.leave(NC)
        dve.wait_ge(sem("n4root_done"), 1)
        dve.tensor_scalar(n4, n4, 1e-15, None, ALU.max).then_inc(sem("n4_ready"), 1)
        dve.wait_ge(sem("tanh_done"), 1)
        done.did(dve.tensor_scalar(f4, f4, BALL, None, ALU.min))
        done.did(dve.reciprocal(n4, n4))
        done.settle()
        dve.tensor_tensor(f4, f4, n4, ALU.mult).then_inc(sem("f4_ready"), 1)
        dve.wait_ge(sem("rowb_loaded"), 16 * 8)
        dve.wait_ge(sem("scattered"), 16 * EC)

        def rows_out(t, width, tile, scale, layer):
            dve.wait_ge(sem(f"h{layer}_done"), t + 1)
            dve.wait_ge(sem(f"lo{layer}_done"), t)
            dve.tensor_scalar(hbuf[:, 0:width], bank(7, P, width), scale[:, bass.ds(t, 1)], None,
                              ALU.mult).then_inc(sem(f"hbuf{layer}_done"), 1)
            dve.wait_ge(sem(f"hi{layer}_done"), t + 1)
            dve.tensor_tensor(tile[:, t, 1, :], hbuf[:, 0:width], tile[:, t, 0, :], ALU.subtract).then_inc(
                sem(f"lo{layer}_done"), 1)

        def normalise(t, buf, width, relu, xhat):
            dve.wait_ge(sem(relu), t + 1)
            layernorm_stats(buf, width, 1 if width == D1 else 2, t)
            dve.tensor_scalar(buf, buf, mv2[:, 0:1], rs2, ALU.subtract, ALU.mult).then_inc(sem(xhat), 1)

        def step1(t, b, b4, xv, first=False, last=False):
            if not last:
                dve.wait_ge(sem("yhi_done"), t + 1)
                dve.tensor_tensor(ysum, bank(b, P, D, D), yhi, ALU.add).then_inc(sem("y_done"), 1)
                dve.wait_ge(sem("p1_done"), t + 1)
                dve.scalar_tensor_tensor(out=pre[b].rearrange("p (h n) -> p h n", h=2), in0=psum[:P, 3:5, :],
                                         scalar=ca[:, bass.ds(t, 1)],
                                         in1=b1r.rearrange("p (h n) -> p h n", h=2), op0=ALU.mult,
                                         op1=ALU.add).then_inc(sem("pre1_done"), 1)
                normalise(t, pre[b], D1, "relu1_done", "xhat1_done")
                dve.wait_ge(sem(f"xslot{b4}_loaded"), xv)
                dve.scalar_tensor_tensor(out=accv[:, t, :], in0=accv[:, t, :], scalar=f4[:, bass.ds(t, 1)],
                                         in1=xslot[b4], op0=ALU.mult, op1=ALU.add).then_inc(sem("fx_done"), 1)
            if not first:
                rows_out(t - 1, D2, h2in, d2in, 2)

        dve.wait_ge(sem("f4_ready"), 1)
        step1(0, 0, 0, 16, first=True)
        with dve.Fori(0, 6) as i:
            done.enter(i, 4 * 4)
            for k in range(1, 5):
                step1(i * 4 + k, k % 2, k % RING, i * 16 + (32 if k == RING else 16))
            done.leave(6)
        step1(T, T % 2, None, None, last=True)

        def step2(t, b, first=False, last=False):
            if not first:
                rows_out(t - 1, D3, x2, d3in, 3)
            if not last:
                dve.wait_ge(sem("agg_done"), t + (T + 1))
                dve.scalar_tensor_tensor(out=pre[b][:, 0:D2], in0=bank(b, P, D2), scalar=d2out[:, bass.ds(t, 1)],
                                         in1=b2r, op0=ALU.mult, op1=ALU.add).then_inc(sem("pre2_done"), 1)
                normalise(t, pre[b][:, 0:D2], D2, "relu2_done", "xhat2_done")

        step2(0, 0, first=True)
        with dve.Fori(0, 6) as i:
            done.enter(i, 3 * 4)
            for k in range(1, 5):
                step2(i * 4 + k, k % 2)
            done.leave(6)
        step2(T, T % 2, last=True)

        def row_stats(src, stat, mean_var, n):
            done.did(dve.bn_stats(stat, src))
            done.settle()
            done.did(dve.memset(pause, 0.0))
            dve.bn_aggr(mean_var, stat).then_inc(sem(f"var{n}_done"), 1)

        summed = pre[1][:, 0:D]
        post = pre[1][:, D:2 * D]

        def router(t):
            dve.wait_ge(sem("root4_done"), t + 1)
            done.did(dve.reciprocal(rs4, root4))
            done.settle()
            dve.tensor_scalar(xn2[:, t, :], summed, mv4[:, 0:1], rs4, ALU.subtract, ALU.mult).then_inc(
                sem("xn2_done"), 1)
            dve.wait_ge(sem("xn2_done"), t + 1)
            dve.wait_ge(sem("w_done"), t)
            dve.tensor_tensor(post, xn2[:, t, :], wrr, ALU.mult).then_inc(sem("wprod_done"), 1)

        def step3(t, b, first=False):
            buf = pre[0][:, 0:D]
            dve.wait_ge(sem("agg_done"), t + (2 * T + 1))
            s = d3out[:, bass.ds(t, 1)]
            done.did(dve.scalar_tensor_tensor(out=buf, in0=bank(b, P, D), scalar=s, in1=b3r, op0=ALU.mult,
                                              op1=ALU.add))
            done.settle()
            dve.scalar_tensor_tensor(out=buf, in0=bank(b, P, D, D), scalar=s, in1=buf, op0=ALU.mult,
                                     op1=ALU.add).then_inc(sem("pre3_done"), 1)
            dve.wait_ge(sem("pre3_done"), t + 1)
            done.did(dve.tensor_scalar(buf, buf, 0.0, None, ALU.max))
            done.settle()
            row_stats(buf, st3, mv3, 3)
            if not first:
                router(t - 1)
            dve.wait_ge(sem("root3_done"), t + 1)
            done.did(dve.reciprocal(rs3, root3))
            done.did(dve.scalar_tensor_tensor(out=buf, in0=buf, scalar=mv3[:, 0:1], in1=g3r, op0=ALU.subtract,
                                              op1=ALU.mult))
            done.settle()
            dve.wait_ge(sem("sum_done"), t)
            done.did(dve.scalar_tensor_tensor(out=summed, in0=buf, scalar=rs3, in1=accv[:, t, :], op0=ALU.mult,
                                              op1=ALU.add))
            done.settle()
            row_stats(summed, st4, mv4, 4)

        STEP3 = 10
        dve.wait_ge(sem("be3_added"), T)
        dve.wait_ge(sem("lo3_done"), T)
        step3(0, 0, first=True)
        with dve.Fori(0, 6) as i:
            done.enter(i, STEP3 * 4)
            for k in range(1, 5):
                step3(i * 4 + k, k % 2)
            done.leave(6)
        router(T - 1)
        dve.wait_ge(sem("w_done"), T)
        done.did(dve.tensor_scalar(wv, wv, brc[:, 0:1], None, ALU.add))
        done.settle()
        dve.tensor_scalar(pref, wv, -1.0, None, ALU.mult).then_inc(sem("negw_done"), 1)
        dve.wait_ge(sem("wall_loaded"), 16)

        def count_above(t):
            done.settle()
            done.did(dve.tensor_scalar(gtjunk, wall, wv[:, t:t + 1], 0.0, ALU.is_gt, ALU.add,
                                       accum_out=gt[:, t:t + 1]))

        def take_y(t):
            dve.wait_ge(sem("yffn_done"), t + 1)
            dve.tensor_tensor(x_rows[:, t, :], bank(3 - t % G % 2, P, D), fb2r, ALU.add).then_inc(
                sem("yffn_evac"), 1)

        def finish(t):
            dve.wait_ge(sem("yffn_evac"), t + 1)
            dve.scalar_tensor_tensor(out=accv[:, t, :], in0=x_rows[:, t, :], scalar=wsel[:, t:t + 1],
                                     in1=accv[:, t, :], op0=ALU.mult, op1=ALU.add).then_inc(
                sem("final_done"), 1)

        for c in range(COUNTED):
            for t in range(c * T // COUNTED, (c + 1) * T // COUNTED):
                count_above(t)
            for t in range(c * G, c * G + G):
                take_y(t)
        done.settle()
        dve.wait_ge(sem("sign_done"), T)
        done.did(dve.tensor_tensor(sg, sg, gt, ALU.subtract))
        done.did(dve.tensor_scalar(cc, gt, float(KSEL), None, ALU.is_lt))
        done.settle()
        done.did(dve.tensor_scalar(sg, sg, float(N), float(KSEL), ALU.add, ALU.is_gt))
        done.settle()
        done.did(dve.tensor_tensor(bnd, sg, cc, ALU.mult))
        done.did(dve.memset(cd, 0.0))
        done.settle()
        dve.tensor_tensor_scan(pref, bnd, cd, 0.0, ALU.add, ALU.add).then_inc(sem("prefix_done"), 1)
        for t in range(COUNTED * G, T - G):
            take_y(t)
        dve.wait_ge(sem("before_done"), 1)
        done.did(dve.tensor_tensor(pref, pref, bnd, ALU.subtract))
        dve.tensor_copy(n4[:, 0:1], bank(0, P, 1)).then_inc(sem("before_read"), 1)
        dve.wait_ge(sem("before_read"), 1)
        done.settle()
        done.did(dve.tensor_scalar(pref, pref, n4[:, 0:1], None, ALU.add))
        done.settle()
        done.did(dve.tensor_tensor(pref, pref, gt, ALU.add))
        done.settle()
        done.did(dve.tensor_scalar(pref, pref, float(KSEL), None, ALU.is_lt))
        done.did(dve.tensor_scalar(cd, bnd, -1.0, 1.0, ALU.mult, ALU.add))
        done.settle()
        done.did(dve.tensor_tensor(pref, pref, bnd, ALU.mult))
        done.did(dve.tensor_tensor(cd, cd, cc, ALU.mult))
        done.settle()
        done.did(dve.tensor_tensor(pref, pref, cd, ALU.add))
        done.settle()
        done.did(dve.tensor_tensor(wsel, pref, wv, ALU.mult))
        done.settle()
        dve.wait_ge(sem("xn2_added"), NC)
        for t in range(T - G):
            finish(t)
        for t in range(T - G, T):
            take_y(t)
            finish(t)

    @block.scalar
    def _(act):
        done = Steps(act, sem("act_steps"))
        for b in range(PB):
            both_oh = onehot[b % 2][0]
            act.wait_ge(sem("offset_done"), 2 * b + 2)
            done.did(act.activation(both_oh, both_oh, ACT.Square))
            done.settle()
            act.activation(both_oh, both_oh, ACT.Relu, scale=-1.0, bias=ones[:P, 0:1]).then_inc(
                sem("onehot_done"), 1)
        act.wait_ge(sem("eps_ready"), 1)
        act.wait_ge(sem("xvar_done"), 1)
        act.activation(rstd, ca, ACT.Sqrt).then_inc(sem("xroot_done"), 1)
        act.wait_ge(sem("ratio2_done"), 1)
        act.activation(cb, cb, ACT.Sqrt, scale=float(D)).then_inc(sem("norm_done"), 1)
        act.wait_ge(sem("ratio_done"), 1)
        act.activation(cd, cc, ACT.Ln).then_inc(sem("log_done"), 1)
        act.wait_ge(sem("ident_ready"), 3)
        for c in range(NC):
            for k in range(2):
                act.wait_ge(sem("trz_done"), 3 * c + k + 1)
                act.copy(zT[:, k, c * CW:c * CW + 4 * P], bank(4 + k, 128, 4 * P)).then_inc(sem("zT_done"), 1)
            act.wait_ge(sem("trz_done"), 3 * c + 3)
            act.copy(zT[:, :, c * CW + 4 * P:c * CW + 5 * P],
                     bank(6, 128, 2 * P).rearrange("p (k q) -> p k q", k=2)).then_inc(sem("zT_done"), 1)
        act.wait_ge(sem("zsum_done"), 1)
        act.copy(zrow, bank(3, 1, D)).then_inc(sem("zrow_done"), 1)
        act.wait_ge(sem("dinv_read"), 1)
        act.activation(dinv, dinv, ACT.Sqrt).then_inc(sem("droot_done"), 1)
        act.wait_ge(sem("layerw_loaded"), 48)
        act.wait_ge(sem("cols_loaded"), 80)
        junk = sqw
        for L, (w, nk, width, g, be) in enumerate(((w2, 8, D2, g1c, be1c), (w3, 4, D3, g2c, be2c))):
            o = 8 * L
            for k in range(nk):
                done.settle()
                done.did(act.activation(junk[:, 0:width], w[:, k, :], ACT.Square,
                                        accum_out=ssw[:, o + k:o + k + 1]))
                done.settle()
                done.did(act.activation(junk[:, 0:width], w[:, k, :], ACT.Square, scale=g[:, k:k + 1],
                                        accum_out=ssg[:, o + k:o + k + 1]))
            done.settle()
            last = act.activation(ssb[:, o:o + nk], be, ACT.Square)
            last.then_inc(sem("squares_done"), 1)

        act.wait_ge(sem("bnvar_done"), 1)
        act.activation(tmp6, tmp6, ACT.Sqrt, bias=eps).then_inc(sem("bnroot_done"), 1)
        act.wait_ge(sem("bounds_done"), 1)
        act.activation(bound[:, 0:6], bank(6, 128, 6, 16), ACT.Sqrt).then_inc(sem("bounds_read"), 1)
        act.wait_ge(sem("bn_done"), 1)
        act.preload_act_table(ACT.Sqrt)
        with act.Fori(0, NC) as i:
            def square(dst_slot, src, name, n, c):
                act.wait_ge(sem("nc_done"), i * 12 + c - 2 if c >= 2 else i * 12)
                act.activation(dst_slot, src, ACT.Square).then_inc(sem("sq_done"), 1)
            for m in range(NT):
                act.wait_ge(sem("qkv_done"), i * NT + (m + 1))
                if m == 0:
                    act.wait_ge(sem("res_done"), i * G)
                act.activation(halves(hT[:, m, :]), pair(m % 2), ACT.Relu, scale=bns[:, m:m + 1],
                               bias=bnt[:, m:m + 1]).then_inc(sem("h_done"), 1)
                act.wait_ge(sem("h_done"), i * NT + (m + 1))
                square(sq[:, m % 3, :], hT[:, m, :], "h", m, m)
            for m in range(NT):
                act.wait_ge(sem("s_evac"), i * NT + (m + 1))
                square(halves(sq[:, m % 3, :]), pair(m % 2), "s", m, NT + m)
            act.wait_ge(sem("u_done"), i + 1)
            act.activation(veps, umax, ACT.Sqrt, scale=1e-30).then_inc(sem("veps_done"), 1)
            for n in range(4):
                act.wait_ge(sem("o_done"), i * 4 + (n + 1))
                src, half = (hT, n) if n < 2 else (sT, n - 2)
                act.activation(src[:, 2 + half, :], src[:, half, :], ACT.Square).then_inc(sem("osq_done"), 1)
            act.wait_ge(sem("cols_done"), i + 1)
            act.activation(ocol, bank(6, P, G, 16), ACT.Sqrt, scale=1.0 / RMAX ** 2).then_inc(sem("ocol_read"), 1)
            for j in range(G):
                t = i * G + j
                act.wait_ge(sem("ft_done"), t + 1)
                act.wait_ge(sem("n4_done"), t)
                act.activation(sqjunk, accv[:, t, :], ACT.Square, accum_out=n4[:, bass.ds(t, 1)]).then_inc(
                    sem("n4_done"), 1)
        act.wait_ge(sem("n4_done"), T)
        act.activation(n4, n4, ACT.Sqrt).then_inc(sem("n4root_done"), 1)
        act.wait_ge(sem("n4_ready"), 1)
        act.activation(f4, n4, ACT.Tanh).then_inc(sem("tanh_done"), 1)
        act.preload_act_table(ACT.Sqrt)

        def turn_in(t, k_tiles, g, be, layer):
            act.wait_ge(sem(f"trx{layer}_done"), t + 1)
            act.wait_ge(sem(f"h{layer}_done"), t)
            for k in range(k_tiles):
                last = act.activation(xT[:, k, :], bank(5 + k // 4, 128, P, (k % 4) * P), ACT.Identity,
                                      scale=g[:, k:k + 1], bias=be[:, k:k + 1])
            last.then_inc(sem(f"xT{layer}_done"), 1)

        def root(t, n):
            act.wait_ge(sem(f"var{n}_done"), t + 1)
            act.activation(root2, mv2[:, 1:2], ACT.Sqrt, bias=eps[:P]).then_inc(sem(f"root{n}_done"), 1)

        def high(t, width, tile, layer):
            act.wait_ge(sem(f"hbuf{layer}_done"), t + 1)
            act.copy(tile[:, t, 0, :], hbuf[:, 0:width]).then_inc(sem(f"hi{layer}_done"), 1)

        def step1(t, b, first=False, last=False):
            if not last:
                act.wait_ge(sem("agg_done"), t + 1)
                act.wait_ge(sem("y_done"), t)
                act.copy(yhi, bank(b, P, D)).then_inc(sem("yhi_done"), 1)
                act.wait_ge(sem("try_done"), t + 1)
                act.wait_ge(sem("p1_done"), t)
                act.copy(yT, bank(2, 128, 2 * P).rearrange("p (k q) -> p k q", k=2)).then_inc(sem("yT_done"), 1)
            if not first:
                turn_in(t - 1, 8, g1c, be1c, 2)
            if not last:
                act.wait_ge(sem("pre1_done"), t + 1)
                act.activation(pre[b], pre[b], ACT.Relu).then_inc(sem("relu1_done"), 1)
                root(t, 1)
            if not first:
                high(t - 1, D2, h2in, 2)

        act.wait_ge(sem("rows1_ready"), T)
        step1(0, 0, first=True)
        with act.Fori(0, 6) as i:
            for k in range(1, 5):
                step1(i * 4 + k, k % 2)
        step1(T, 1, last=True)

        def step2(t, b, first=False, last=False):
            if not first:
                turn_in(t - 1, 4, g2c, be2c, 3)
                high(t - 1, D3, x2, 3)
            if not last:
                act.wait_ge(sem("pre2_done"), t + 1)
                act.activation(pre[b][:, 0:D2], pre[b][:, 0:D2], ACT.Relu).then_inc(sem("relu2_done"), 1)
                root(t, 2)

        step2(0, 0, first=True)
        with act.Fori(0, 6) as i:
            for k in range(1, 5):
                step2(i * 4 + k, k % 2)
        step2(T, 1, last=True)

        def root3_(t):
            act.wait_ge(sem("var3_done"), t + 1)
            act.activation(root3, mv3[:, 1:2], ACT.Sqrt, bias=eps[:P]).then_inc(sem("root3_done"), 1)

        def root4_(t):
            act.wait_ge(sem("var4_done"), t + 1)
            act.activation(root4, mv4[:, 1:2], ACT.Sqrt, bias=eps[:P]).then_inc(sem("root4_done"), 1)
            act.copy(accv[:, t, :], pre[1][:, 0:D]).then_inc(sem("sum_done"), 1)

        def router_sum(t):
            act.wait_ge(sem("wprod_done"), t + 1)
            act.activation(pre[1][:, D:2 * D], pre[1][:, D:2 * D], ACT.Identity,
                           accum_out=wv[:, bass.ds(t, 1)]).then_inc(sem("w_done"), 1)

        root3_(0)
        root4_(0)
        with act.Fori(1, T) as t:
            root3_(t)
            router_sum(t - 1)
            root4_(t)
        router_sum(T - 1)

        act.wait_ge(sem("negw_done"), 1)
        act.wait_ge(sem("wall_loaded"), 16)
        act.preload_act_table(ACT.Gelu_apprx_tanh)
        for i in range(NC):
            for k in range(2):
                act.wait_ge(sem("trn_done"), i + 1)
                act.wait_ge(sem("hid_done"), i * 8)
                act.copy(nT[:, k, 0:4 * P], bank(k, 128, 4 * P)).then_inc(sem("nT_done"), 1)
            act.copy(nT[:, :, 4 * P:5 * P], bank(2, 128, 2 * P).rearrange("p (k q) -> p k q", k=2)).then_inc(
                sem("nT_done"), 1)
            for m in range(8):
                act.wait_ge(sem("hid_done"), i * 8 + (m + 1))
                if m == 0:
                    act.wait_ge(sem("yffn_done"), i * G)
                act.activation(halves(gT[:, m, :]), pair(2 + m % 2), ACT.Gelu_apprx_tanh,
                               bias=fb1c[:, m:m + 1]).then_inc(sem("gelu_done"), 1)
            if i < COUNTED:
                for t in range(i * T // COUNTED, (i + 1) * T // COUNTED):
                    act.wait_ge(sem("sign_done"), t)
                    act.activation(sgjunk, wall, ACT.Sign, bias=pref[:, t:t + 1],
                                   accum_out=sg[:, t:t + 1]).then_inc(sem("sign_done"), 1)

    @block.tensor
    def _(pe):
        def mm(o, l, r, start, stop):
            return pe.matmul(o, l, r, start=start, stop=stop)

        pe.wait_ge(sem("ident_ready"), 3)
        pe.wait_ge(sem("flag_part"), 1)
        mm(bank(7, 1, 1), ones[:P, 0:1], flagf[:P], True, True).then_inc(sem("flag_sum"), 1)

        pe.wait_ge(sem("flag_ready"), 1)
        def degree(b):
            both_oh, ohp, oht = onehot[b % 2]
            pe.wait_ge(sem("onehot_done"), b + 1)
            for j in range(EB):
                last = mm(bank(7, P, T), ohp[:, j, :], oht[:, j, :], b + j == 0, b == EC // EB - 1 and j == EB - 1)
            last.then_inc(sem("degree_used"), 1)

        for b in range(PB):
            degree(b)

        for c in range(NC):
            for k in range(2):
                pe.wait_ge(sem("z_done"), G * c + 4)
                pe.wait_ge(sem("zT_done"), 3 * c - 3 + k + 1 if c else 0)
                for j in range(4):
                    last = pe.transpose(bank(4 + k, 128, P, j * P), zv[:, G * c + j, k * 128:(k + 1) * 128],
                                        ident[:P, 0:P])
                last.then_inc(sem("trz_done"), 1)
            pe.wait_ge(sem("z_done"), G * c + 5)
            pe.wait_ge(sem("zT_done"), 3 * c)
            for k in range(2):
                last = pe.transpose(bank(6, 128, P, k * P), zv[:, G * c + 4, k * 128:(k + 1) * 128], ident[:P, 0:P])
            last.then_inc(sem("trz_done"), 1)
        for t in range(T):
            for m in range(2):
                mm(bank(m, 128, D), zv[:, t, m * 128:(m + 1) * 128], zv[:, t, :], t == 0, False)
            last = mm(bank(3, 1, D), ones[:P, 0:1], zv[:, t, :], t == 0, t == T - 1)
        last.then_inc(sem("zsum_done"), 1)
        for b in range(PB, EC // EB):
            degree(b)
        pe.wait_ge(sem("nzrow_done"), 1)
        for m in range(2):
            mm(bank(m, 128, D), nzrow[:, m * 128:(m + 1) * 128], zrow, False, True)
        for k in range(2):
            last = mm(bank(2, 128, 1, k), zrow[:, k * 128:(k + 1) * 128], ones[0:1, 0:1], True, True)
        last.then_inc(sem("gram_done"), 1)
        pe.wait_ge(sem("gram_copied"), 1)
        pe.wait_ge(sem("mixw_loaded"), 16 * 10)
        pe.wait_ge(sem("zT_done"), 3 * NC)
        pe.wait_ge(sem("dinv_read"), 1)
        for m in range(2):
            for n0, n1, b in ((0, 512, 4 + 2 * m), (512, 768, 5 + 2 * m)):
                for k in range(2):
                    last = mm(bank(b, 128, n1 - n0), gram[:, k, m * 128:(m + 1) * 128], wq[:, k, n0:n1],
                              k == 0, k == 1)
        last.then_inc(sem("gw_done"), 1)
        pe.wait_ge(sem("wgw_done"), 2)
        pe.wait_ge(sem("zrow_done"), 1)
        for m in range(NT):
            for k in range(2):
                mm(bank(3, 128, 1, m), gw[:, k, m * 128:(m + 1) * 128], ones[:, 0:1], k == 0, k == 1)
            for k in range(2):
                last = mm(bank(3, 128, 1, 16 + m), wq[:, k, m * 128:(m + 1) * 128], zcol[:, k:k + 1],
                          k == 0, k == 1)
        last.then_inc(sem("bnsum_done"), 1)
        pe.wait_ge(sem("squares_done"), 2)
        n = 0
        for L, nk in ((0, 8), (1, 4)):
            for s in (ssw, ssg, ssb):
                for k in range(nk):
                    last = mm(bank(6, 128, 1, 16 + n), ones[:, :], s[:, 8 * L + k:8 * L + k + 1], k == 0, k == nk - 1)
                n += 1
        last.then_inc(sem("bounds_done"), 1)

        pe.wait_ge(sem("bn_done"), 1)
        pe.wait_ge(sem("wp_done"), 1)
        pe.wait_ge(sem("bounds_read"), 1)
        with pe.Fori(0, NC) as i:
            def norm2(c):
                pe.wait_ge(sem("sq_done"), i * 12 + (c + 1))
                for h in range(2):
                    last = mm(bank(4 + h, 128, CH), ones[:, :], sq[:, c % 3, h * CH:(h + 1) * CH], c == 0, c == 11)
                last.then_inc(sem("nc_done"), 1)

            for m in range(NT):
                if m < 2:
                    pe.wait_ge(sem("s_evac"), i * NT)
                    pe.wait_ge(sem("sq_done"), i * 12)
                else:
                    pe.wait_ge(sem("h_done"), i * NT + (m - 1))
                for k in range(2):
                    for h in range(2):
                        last = mm(bank(2 * (m % 2) + h, 128, CH), wq[:, k, m * 128:(m + 1) * 128],
                                  zT[:, k, bass.ds(i * CW + h * CH, CH)], k == 0, k == 1)
                last.then_inc(sem("qkv_done"), 1)
                if m == 2:
                    pe.wait_ge(sem("ft_done"), i * G)
                if m >= 2:
                    norm2(m - 2)
            for m in range(NT):
                if m < 2:
                    pe.wait_ge(sem("h_done"), i * NT + (m + 5))
                else:
                    pe.wait_ge(sem("s_evac"), i * NT + (m - 1))
                    pe.wait_ge(sem("sq_done"), i * 12 + (NT + m - 1))
                pe.wait_ge(sem("h_done"), i * NT + (m + 1))
                for h in range(2):
                    last = mm(bank(2 * (m % 2) + h, 128, CH), wp[:, m, :], hT[:, m, h * CH:(h + 1) * CH], True, True)
                last.then_inc(sem("s_done"), 1)
                norm2(m + 4)
            norm2(10)
            norm2(11)
            for n in range(4):
                src, half = (hT, n) if n < 2 else (sT, n - 2)
                pe.wait_ge(sem("qk_done"), i * 4 + n)
                if n == 0:
                    pe.wait_ge(sem("ucol_read"), i)
                    pe.wait_ge(sem("ocol_read"), i)
                if n == 2:
                    pe.wait_ge(sem("s_evac"), i * NT + 4)
                for h in range(2):
                    last = mm(bank(6 + h, 128, CH), kones[:, :], src[:, 2 + half, h * CH:(h + 1) * CH], True, True)
                last.then_inc(sem("k_done"), 1)
            pe.wait_ge(sem("u_done"), i + 1)
            pe.wait_ge(sem("qk_done"), i * 4 + 4)
            for j in range(G):
                mm(bank(6, P, 1, j), umax[0:1, j * P:(j + 1) * P], ones[0:1, 0:1], True, True)
            pe.wait_ge(sem("osq_done"), i * 4 + 4)
            for j in range(G):
                for n in range(4):
                    src, half = (hT, n) if n < 2 else (sT, n - 2)
                    last = mm(bank(6, P, 1, 16 + j), src[:, 2 + half, j * P:(j + 1) * P], ones[:, 0:1], n == 0, n == 3)
            last.then_inc(sem("cols_done"), 1)
            for j in range(G):
                if j >= 2:
                    pe.wait_ge(sem("ft_done"), i * G + (j - 1))
                for n in range(4):
                    src, half = (hT, n) if n < 2 else (sT, n - 2)
                    last = mm(bank(4 + j % 2, P, D), src[:, half, j * P:(j + 1) * P], wres[:, n, :], n == 0, n == 3)
                last.then_inc(sem("res_done"), 1)

        def aggregate(layer, t, slot, b, parts, visit, free_sem, free_at, between=()):
            pe.wait_ge(sem(f"ring_loaded{slot}"), visit)
            if free_at is not None:
                pe.wait_ge(sem(free_sem), free_at)
            for s in range(T):
                for at_s, work in between:
                    if s == at_s:
                        work()
                for h in range(len(parts)):
                    last = mm(bank(b, P, 512), ring[slot][:, s, :], parts[h](s), s == 0 and h == 0,
                              s == T - 1 and h == len(parts) - 1)
            last.then_inc(sem("agg_done"), 1)

        both = [lambda s: x2[:, s, :, :].rearrange("p h d -> p (h d)")]
        wide = [lambda s: h2in[:, s, 0, :], lambda s: h2in[:, s, 1, :]]
        SLOT0 = (T + RING - 1) // RING

        def visits(layer, slot):
            return layer * (SLOT0 if slot == 0 else SLOT0 - 1)

        def turn(t, b, k_tiles, layer):
            pe.wait_ge(sem(f"xhat{layer - 1}_done"), t + 1)
            pe.wait_ge(sem(f"xT{layer}_done"), t)
            for k in range(k_tiles):
                last = pe.transpose(bank(5 + k // 4, 128, P, (k % 4) * P), pre[b][:, k * 128:(k + 1) * 128],
                                    ident[:P, 0:P])
            last.then_inc(sem(f"trx{layer}_done"), 1)

        def product(t, k_tiles, w, width, layer):
            pe.wait_ge(sem(f"xT{layer}_done"), t + 1)
            pe.wait_ge(sem(f"hbuf{layer}_done"), t)
            for k in range(k_tiles):
                last = mm(bank(7, P, width), xT[:, k, :], w[:, k, :], k == 0, k == k_tiles - 1)
            last.then_inc(sem(f"h{layer}_done"), 1)

        def step1(t, k, i, first=False, last=False):
            b, slot = k % 2, k % RING
            if not last:
                it = 1 if i is None else (i * 16 + (32 if slot == 0 else 16))
                aggregate(0, t, slot, b, both, 16 if i is None else it, "y_done", t - 1 if i is not None else None)
            if not first:
                turn(t - 1, (k - 1) % 2, 8, 2)
            if not last:
                pe.wait_ge(sem("y_done"), t + 1)
                pe.wait_ge(sem("yT_done"), t)
                for c in range(2):
                    z = pe.transpose(bank(2, 128, P, c * P), ysum[:, c * 128:(c + 1) * 128], ident[:P, 0:P])
                z.then_inc(sem("try_done"), 1)
                pe.wait_ge(sem("yT_done"), t + 1)
                pe.wait_ge(sem("pre1_done"), t)
                for h in range(2):
                    for c in range(2):
                        z = mm(bank(3 + h, P, 512), yT[:, c, :], w1[:, c, h * 512:(h + 1) * 512], c == 0, c == 1)
                z.then_inc(sem("p1_done"), 1)
            if not first:
                product(t - 1, 8, w2, D2, 2)

        pe.wait_ge(sem("rows1_ready"), T)
        pe.wait_ge(sem("ft_done"), T)
        step1(0, 0, None, first=True)
        with pe.Fori(0, 6) as i:
            for k in range(1, 5):
                step1(i * 4 + k, k, i)
        step1(T, T, 0, last=True)

        def step2(t, k, i, first=False, last=False):
            b, slot = k % 2, k % RING
            previous = [] if first else [
                (12, lambda: turn(t - 1, (k - 1) % 2, 4, 3)),
                (19, lambda: product(t - 1, 4, w3, D3, 3))]
            if last:
                for _, work in previous:
                    work()
                return
            v = 16 * visits(1, slot)
            it = v + 16 if i is None else i * 16 + (v + (32 if slot == 0 else 16))
            if i is None:
                aggregate(1, t, slot, b, wide, it, None, None)
            else:
                aggregate(1, t, slot, b, wide, it, "pre2_done", t - 1, previous)

        pe.wait_ge(sem("lo2_done"), T)
        step2(0, 0, None, first=True)
        with pe.Fori(0, 6) as i:
            for k in range(1, 5):
                step2(i * 4 + k, k, i)
        step2(T, T, 0, last=True)

        pe.wait_ge(sem("lo3_done"), T)
        def step3(t, k, i):
            b, slot = k % 2, k % RING
            v = 16 * visits(2, slot)
            it = v + 16 if i is None else i * 16 + (v + (32 if slot == 0 else 16))
            if i is None:
                aggregate(2, t, slot, b, both, it, None, None)
            else:
                aggregate(2, t, slot, b, both, it, "pre3_done", t - 1)
        step3(0, 0, None)
        with pe.Fori(0, 6) as i:
            for k in range(1, 5):
                step3(i * 4 + k, k, i)

        pe.wait_ge(sem("ffnw_loaded"), 32)
        pe.wait_ge(sem("pre3_done"), T)
        pe.wait_ge(sem("npad_done"), 1)
        for i in range(NC):
            pe.wait_ge(sem("stage_done"), i + 1)
            pe.wait_ge(sem("nT_done"), i * 3)
            pe.wait_ge(sem("yffn_evac"), i * G)
            if i == COUNTED + 1:
                pe.wait_ge(sem("before_read"), 1)
            for k in range(2):
                for j in range(4):
                    pe.transpose(bank(k, 128, P, j * P), stage[:, j, k * 128:(k + 1) * 128], ident[:P, 0:P])
                last = pe.transpose(bank(2, 128, P, k * P), stage[:, 4, k * 128:(k + 1) * 128], ident[:P, 0:P])
            last.then_inc(sem("trn_done"), 1)
            pe.wait_ge(sem("nT_done"), i * 3 + 3)
            for m in range(8):
                pe.wait_ge(sem("gelu_done"), i * 8 + (m - 1 if m >= 2 else 0))
                for k in range(2):
                    for h in range(2):
                        last = mm(bank(4 + 2 * (m % 2) + h, 128, CH), f1[:, k, m * 128:(m + 1) * 128],
                                  nT[:, k, h * CH:(h + 1) * CH], k == 0, k == 1)
                last.then_inc(sem("hid_done"), 1)
            pe.wait_ge(sem("gelu_done"), i * 8 + 8)
            for j in range(G):
                pe.wait_ge(sem("yffn_evac"), i * G + (j - 1 if j >= 2 else 0))
                for m in range(8):
                    last = mm(bank(3 - j % 2, P, D), gT[:, m, j * P:(j + 1) * P], f2[:, m, :], m == 0, m == 7)
                last.then_inc(sem("yffn_done"), 1)
            if i == COUNTED:
                pe.wait_ge(sem("tri"), 2)
                pe.wait_ge(sem("prefix_done"), 1)
                mm(bank(0, P, 1), tri[:P, 0:P], pref[:, T - 1:T], True, True).then_inc(sem("before_done"), 1)


def _plan(v):
    pad = lambda e, fill: np.concatenate([np.full(PADE, fill, e.dtype), e, np.full(PADE, fill, e.dtype)])
    order = np.concatenate([np.arange(32 * g, 32 * g + 32) for k in range(3) for g in range(k, 24, 3)])
    tiles = lambda x: np.ascontiguousarray(x.reshape(-1, 128).T)
    wpw = v["L0_mix_w_pw"][order, :, 0].reshape(NT, 4, 32, 32).transpose(1, 3, 0, 2)
    return {
        "x": v["x"], "src_pad": pad(v["src"], 100000), "dst_pad": pad(v["dst"], 75000),
        "w1": v["L0_gnn_W1"], "w2": v["L0_gnn_W2"], "w3": v["L0_gnn_W3"],
        "b1": v["L0_gnn_b1"], "b2": v["L0_gnn_b2"], "b3": v["L0_gnn_b3"],
        "g1": tiles(v["L0_gnn_g1"]), "be1": tiles(v["L0_gnn_beta1"]),
        "g2": tiles(v["L0_gnn_g2"]), "be2": tiles(v["L0_gnn_beta2"]),
        "g3": v["L0_gnn_g3"], "be3": v["L0_gnn_beta3"],
        "wq": np.ascontiguousarray(v["L0_mix_w_qkv"][order, :, 2].T),
        "bng": tiles(v["L0_mix_bn_gamma"][order]), "bnb": tiles(v["L0_mix_bn_beta"][order]),
        "wdw": tiles(v["L0_mix_w_dw"][order, 0, 2]), "wpw": np.ascontiguousarray(wpw),
        "wres": np.ascontiguousarray(v["L0_mix_w_res"][:, :, 0].T), "bres": v["L0_mix_b_res"],
        "wr": v["L0_ffn_wr"][:, 0], "br": v["L0_ffn_br"], "f1": v["L0_ffn_w1"],
        "fb1": tiles(v["L0_ffn_b1"]), "f2": v["L0_ffn_w2"], "fb2": v["L0_ffn_b2"],
    }


def kernel(**inputs):
    import concourse.bacc as bacc
    from concourse.bass_utils import run_bass_kernel_spmd

    nc = bacc.Bacc("TRN2", target_bir_lowering=False, num_devices=1)
    arrays, aps = {}, {}
    for name, x in _plan({k: np.asarray(x) for k, x in inputs.items()}).items():
        x = np.ascontiguousarray(x)
        arrays[f"in_{name}"] = x
        aps[name] = nc.dram_tensor(f"in_{name}", x.shape, mybir.dt.from_np(x.dtype), kind="ExternalInput").ap()
    out = nc.dram_tensor("out", (N, D), F32, kind="ExternalOutput").ap()
    scratch = {"counts": nc.dram_tensor("counts", (T, P, N), F16).ap(), "w": nc.dram_tensor("w_nodes", (N,), F32).ap()}
    build(nc, aps, out, scratch)
    return run_bass_kernel_spmd(nc, [arrays], core_ids=[0]).results[0]["out"]
```

```python
from contextlib import ExitStack

import numpy as np
import concourse.bass as bass
from concourse import mybir

F32 = mybir.dt.float32
F16 = mybir.dt.float16
BF16 = mybir.dt.bfloat16
I32 = mybir.dt.int32
ALU = mybir.AluOpType
ACT = mybir.ActivationFunctionType
AX = mybir.AxisListType.X

N = 3125
E = 53125
P = 125
T = N // P
G = 5
D = 256
D1, D2, D3 = 1024, 512, 256
CW = G * P + 1
CH = CW // 2
NC = T // G
EC = E // P
HALO = 40
EW = EC + 2 * HALO
NWIN = -(-E // HALO)
EB = 25
PADE = NWIN * HALO + HALO
HUGE = 3e38
SB = EC // 5
KSEL = N // 2 - 1
EPS = 1e-5
F16_TOP = 32000.0
X_SCALE = 2048.0
BALL = float(np.float32(1.0 - 1e-5))
RMAX = float(np.arctanh(np.float64(np.float32(1.0 - 1e-5))))
ROUND = 1.5 * 2 ** 23
NT = 6
NORMED = 256.0
GR = 4
ACT_COUNTS = 7
COUNTED = 4
PB = 8
RING = 4
XHAT = 256.0
HEAD = 5
LOOPS = (T - HEAD) // RING


ACT_MILESTONES = (
    "ident16_ready", "xroot_done", "norm_done", "log_done", "zrow_done", "droot_done", "bnroot_done",
    "bounds_read", "n4root_done", "tanh_done", "fnorm_done",
)
DVE_MILESTONES = (
    "keys_ready", "flag_part", "flag_ready", "edges_ready", "xvar_done", "ratio2_done", "ratio_done",
    "dinv_read", "nzrow_done", "gram_copied", "wp_done", "bnvar_done", "bn_done", "be2w_read",
    "n4_ready", "f4_ready", "fscale_done", "router_done", "negw_done", "least_done", "last_done",
    "prefix_done", "before_read",
)
AFTER = {name: n + 1 for names in (ACT_MILESTONES, DVE_MILESTONES) for n, name in enumerate(names)}


class Steps:

    def __init__(self, eng, sem):
        self.eng, self.sem, self.base, self.k = eng, sem, 0, 0

    def did(self, ins):
        ins.then_inc(self.sem, 1)
        self.k += 1

    def settle(self):
        self.eng.wait_ge(self.sem, self.base + self.k)

    def enter(self, i, per):
        self.outer, self.per = self.k, per
        self.base, self.k = i * per + self.outer, 0

    def leave(self, times):
        assert self.k == self.per, (self.k, self.per)
        self.base, self.k = 0, self.outer + times * self.per


def free(ap, offset, dims):
    return bass.AP(ap.tensor, ap.offset + offset, [list(ap.ap[0])] + [list(d) for d in dims])


def build(nc, a, out, scratch):
    with ExitStack() as ctx:
        _build(ctx, nc, a, out, scratch)


def _build(ctx, nc, a, out, scratch):
    counts_dram, w_dram = scratch["counts"], scratch["w"]

    def sb(name, shape, dt):
        return ctx.enter_context(nc.sbuf_tensor(name, shape, dt))

    sems = {}

    def sem(name):
        if name not in sems:
            sems[name] = ctx.enter_context(nc.semaphore(name))
        return sems[name]

    def milestone(name):
        return sem("act_milestones" if name in ACT_MILESTONES else "dve_milestones")

    psum = ctx.enter_context(nc.psum_tensor("psum", [128, 8, 512], F32))
    rows = sb("rows", [128, T * D], F32)
    acc = sb("acc", [128, T * D], F32)
    big = sb("big", [128, 12800], F32)
    wa = sb("wa", [128, 2048], F32)
    wb = sb("wb", [128, 4096], F32)
    wc = sb("wc", [128, 1024], F32)
    wm = sb("wm", [128, 3328], F32)
    scr = sb("scr", [128, 15328], F32)
    ident = sb("ident", [128, 128], F32)
    ones = sb("ones", [128, 128], F32)
    ident16 = sb("ident16", [128, 128], F16)
    kones = sb("kones", [128, 128], F32)
    col = sb("col", [128, 998], F32)

    at = {"scr": 0, "col": 0, "wm": 0, "big": 0}

    def take(region, n):
        t = {"scr": scr, "col": col, "wm": wm, "big": big}[region]
        o = at[region]
        at[region] = o + n
        assert at[region] <= t.shape[1], (region, at[region])
        return t[:, o:o + n]

    x_rows = rows[:P, :].rearrange("p (t d) -> p t d", t=T)
    x2 = rows[:P, :].bitcast(F16).rearrange("p (t h d) -> p t h d", t=T, h=2)
    accv = acc[:P, :].rearrange("p (t d) -> p t d", t=T)
    zv = accv
    zT = take("big", 2 * NC * CW).rearrange("p (k c) -> p k c", k=2)
    hT0 = take("big", NT * CW).rearrange("p (m c) -> p m c", m=NT)
    sq = take("big", 3 * CW).rearrange("p (m c) -> p m c", m=3)
    umax = take("big", CW)
    h2in = big[:P, :].bitcast(F16).rearrange("p (t h d) -> p t h d", t=T, h=2)
    xn2 = big[:P, 0:6400].rearrange("p (t d) -> p t d", t=T)
    gT16 = big[:, 6400:6400 + GR * CW].bitcast(F16).rearrange("p (m h c) -> p m h c", m=GR, h=2)
    gtemp = [big[:, 6400 + (GR + s) * CW:6400 + (GR + 1 + s) * CW] for s in range(GR)]
    nT16 = [big[:, 6400 + 2 * GR * CW:6400 + (2 * GR + 2) * CW],
            None]
    w1 = wa[:, :].rearrange("p (k n) -> p k n", k=2)
    w2 = wb[:, :].rearrange("p (k n) -> p k n", k=8)
    w1s = wa[:, :].bitcast(F16).rearrange("p (c h n) -> p c h n", c=4, h=2)
    w2s = wb[:, :].bitcast(F16).rearrange("p (c h n) -> p c h n", c=8, h=2)
    w3 = wc[:, :].rearrange("p (k n) -> p k n", k=4)
    f1 = wa[:, :].rearrange("p (k n) -> p k n", k=2)
    f2 = wb[:, 0:2048].rearrange("p (k n) -> p k n", k=8)
    f1s = wa[:, :].bitcast(F16).rearrange("p (c h n) -> p c h n", c=4, h=2)
    f2s = wb[:, 0:2048].bitcast(F16).rearrange("p (c h n) -> p c h n", c=4, h=2)
    zi = wb[:P, 0:3072].bitcast(F16)
    wq = take("wm", 2 * 768).rearrange("p (k n) -> p k n", k=2)
    wp = take("wm", NT * 128).rearrange("p (m n) -> p m n", m=NT)
    wres = take("wm", 4 * D).rearrange("p (k n) -> p k n", k=4)
    b1r, b2r, b3r = wm[:P, 0:1024], wm[:P, 1024:1536], wm[:P, 1536:1792]
    g3r, be3r = wm[:P, 1792:2048], wm[:P, 2048:2304]
    fb2r, wrr = wm[:P, 2304:2560], wm[:P, 2560:2816]
    sT = take("scr", NT * CW).rearrange("p (m c) -> p m c", m=NT)
    veps = take("scr", CW)
    tdiv = take("scr", CW)
    xbuf = take("scr", G * D)[:P].rearrange("p (t d) -> p t d", t=G)
    gram = take("scr", 512).rearrange("p (k n) -> p k n", k=2)
    bresr = take("scr", 256)[:P]
    sqjunk = take("scr", 256)[:P]
    wdp, wdt = scr[:P, 0:EW], scr[:P, EW:2 * EW]
    gw = scr[:, 0:2 * 768].rearrange("p (k n) -> p k n", k=2)
    wtemp = [scr[:, NT * CW + 512 * s:NT * CW + 512 * s + 512] for s in range(2)]
    sqw = scr[:, NT * CW:NT * CW + 512]
    at_edges = at["scr"]
    esrc_i = take("scr", EW)[:P].bitcast(I32)
    edst_i = take("scr", EW)[:P].bitcast(I32)
    esrc = take("scr", EW)[:P]
    ekey = take("scr", EW)[:P]
    edp = take("scr", EW)[:P]
    edt = take("scr", EW)[:P]
    wkey = take("scr", EW)[:P]
    fwd = take("scr", EC)[:P]
    bwd = take("scr", EC)[:P]
    hTs = [hT0, scr[:, at_edges:at_edges + NT * CW].rearrange("p (m c) -> p m c", m=NT)]
    eidx = take("scr", EC)[:P].bitcast(I32)
    evalue = take("scr", EC // 2 + 1)[:P].bitcast(F16)
    equal = acc[:P, :].bitcast(BF16)
    OW = EB * (P + T)
    onehot = []
    for s in range(2):
        o = 2 * NC * CW + s * OW // 2
        oh = big[:P, o:o + OW // 2].bitcast(BF16)
        onehot.append((oh, oh[:, 0:EB * P].rearrange("p (j q) -> p j q", j=EB),
                       oh[:, EB * P:OW].rearrange("p (j q) -> p j q", j=EB)))
    sidx = take("scr", SB)[:P].bitcast(I32)
    svalue = take("scr", (SB + 1) // 2)[:P].bitcast(F16)
    iop = take("scr", (P + 1) // 2)[:P].bitcast(BF16)
    at["scr"] = at_edges
    ring = take("scr", RING * 1563)[:P].bitcast(F16)
    ring = [ring[:, s * 3126:s * 3126 + N].rearrange("p (t q) -> p t q", t=T) for s in range(RING)]
    nT16[1] = take("scr", 2 * CW)
    nT16 = [x.bitcast(F16).rearrange("p (n c) -> p n c", n=4) for x in nT16]
    be2w = take("scr", 512)[:P]
    at["scr"] = 0
    pre = [take("scr", 1024)[:P] for _ in range(2)]
    xT = take("scr", 8 * P).rearrange("p (k q) -> p k q", k=8)
    xT16 = scr[:, 2048:2048 + 8 * P].bitcast(F16).rearrange("p (h k q) -> p h k q", h=2, k=8)
    x16 = pre[1].bitcast(F16).rearrange("p (h n) -> p h n", h=2)
    y16 = take("scr", D)[:P].bitcast(F16).rearrange("p (h n) -> p h n", h=2)
    ysum, yhi = take("scr", D)[:P], take("scr", D)[:P]
    yT16 = take("scr", 2 * P).bitcast(F16).rearrange("p (h c q) -> p h c q", h=2, c=2)
    xslot = [take("scr", D)[:P] for _ in range(RING)]
    stage = take("scr", G * D)[:P].rearrange("p (t d) -> p t d", t=G)
    hbuf = take("scr", 512)[:P]
    assert at["scr"] <= at_edges
    fjunk = scr[:, 3048:3048 + 1024]
    ftemp = [scr[:, 3048 + 512 * s:3560 + 512 * s] for s in range(2)]
    stage16 = [scr[:P, 2048 + 1280 * s:3328 + 1280 * s].bitcast(F16).rearrange("p (h t d) -> p h t d", h=2, t=G)
               for s in range(2)]
    wall = scr[:P, at_edges:at_edges + N]
    gtjunk = scr[:P, at_edges + N + 1:at_edges + N + 1 + 1563].bitcast(BF16)[:, 0:N]
    above = scr[:P, at_edges + N + 1 + 1563:at_edges + N + 1 + 2 * 1563].bitcast(BF16)[:, 0:N]
    def c_(n):
        return take("col", n)
    stats = c_(T * 6)[:P].rearrange("p (t s) -> p t s", t=T)
    mv = c_(T * 2)[:P].rearrange("p (t s) -> p t s", t=T)
    rstd, dinv, ca, cb, cc, cd = (c_(T)[:P] for _ in range(6))
    dx, d2in, d2out, d3in, d3out = (c_(T)[:P] for _ in range(5))
    st2 = c_(12)[:P].rearrange("p (a s) -> p a s", a=2)
    st3, st4, mv3, mv4 = c_(6)[:P], c_(6)[:P], c_(2)[:P], c_(2)[:P]
    rs3, rs4, root3, root4 = (c_(1)[:P] for _ in range(4))
    mv2, rs2, root2 = c_(2)[:P], c_(1)[:P], c_(1)[:P]
    eps = c_(1)
    bng, bnb, bns, bnt, wdw, tmp6 = (c_(NT) for _ in range(6))
    zcol = c_(2)
    zrow = big[0:1, 10016:10016 + 256]
    nzrow = big[0:1, 10016 + 256:10016 + 512]
    g1c, be1c, fb1c, g2c, be2c = c_(8), c_(8), c_(8), c_(4), c_(4)
    ssw, ssg = c_(12), c_(12)
    ssb = c_(12)
    ss1 = c_(4)
    bound = c_(8)
    w1_scale, w1_back, gw2_scale, gw2_back = (c_(1) for _ in range(4))
    y_scale, y_back, h2_scale = (c_(T)[:P] for _ in range(3))
    eps_x = c_(1)
    ssf, fnorm = c_(5), c_(3)
    f_scale, f_back = c_(2), c_(2)
    g_scale, g_back, hid_back, out_back = (c_(1) for _ in range(4))
    ocol = c_(G)[:P]
    n4, f4 = (c_(T)[:P] for _ in range(2))
    flagf, flagi = c_(1), c_(1).bitcast(I32)
    wv, wsel, gt, sg, bnd, pref, brc = (c_(T)[:P] for _ in range(7))
    tri = kones
    pause, pool_pause = c_(1)[:P], c_(1)[:P]

    wpieces = [(wa[:, c * 512:(c + 1) * 512], w1s[:, c]) for c in range(4)]
    wpieces += [(wb[:, c * 512:(c + 1) * 512], w2s[:, c]) for c in range(8)]

    def bank(b, p, n, o=0):
        return psum[:p, b, o:o + n]

    def turned(b, n):
        return psum[:, b, :].bitcast(F16)[:, 0:n * (P + 1)].rearrange("p (n q) -> p n q", n=n)[:, :, 0:P]

    def pair(i, p=128):
        return psum[:p, 2 * i:2 * i + 2, 0:CH]

    def accumulator(j):
        return bank(j // 2, P, D, (j % 2) * D)

    def inner(m):
        return psum[:, 3 + 2 * (m % 2):5 + 2 * (m % 2), 0:CH]

    out_row = tdiv[0:1, :]

    def res_bank(j):
        return bank(j if j < 4 else 7, P, D)

    ROUNDS = ((0, 1), (2, 3), (4,))

    def halves(ap):
        return ap.rearrange("p (h c) -> p h c", h=2)

    block = ctx.enter_context(nc.Block())

    @block.sync
    def _(sp):
        def load(dst, src, name):
            sp.dma_start(dst, src).then_inc(sem(name), 16)

        src_w = bass.AP(a["src_pad"].tensor, PADE - HALO, [[EC, P], [1, EW]])
        dst_w = bass.AP(a["dst_pad"].tensor, PADE - HALO, [[EC, P], [1, EW]])
        load(esrc_i, src_w, "edges_loaded")
        load(edst_i, dst_w, "edges_loaded")
        load(x_rows, a["x"].rearrange("(p t) d -> p t d", t=T), "x_loaded")
        load(wq, a["wq"].rearrange("(k p) n -> p k n", p=128), "mixw_loaded")
        load(wres, a["wres"].rearrange("(k p) n -> p k n", p=128), "mixw_loaded")
        load(bresr, bass.AP(a["bres"].tensor, 0, [[0, P], [1, D]]), "mixw_loaded")
        load(bng, a["bng"], "mixw_loaded")
        load(bnb, a["bnb"], "mixw_loaded")
        load(wdw, a["wdw"], "mixw_loaded")
        sp.wait_ge(sem("blocks_cleared"), 1)
        for b in range(4):
            load(wp[32 * b:32 * b + 32, :, 32 * b:32 * b + 32], a["wpw"][b], "mixw_loaded")
        for dst, name in ((g1c, "g1"), (be1c, "be1"), (fb1c, "fb1"), (g2c, "g2"), (be2c, "be2")):
            load(dst, a[name], "cols_loaded")
        sp.wait_ge(sem("zi_ready"), 2)
        for t in range(T):
            sp.dma_start(counts_dram[t], free(zi, (T - 1 - t) * P, [[1, N]])).then_inc(sem("counts_cleared"), 16)
        load(w1, a["w1"].rearrange("(k p) n -> p k n", p=128), "layerw_loaded")
        load(w3, a["w3"].rearrange("(k p) n -> p k n", p=128), "layerw_loaded")
        sp.wait_ge(milestone("flag_ready"), AFTER["flag_ready"])
        far = sp.value_load(flagi[0:1, 0:1], min_val=0, max_val=1)
        with sp.If(far > 0):
            with sp.Fori(1, NWIN) as w:
                for side in (0, 1):
                    sp.wait_ge(sem("window_used"), w * 2 + (side - 1))
                    for dst, name in ((esrc_i, "src_pad"), (edst_i, "dst_pad")):
                        o = PADE - HALO + (w * HALO if side == 0 else w * (-HALO))
                        sp.dma_start(dst, bass.AP(a[name].tensor, o, [[EC, P], [1, EW]])).then_inc(
                            sem("window_loaded"), 16)
        sp.wait_ge(sem("counts_cleared"), 16 * T)
        load(w2, a["w2"].rearrange("(k p) n -> p k n", p=128), "layerw_loaded")
        sp.wait_ge(sem("scattered"), 16 * EC)
        sp.wait_ge(sem("rows1_ready"), T)
        sp.wait_ge(sem("res_done"), T - G)
        xd = a["x"].rearrange("(p t) d -> p t d", t=T)

        def fetch(t, s):
            sp.dma_start(ring[s], counts_dram[t].rearrange("p (t q) -> p t q", t=T)).then_inc(
                sem(f"ring_loaded{s}"), 16)

        def fetch_x(t, s):
            sp.dma_start(xslot[s], xd[:, bass.ds(t, 1), :].rearrange("p o d -> p (o d)")).then_inc(
                sem(f"xslot{s}_loaded"), 16)

        for layer in range(3):
            base = layer * T
            for t in range(HEAD):
                if base + t >= RING:
                    sp.wait_ge(sem("agg_done"), base + t - RING + 1)
                fetch(t, (base + t) % RING)
                if layer == 0 and t == RING - 1:
                    sp.wait_ge(sem("ft_done"), T)
                    sp.wait_ge(sem("res_done"), T)
                    for s in range(RING):
                        fetch_x(s, s)
                    for dst, name, n in ((b1r, "b1", D1), (b2r, "b2", D2), (b3r, "b3", D3), (g3r, "g3", D3),
                                         (be3r, "be3", D3), (fb2r, "fb2", D), (wrr, "wr", D)):
                        load(dst, bass.AP(a[name].tensor, 0, [[0, P], [1, n]]), "rowb_loaded")
                    load(brc[:, 0:1], bass.AP(a["br"].tensor, 0, [[0, P], [1, 1]]), "rowb_loaded")
                if layer == 0 and t == RING:
                    sp.wait_ge(sem("fx_done"), 1)
                    fetch_x(t, 0)
            if layer == 1:
                sp.wait_ge(sem("h2_done"), T)
                load(f1, a["f1"].rearrange("(k p) n -> p k n", p=128), "ffnw_loaded")
                load(f2, a["f2"].rearrange("(k p) n -> p k n", p=128), "ffnw_loaded")
            with sp.Fori(0, LOOPS) as i:
                for k in range(HEAD, HEAD + RING):
                    sp.wait_ge(sem("agg_done"), i * RING + (base + k - RING + 1))
                    fetch(i * RING + k, (base + k) % RING)
                    if layer == 0:
                        sp.wait_ge(sem("fx_done"), i * RING + (k - RING + 1))
                        fetch_x(i * RING + k, k % RING)
        sp.wait_ge(milestone("router_done"), AFTER["router_done"])
        sp.wait_ge(sem("agg_done"), 3 * T)
        sp.dma_start(w_dram.rearrange("(p t) -> p t", t=T), wv).then_inc(sem("w_stored"), 16)
        sp.wait_ge(sem("w_stored"), 16)
        sp.dma_start(wall, bass.AP(w_dram.tensor, 0, [[0, P], [1, N]])).then_inc(sem("wall_loaded"), 16)
        od = out.rearrange("(p t) d -> p t d", t=T)
        with sp.Fori(0, NC) as i:
            sp.wait_ge(sem("final_done"), i * G + G)
            sp.dma_start(od[:, bass.ds(i * G, G), :], accv[:, bass.ds(i * G, G), :]).then_inc(sem("stored"), 16)
        sp.wait_ge(sem("stored"), 16 * NC)

    @block.gpsimd
    def _(pool):
        done = Steps(pool, sem("pool_steps"))
        pool.memset(wb[:P, 0:3072], 0.0).then_inc(sem("zi_ready"), 1)
        pool.memset(eps, EPS).then_inc(sem("eps_ready"), 1)
        done.did(pool.memset(pool_pause, 0.0))
        pool.memset(eps_x, EPS / XHAT ** 2).then_inc(sem("eps_ready"), 1)
        pool.memset(wp[:, :, :], 0.0).then_inc(sem("blocks_cleared"), 1)
        done.did(pool.memset(ident[:, :], 0.0))
        done.did(pool.memset(ones[:, :], 1.0))
        done.did(pool.memset(kones[:, :], 0.0))
        done.settle()
        pool.affine_select(out=ident[:, :], in_=ident[:, :], compare_op=ALU.not_equal, fill=1.0, base=0,
                           pattern=[[-1, 128]], channel_multiplier=1).then_inc(sem("ident_ready"), 1)
        pool.wait_ge(sem("ident_ready"), 1)
        for b in range(4):
            done.did(pool.memset(kones[32 * b:32 * b + 32, 32 * b:32 * b + 32], 1.0))
            done.settle()
        pool.iota(iop[:, 0:P], pattern=[[1, P]], base=0, channel_multiplier=0,
                  allow_small_or_imprecise_dtypes=True).then_inc(sem("ident_ready"), 1)
        pool.wait_ge(sem("ident_ready"), 2)
        pool.memset(free(zT, P * G, [[NC * CW, 2], [CW, NC], [1, 1]]), 0.0).then_inc(sem("ident_ready"), 1)
        pool.wait_ge(sem("ident_ready"), 3)
        pool.wait_ge(sem("zi_ready"), 1)
        pool.tensor_copy(zi[:, (T - 1) * P:T * P], ident[:P, 0:P]).then_inc(sem("zi_ready"), 1)
        pool.wait_ge(milestone("keys_ready"), AFTER["keys_ready"])
        for b in range(PB):
            both_oh, ohp, oht = onehot[b % 2]
            if b >= 2:
                pool.wait_ge(sem("degree_used"), b - 1)
            pool.tensor_tensor(ohp, free(edp, HALO + b * EB, [[1, EB], [0, P]]), free(iop, 0, [[0, EB], [1, P]]),
                               ALU.subtract).then_inc(sem("offset_done"), 1)
            pool.tensor_tensor(oht, free(edt, HALO + b * EB, [[1, EB], [0, T]]), free(iop, 0, [[0, EB], [1, T]]),
                               ALU.subtract).then_inc(sem("offset_done"), 1)
        pool.wait_ge(sem("counts_cleared"), 16 * T)
        pool.wait_ge(milestone("edges_ready"), AFTER["edges_ready"])
        cells = counts_dram.rearrange("t p (n o) -> (t p n) o", o=1)
        with pool.Fori(0, EC // SB) as i:
            at_j = pool.snap(i * SB)
            done.enter(i, 2)
            pool.tensor_copy(sidx, eidx[:, bass.ds(at_j, SB)]).then_inc(sem("staged"), 1)
            pool.tensor_copy(svalue[:, 0:SB], evalue[:, bass.ds(at_j, SB)]).then_inc(sem("staged"), 1)
            pool.wait_ge(sem("staged"), i * 2 + 2)
            done.settle()
            done.did(pool.tensor_tensor(pool_pause, pool_pause, pool_pause, ALU.add))
            for j in range(SB):
                pool.indirect_dma_start(cells, bass.IndirectOffsetOnAxis(ap=sidx[:, j:j + 1], axis=0),
                                        svalue[:, j:j + 1], None, bounds_check=N * N - 1,
                                        oob_is_err=False).then_inc(sem("scattered"), 16)
            pool.wait_ge(sem("scattered"), i * (16 * SB) + 16 * SB)
            done.settle()
            done.did(pool.tensor_tensor(pool_pause, pool_pause, pool_pause, ALU.add))
            done.leave(EC // SB)
        pool.wait_ge(sem("k_done"), 4 * NC)
        pool.memset(tri[:, :], 0.0).then_inc(sem("tri"), 1)
        pool.wait_ge(sem("tri"), 1)
        pool.affine_select(out=tri[:, :], in_=tri[:, :], compare_op=ALU.is_ge, fill=1.0, base=0,
                           pattern=[[-1, 128]], channel_multiplier=1).then_inc(sem("tri"), 1)
        pool.wait_ge(sem("rows1_ready"), T)
        pool.wait_ge(sem("scattered"), 16 * EC)
        pool.memset(free(nT16[1], P * G, [[CW, 4], [1, 1]]), 0.0).then_inc(sem("npad_done"), 1)
        pool.wait_ge(sem("lo2_done"), T)
        pool.wait_ge(sem("agg_done"), 2 * T)
        pool.memset(free(nT16[0], P * G, [[CW, 4], [1, 1]]), 0.0).then_inc(sem("npad_done"), 1)
        pool.wait_ge(sem("rowb_loaded"), 16 * 8)
        pool.wait_ge(sem("fx_done"), T)
        for t in range(T):
            pool.tensor_tensor(accv[:, t, :], accv[:, t, :], be3r, ALU.add).then_inc(sem("be3_added"), 1)
        pool.wait_ge(milestone("fscale_done"), AFTER["fscale_done"])
        pieces = [(wa[:, c * 512:(c + 1) * 512], f1s[:, c], 0) for c in range(4)]
        pieces += [(wb[:, c * 512:(c + 1) * 512], f2s[:, c], 1) for c in range(4)]
        for c, (raw, kept, which) in enumerate(pieces):
            temp = ftemp[c % 2]
            done.did(pool.tensor_scalar(temp, raw, f_scale[:, which:which + 1], None, ALU.mult))
            done.settle()
            done.did(pool.tensor_copy(kept[:, 0, :], temp))
            done.settle()
            pool.tensor_tensor(kept[:, 1, :], temp, kept[:, 0, :], ALU.subtract).then_inc(sem("fpiece_done"), 1)
            pool.wait_ge(sem("fpiece_done"), c + 1)

        def stage_rows(c):
            pool.wait_ge(sem("xn2_done"), c * G + G)
            if c >= 2:
                pool.wait_ge(sem("tr_done"), 3 * c - 3)
            done.did(pool.tensor_scalar(stage, xn2[:, c * G:c * G + G, :], NORMED, None, ALU.mult))
            done.settle()
            done.did(pool.tensor_copy(stage16[c % 2][:, 0], stage))
            done.settle()
            pool.tensor_tensor(stage16[c % 2][:, 1], stage, stage16[c % 2][:, 0], ALU.subtract).then_inc(
                sem("stage_done"), 1)
            pool.wait_ge(sem("stage_done"), c + 1)
            pool.wait_ge(sem("sum_done"), c * G + G)
            chunk = accv[:, c * G:c * G + G, :]
            pool.tensor_tensor(chunk, chunk, xn2[:, c * G:c * G + G, :], ALU.add).then_inc(sem("xn2_added"), 1)

        stage_rows(0)
        stage_rows(1)
        for c in range(2, NC):
            stage_rows(c)

    def edge_keys(dve, done, key, esrc, edp, edt):
        done.did(dve.tensor_copy(esrc, esrc_i))
        done.did(dve.tensor_copy(edt, edst_i))
        done.settle()
        done.did(dve.tensor_scalar(edp, edt, 1.0 / T, -0.48, ALU.mult, ALU.add))
        done.settle()
        done.did(dve.tensor_scalar(edp, edp, ROUND, ROUND, ALU.add, ALU.subtract))
        done.settle()
        done.did(dve.scalar_tensor_tensor(out=edt, in0=edp, scalar=-float(T), in1=edt, op0=ALU.mult, op1=ALU.add))
        done.settle()
        done.did(dve.scalar_tensor_tensor(out=key, in0=esrc, scalar=float(P), in1=edp,
                                          op0=ALU.mult, op1=ALU.add))
        done.settle()
        done.did(dve.scalar_tensor_tensor(out=key, in0=edt, scalar=float(P * N), in1=key,
                                          op0=ALU.mult, op1=ALU.add))
        done.settle()

    KEY_STEPS = 7

    def count_equal(dve, done, other, shift, into, lo, tmp):
        mine = free(ekey, HALO + lo, [[1, EB], [0, HALO]])
        theirs = free(other, HALO + lo + shift, [[1, EB], [1, HALO]])
        pairs = free(equal, 0, [[HALO, EB], [1, HALO]])
        done.did(dve.tensor_tensor(pairs, mine, theirs, ALU.is_equal))
        done.settle()
        done.did(dve.tensor_reduce(tmp, pairs, AX, ALU.add))
        done.settle()

    @block.vector
    def _(dve):
        done = Steps(dve, sem("dve_steps"))

        def layernorm_stats(src, width, n, t):
            parts = max(1, width // 512)
            for h in range(parts):
                done.did(dve.bn_stats(st2[:, h, :], src[:, h * 512:(h + 1) * 512] if parts > 1 else src))
            done.settle()
            done.did(dve.memset(pause, 0.0))
            dve.bn_aggr(mv2, st2[:, 0:parts, :]).then_inc(sem(f"var{n}_done"), 1)
            dve.wait_ge(sem(f"root{n}_done"), t + 1)
            done.did(dve.reciprocal(rs2, root2))
            done.settle()

        dve.wait_ge(sem("edges_loaded"), 32)
        edge_keys(dve, done, ekey, esrc, edp, edt)
        done.settle()
        dve.memset(pause, 0.0).then_inc(milestone("keys_ready"), 1)
        dstf = wkey
        done.did(dve.tensor_copy(dstf, edst_i))
        done.settle()
        mid, nxt, far_ = (free(dstf, HALO + s, [[1, EC]]) for s in (0, 1, HALO))
        done.did(dve.tensor_tensor(fwd, mid, nxt, ALU.is_gt))
        done.did(dve.tensor_tensor(bwd, mid, far_, ALU.is_equal))
        done.settle()
        done.did(dve.tensor_tensor(fwd, fwd, bwd, ALU.max))
        done.settle()
        dve.tensor_reduce(flagf[:P], fwd, AX, ALU.max).then_inc(milestone("flag_part"), 1)
        dve.wait_ge(sem("flag_sum"), 1)
        done.did(dve.tensor_scalar(flagf[0:1], bank(7, 1, 1), 1.0, None, ALU.min))
        done.settle()
        dve.tensor_copy(flagi[0:1, 0:1], flagf[0:1]).then_inc(milestone("flag_ready"), 1)
        done.settle()
        for lo, hi in ((0, EC // 2), (EC // 2, EC)):
            n = hi - lo + HALO
            done.did(dve.tensor_tensor(free(equal, 0, [[HALO, n], [1, HALO]]), free(ekey, lo, [[1, n], [0, HALO]]),
                                       free(ekey, lo + 1, [[1, n], [1, HALO]]), ALU.is_equal))
            done.settle()
            done.did(dve.tensor_reduce(fwd[:, lo:hi], free(equal, HALO * HALO, [[HALO, hi - lo], [1, HALO]]), AX,
                                       ALU.add))
            done.did(dve.tensor_reduce(bwd[:, lo:hi],
                                       free(equal, (HALO - 1) * HALO, [[HALO, hi - lo], [1 - HALO, HALO]]), AX,
                                       ALU.add))
            done.settle()
        self_ = evalue[:, 0:EC]
        done.did(dve.tensor_tensor(self_, free(dstf, HALO, [[1, EC]]), free(esrc, HALO, [[1, EC]]), ALU.is_equal))
        done.settle()
        dve.wait_ge(milestone("flag_ready"), AFTER["flag_ready"])
        far = dve.value_load(flagi[0:1, 0:1], min_val=0, max_val=1)
        with dve.If(far > 0):
            dve.memset(sqjunk[:, 0:1], 0.0).then_inc(sem("window_used"), 1)
            with dve.Fori(1, NWIN) as w:
                for side in (0, 1):
                    fs = sem("far_steps")
                    per = KEY_STEPS + 3 * (EC // EB)
                    inner = Steps(dve, fs)
                    inner.base = w * (2 * per) + (side - 2) * per
                    dve.wait_ge(sem("window_loaded"), w * 64 + (32 * side - 32))
                    edge_keys(dve, inner, wkey, wkey, wdp, wdt)
                    into = fwd if side == 0 else bwd
                    for b in range(0, EC, EB):
                        part = sqjunk[:, 0:EB]
                        count_equal(dve, inner, wkey, 1 if side == 0 else -HALO, None, b, part)
                        inner.did(dve.tensor_tensor(free(into, b, [[1, EB]]), free(into, b, [[1, EB]]), part,
                                                    ALU.add))
                        inner.settle()
                    assert inner.k == per
                    dve.memset(sqjunk[:, 0:1], 0.0).then_inc(sem("window_used"), 1)
        done.did(dve.scalar_tensor_tensor(out=bwd, in0=bwd, scalar=2.0e7, in1=free(ekey, HALO, [[1, EC]]),
                                          op0=ALU.mult, op1=ALU.add))
        done.did(dve.tensor_scalar(fwd, fwd, 1.0, None, ALU.add))
        done.settle()
        done.did(dve.tensor_scalar(bwd, bwd, 2.0e7, None, ALU.min))
        done.did(dve.tensor_tensor(evalue[:, 0:EC], fwd, self_, ALU.add))
        done.settle()
        dve.tensor_copy(eidx, bwd).then_inc(milestone("edges_ready"), 1)
        dve.wait_ge(sem("x_loaded"), 16)
        for t in range(T):
            done.did(dve.bn_stats(stats[:, t, :], x_rows[:, t, :]))
        done.settle()
        for t in range(T):
            done.did(dve.bn_aggr(mv[:, t, :], stats[:, t:t + 1, :]))
        done.settle()
        var = mv[:, :, 1:2].rearrange("p t o -> p (t o)")
        dve.tensor_scalar(ca, var, EPS, None, ALU.add).then_inc(milestone("xvar_done"), 1)
        dve.wait_ge(milestone("xroot_done"), AFTER["xroot_done"])
        done.did(dve.reciprocal(rstd, rstd))
        dve.wait_ge(milestone("xvar_done"), AFTER["xvar_done"])
        done.did(dve.reciprocal(cb, ca))
        done.settle()
        dve.tensor_tensor(cb, var, cb, ALU.mult).then_inc(milestone("ratio2_done"), 1)
        for t in range(T):
            done.did(dve.tensor_scalar(x_rows[:, t, :], x_rows[:, t, :], mv[:, t, 0:1], rstd[:, t:t + 1],
                                       ALU.subtract, ALU.mult))
        dve.wait_ge(milestone("norm_done"), AFTER["norm_done"])
        done.did(dve.tensor_scalar(ca, cb, BALL, None, ALU.min))
        done.did(dve.tensor_scalar(cb, cb, 1e-15, None, ALU.max))
        done.settle()
        done.did(dve.tensor_scalar(cc, ca, 1.0, None, ALU.add))
        done.did(dve.tensor_scalar(cd, ca, -1.0, 1.0, ALU.mult, ALU.add))
        done.settle()
        done.did(dve.reciprocal(cd, cd))
        done.settle()
        dve.tensor_tensor(cc, cc, cd, ALU.mult).then_inc(milestone("ratio_done"), 1)
        done.did(dve.tensor_tensor(dx, ca, ca, ALU.mult))
        done.settle()
        done.did(dve.tensor_scalar(rstd, dx, 1.0 / 9.0, 1.0 / 7.0, ALU.mult, ALU.add))
        done.settle()
        for c in (1.0 / 5.0, 1.0 / 3.0, 1.0):
            done.did(dve.tensor_tensor(rstd, rstd, dx, ALU.mult))
            done.settle()
            done.did(dve.tensor_scalar(rstd, rstd, c, None, ALU.add))
            done.settle()
        dve.wait_ge(milestone("log_done"), AFTER["log_done"])
        done.did(dve.tensor_scalar(cd, cd, 0.5, None, ALU.mult))
        done.did(dve.reciprocal(cb, cb))
        done.settle()
        done.did(dve.tensor_tensor(cd, cd, cb, ALU.mult))
        done.did(dve.tensor_scalar(cc, ca, 0.1, None, ALU.is_lt))
        done.settle()
        done.did(dve.tensor_tensor(rstd, rstd, cd, ALU.subtract))
        done.settle()
        done.did(dve.tensor_tensor(rstd, rstd, cc, ALU.mult))
        done.settle()
        done.did(dve.tensor_tensor(cd, rstd, cd, ALU.add))
        done.settle()
        for t in range(T):
            dve.tensor_scalar(zv[:, t, :], x_rows[:, t, :], cd[:, t:t + 1], None, ALU.mult).then_inc(
                sem("z_done"), 1)
        for b in range(PB, EC // EB):
            both_oh, ohp, oht = onehot[b % 2]
            dve.wait_ge(sem("degree_used"), b - 1)
            done.did(dve.tensor_tensor(ohp, free(edp, HALO + b * EB, [[1, EB], [0, P]]),
                                       free(iop, 0, [[0, EB], [1, P]]), ALU.is_equal))
            dve.tensor_tensor(oht, free(edt, HALO + b * EB, [[1, EB], [0, T]]),
                              free(iop, 0, [[0, EB], [1, T]]), ALU.is_equal).then_inc(sem("onehot_done"), 1)
        dve.wait_ge(sem("degree_used"), EC // EB)
        dve.tensor_scalar(dinv, bank(7, P, T), 1.0, None, ALU.add).then_inc(milestone("dinv_read"), 1)
        dve.wait_ge(milestone("droot_done"), AFTER["droot_done"])
        done.did(dve.reciprocal(dinv, dinv))
        done.settle()
        dve.wait_ge(milestone("zrow_done"), AFTER["zrow_done"])
        dve.tensor_scalar(nzrow, zrow, -1.0 / N, None, ALU.mult).then_inc(milestone("nzrow_done"), 1)
        dve.wait_ge(sem("gram_done"), 1)
        done.did(dve.tensor_copy(zcol, bank(2, 128, 2)))
        dve.tensor_copy(gram, psum[:, 0:2, 0:D]).then_inc(milestone("gram_copied"), 1)
        done.settle()
        dve.wait_ge(sem("mixw_loaded"), 16 * 10)
        dve.wait_ge(sem("gw_done"), 1)
        for k in range(2):
            done.did(dve.tensor_tensor(gw[:, k, 0:512], bank(4 + 2 * k, 128, 512), wq[:, k, 0:512], ALU.mult))
            last = dve.tensor_tensor(gw[:, k, 512:768], bank(5 + 2 * k, 128, 256), wq[:, k, 512:768], ALU.mult)
            last.then_inc(sem("wgw_done"), 1)
        for m in range(NT):
            last = dve.tensor_scalar(wp[:, m, :], wp[:, m, :], wdw[:, m:m + 1], None, ALU.mult)
        last.then_inc(milestone("wp_done"), 1)
        dve.wait_ge(sem("bnsum_done"), 1)
        dve.tensor_scalar(tmp6, bank(3, 128, NT), 1.0 / N, None, ALU.mult).then_inc(milestone("bnvar_done"), 1)
        done.did(dve.tensor_scalar(bnt, bank(3, 128, NT, 16), 1.0 / N, None, ALU.mult))
        done.settle()
        dve.wait_ge(milestone("bnroot_done"), AFTER["bnroot_done"])
        done.did(dve.reciprocal(tmp6, tmp6))
        done.settle()
        done.did(dve.tensor_tensor(bns, tmp6, bng, ALU.mult))
        done.settle()
        done.did(dve.tensor_tensor(bnt, bnt, bns, ALU.mult))
        done.settle()
        dve.tensor_tensor(bnt, bnb, bnt, ALU.subtract).then_inc(milestone("bn_done"), 1)
        done.did(dve.tensor_scalar(dx, dinv, X_SCALE, None, ALU.mult))
        done.did(dve.tensor_scalar(ca, dinv, 1.0 / X_SCALE, None, ALU.mult))
        done.settle()
        dve.wait_ge(milestone("bounds_read"), AFTER["bounds_read"])
        for L, width in ((0, D1), (1, D2)):
            o = 3 * L
            done.did(dve.tensor_tensor(bound[:, o:o + 1], bound[:, o:o + 1], bound[:, o + 2:o + 3], ALU.mult))
            done.settle()
            done.did(dve.scalar_tensor_tensor(out=bound[:, o:o + 1], in0=bound[:, o + 1:o + 2],
                                              scalar=float(width) ** 0.5, in1=bound[:, o:o + 1],
                                              op0=ALU.mult, op1=ALU.add))
            done.settle()
            done.did(dve.tensor_scalar(bound[:, o:o + 1], bound[:, o:o + 1], 1e-20, 1.0 / F16_TOP,
                                       ALU.max, ALU.mult))
            done.settle()
            done.did(dve.reciprocal(bound[:, 6 + L:7 + L], bound[:, o:o + 1]))
            done.settle()
            di, do = (d2in, d2out) if L == 0 else (d3in, d3out)
            done.did(dve.tensor_scalar(di, dinv, bound[:P, 6 + L:7 + L], None, ALU.mult))
            done.did(dve.tensor_scalar(do, dinv, bound[:P, o:o + 1], None, ALU.mult))
            done.settle()
        for back, scale, src in ((w1_back, w1_scale, w1_back), (gw2_back, gw2_scale, bound[:, 1:2])):
            done.did(dve.tensor_scalar(back, src, 1e-20, 1.0 / F16_TOP, ALU.max, ALU.mult))
            done.settle()
            done.did(dve.reciprocal(scale, back))
        done.did(dve.tensor_tensor(y_scale, dinv, dinv, ALU.mult))
        done.did(dve.reciprocal(y_back, dinv))
        done.settle()
        done.did(dve.tensor_scalar(y_back, y_back, w1_back[:P], 1.0 / X_SCALE, ALU.mult, ALU.mult))
        done.did(dve.tensor_scalar(h2_scale, d2in, gw2_back[:P], 1.0 / XHAT, ALU.mult, ALU.mult))
        dve.wait_ge(sem("be2w_done"), 1)
        dve.tensor_scalar(be2w, bank(5, P, D2), gw2_scale[:P], XHAT, ALU.mult, ALU.mult).then_inc(
            milestone("be2w_read"), 1)
        dve.wait_ge(milestone("be2w_read"), AFTER["be2w_read"])
        done.settle()
        for c, (raw, kept) in enumerate(wpieces):
            if c >= 2:
                dve.wait_ge(sem("wpiece_done"), c - 1)
            if c < 4:
                dve.tensor_scalar(wtemp[c % 2], raw, w1_scale, None, ALU.mult).then_inc(sem("wpiece_scaled"), 1)
            else:
                dve.tensor_scalar(wtemp[c % 2], raw, gw2_scale, g1c[:, c - 4:c - 3], ALU.mult,
                                  ALU.mult).then_inc(sem("wpiece_scaled"), 1)
            if c >= 1:
                dve.wait_ge(sem("wpiece_high"), c)
                dve.tensor_tensor(wpieces[c - 1][1][:, 1, :], wtemp[(c - 1) % 2], wpieces[c - 1][1][:, 0, :],
                                  ALU.subtract).then_inc(sem("wpiece_done"), 1)
        dve.wait_ge(sem("wpiece_high"), len(wpieces))
        dve.tensor_tensor(wpieces[-1][1][:, 1, :], wtemp[1], wpieces[-1][1][:, 0, :], ALU.subtract).then_inc(
            sem("wpiece_done"), 1)
        dve.wait_ge(sem("wpiece_done"), len(wpieces))
        for c in range(NC):
            hT = hTs[c % 2]
            for m in range(NT):
                dve.wait_ge(sem("s_done"), c * NT + (m + 1))
                if m == 0:
                    dve.wait_ge(sem("res_done"), c * G)
                if m < 4:
                    dve.tensor_scalar(halves(sT[:, m, :]), pair(m % 2), 0.0, None, ALU.max).then_inc(
                        sem("s_evac"), 1)
                else:
                    dve.tensor_copy(halves(sT[:, m, :]), pair(m % 2)).then_inc(sem("s_evac"), 1)
            dve.wait_ge(sem("nc_done"), c * 12 + 12)
            dve.tensor_scalar(halves(umax), pair(2), 1.0 / RMAX ** 2, 1.0, ALU.mult, ALU.max).then_inc(
                sem("u_done"), 1)
            dve.wait_ge(sem("veps_done"), c + 1)
            for n in range(4):
                src, half = (hT, n) if n < 2 else (sT, n - 2)
                q, v = src[:, half, :], src[:, 4 + half, :]
                dve.wait_ge(sem("k_done"), c * 4 + (n + 1))
                dve.tensor_tensor(halves(q), pair(3), halves(q), ALU.mult).then_inc(sem("qk_done"), 1)
                done.did(dve.tensor_tensor(tdiv, v, veps, ALU.add))
                done.settle()
                done.did(dve.reciprocal(tdiv, tdiv))
                done.settle()
                done.did(dve.tensor_tensor(tdiv, tdiv, v, ALU.mult))
                done.settle()
                dve.wait_ge(sem("qk_done"), c * 4 + (n + 1))
                dve.tensor_tensor(q, q, tdiv, ALU.mult).then_inc(sem("o_done"), 1)
                dve.wait_ge(sem("o_done"), c * 4 + (n + 1))
            dve.wait_ge(sem("rows1_ready"), c * G)
            for j in range(G):
                t = c * G + j
                done.did(dve.tensor_scalar(xbuf[:, j, :], x_rows[:, t, :], dx[:, t:t + 1], None, ALU.mult))
            done.settle()
            for j in range(G):
                done.did(dve.tensor_copy(x2[:, c * G + j, 0, :], xbuf[:, j, :]))
            done.settle()
            for j in range(G):
                t = c * G + j
                dve.tensor_tensor(x2[:, t, 1, :], xbuf[:, j, :], x2[:, t, 0, :], ALU.subtract).then_inc(
                    sem("rows1_ready"), 1)
            dve.wait_ge(sem("out_rooted"), c + 1)
            dve.tensor_tensor(out_row, out_row, umax[0:1, :], ALU.max).then_inc(sem("out_row_done"), 1)
            dve.wait_ge(sem("out_turned"), c + 1)
            done.did(dve.reciprocal(ocol, bank(6, P, G)))
            done.settle()
            for j in range(G):
                t = c * G + j
                dve.wait_ge(sem("res_done"), t + 1)
                dve.scalar_tensor_tensor(out=accv[:, t, :], in0=res_bank(j), scalar=ocol[:, j:j + 1],
                                         in1=bresr, op0=ALU.mult, op1=ALU.add).then_inc(sem("ft_done"), 1)
        dve.wait_ge(milestone("n4root_done"), AFTER["n4root_done"])
        dve.tensor_scalar(n4, n4, 1e-15, None, ALU.max).then_inc(milestone("n4_ready"), 1)
        dve.wait_ge(milestone("tanh_done"), AFTER["tanh_done"])
        done.did(dve.tensor_scalar(f4, f4, BALL, None, ALU.min))
        done.did(dve.reciprocal(n4, n4))
        done.settle()
        dve.tensor_tensor(f4, f4, n4, ALU.mult).then_inc(milestone("f4_ready"), 1)
        dve.wait_ge(sem("rowb_loaded"), 16 * 8)
        dve.wait_ge(sem("scattered"), 16 * EC)

        def rows_out(t, width, tile, scale, layer):
            dve.wait_ge(sem(f"h{layer}_done"), t + 1)
            dve.wait_ge(sem(f"lo{layer}_done"), t)
            dve.tensor_scalar(hbuf[:, 0:width], bank(7, P, width), scale[:, bass.ds(t, 1)], None,
                              ALU.mult).then_inc(sem(f"hbuf{layer}_done"), 1)
            dve.wait_ge(sem(f"hi{layer}_done"), t + 1)
            dve.tensor_tensor(tile[:, t, 1, :], hbuf[:, 0:width], tile[:, t, 0, :], ALU.subtract).then_inc(
                sem(f"lo{layer}_done"), 1)

        def sum_rows(t, b):
            dve.wait_ge(sem("yhi_done"), t + 1)
            dve.scalar_tensor_tensor(out=ysum, in0=bank(b, P, D, D), scalar=y_scale[:, bass.ds(t, 1)], in1=yhi,
                                     op0=ALU.mult, op1=ALU.add).then_inc(sem("y_done"), 1)
            dve.wait_ge(sem("y16_done"), t + 1)
            dve.tensor_tensor(y16[:, 1, :], ysum, y16[:, 0, :], ALU.subtract).then_inc(sem("ylo_done"), 1)

        def add_mix(t, b4, loaded):
            dve.wait_ge(sem(f"xslot{b4}_loaded"), loaded)
            dve.scalar_tensor_tensor(out=accv[:, t, :], in0=accv[:, t, :], scalar=f4[:, bass.ds(t, 1)],
                                     in1=xslot[b4], op0=ALU.mult, op1=ALU.add).then_inc(sem("fx_done"), 1)

        def rows2_sum(t):
            dve.wait_ge(sem("h2_done"), t + 1)
            dve.wait_ge(sem("lo2_done"), t)
            dve.tensor_tensor(hbuf, bank(7, P, D2), be2w, ALU.add).then_inc(sem("hbuf2_done"), 1)

        def rows2_low(t):
            dve.wait_ge(sem("hi2_done"), t + 1)
            dve.scalar_tensor_tensor(out=h2in[:, t, 1, :], in0=hbuf, scalar=h2_scale[:, bass.ds(t, 1)],
                                     in1=h2in[:, t, 0, :], op0=ALU.mult, op1=ALU.subtract).then_inc(
                sem("lo2_done"), 1)

        def hidden1(t):
            buf = pre[0]
            dve.wait_ge(sem("p1_done"), t + 1)
            dve.wait_ge(sem("xlo_done"), t)
            dve.scalar_tensor_tensor(out=buf.rearrange("p (h n) -> p h n", h=2), in0=psum[:P, 3:5, :],
                                     scalar=y_back[:, bass.ds(t, 1)],
                                     in1=b1r.rearrange("p (h n) -> p h n", h=2), op0=ALU.mult,
                                     op1=ALU.add).then_inc(sem("pre1_done"), 1)
            dve.wait_ge(sem("relu1_done"), t + 1)
            layernorm_stats(buf, D1, 1, t)
            dve.tensor_scalar(buf, buf, mv2[:, 0:1], rs2, ALU.subtract, ALU.mult).then_inc(sem("xnorm_done"), 1)

        def hidden1_low(t):
            dve.wait_ge(sem("xhi_done"), t + 1)
            dve.tensor_tensor(x16[:, 1, :], pre[0], x16[:, 0, :], ALU.subtract).then_inc(sem("xlo_done"), 1)

        def step1(t, b, b4, loaded, lagging=True):
            sum_rows(t, b)
            add_mix(t, b4, loaded)
            if lagging:
                rows2_sum(t - 2)
            hidden1(t)
            if lagging:
                rows2_low(t - 2)
            hidden1_low(t)

        dve.wait_ge(milestone("f4_ready"), AFTER["f4_ready"])
        for t in range(HEAD):
            step1(t, t % 2, t % RING, 16 + t // RING * 16, t >= 2)
        with dve.Fori(0, LOOPS) as i:
            done.enter(i, 4 * 4)
            for k in range(HEAD, HEAD + RING):
                step1(i * RING + k, k % 2, k % RING, i * 16 + (16 + k // RING * 16))
            done.leave(LOOPS)
        for t in (T - 2, T - 1):
            rows2_sum(t)
            rows2_low(t)

        def normalise(t, buf, width, relu, xhat):
            dve.wait_ge(sem(relu), t + 1)
            layernorm_stats(buf, width, 2, t)
            dve.tensor_scalar(buf, buf, mv2[:, 0:1], rs2, ALU.subtract, ALU.mult).then_inc(sem(xhat), 1)

        def step2(t, b, first=False, last=False):
            if not first:
                rows_out(t - 1, D3, x2, d3in, 3)
            if not last:
                dve.wait_ge(sem("agg_done"), t + (T + 1))
                dve.scalar_tensor_tensor(out=pre[b][:, 0:D2], in0=bank(b, P, D2), scalar=d2out[:, bass.ds(t, 1)],
                                         in1=b2r, op0=ALU.mult, op1=ALU.add).then_inc(sem("pre2_done"), 1)
                normalise(t, pre[b][:, 0:D2], D2, "relu2_done", "xhat2_done")

        for t in range(HEAD):
            step2(t, t % 2, first=t == 0)
        with dve.Fori(0, LOOPS) as i:
            done.enter(i, 3 * 4)
            for k in range(HEAD, HEAD + RING):
                step2(i * RING + k, k % 2)
            done.leave(LOOPS)
        step2(T, T % 2, last=True)

        def row_stats(src, stat, mean_var, n):
            done.did(dve.bn_stats(stat, src))
            done.settle()
            done.did(dve.memset(pause, 0.0))
            dve.bn_aggr(mean_var, stat).then_inc(sem(f"var{n}_done"), 1)

        summed = pre[1][:, 0:D]
        post = pre[1][:, D:2 * D]

        def router(t):
            dve.wait_ge(sem("root4_done"), t + 1)
            done.did(dve.reciprocal(rs4, root4))
            done.settle()
            dve.tensor_scalar(xn2[:, t, :], summed, mv4[:, 0:1], rs4, ALU.subtract, ALU.mult).then_inc(
                sem("xn2_done"), 1)
            dve.wait_ge(sem("xn2_done"), t + 1)
            dve.wait_ge(sem("w_done"), t)
            dve.tensor_tensor(post, xn2[:, t, :], wrr, ALU.mult).then_inc(sem("wprod_done"), 1)

        def step3(t, b, first=False):
            buf = pre[0][:, 0:D]
            dve.wait_ge(sem("agg_done"), t + (2 * T + 1))
            s = d3out[:, bass.ds(t, 1)]
            done.did(dve.scalar_tensor_tensor(out=buf, in0=bank(b, P, D), scalar=s, in1=b3r, op0=ALU.mult,
                                              op1=ALU.add))
            done.settle()
            dve.scalar_tensor_tensor(out=buf, in0=bank(b, P, D, D), scalar=s, in1=buf, op0=ALU.mult,
                                     op1=ALU.add).then_inc(sem("pre3_done"), 1)
            dve.wait_ge(sem("pre3_done"), t + 1)
            done.did(dve.tensor_scalar(buf, buf, 0.0, None, ALU.max))
            done.settle()
            row_stats(buf, st3, mv3, 3)
            if not first:
                router(t - 1)
            dve.wait_ge(sem("root3_done"), t + 1)
            done.did(dve.reciprocal(rs3, root3))
            done.did(dve.scalar_tensor_tensor(out=buf, in0=buf, scalar=mv3[:, 0:1], in1=g3r, op0=ALU.subtract,
                                              op1=ALU.mult))
            done.settle()
            dve.wait_ge(sem("sum_done"), t)
            done.did(dve.scalar_tensor_tensor(out=summed, in0=buf, scalar=rs3, in1=accv[:, t, :], op0=ALU.mult,
                                              op1=ALU.add))
            done.settle()
            row_stats(summed, st4, mv4, 4)

        dve.wait_ge(milestone("fnorm_done"), AFTER["fnorm_done"])
        done.did(dve.tensor_scalar(f_back, fnorm[:, 0:2], 1e-20, 1.0 / F16_TOP, ALU.max, ALU.mult))
        done.did(dve.tensor_scalar(g_back, fnorm[:, 0:1], float(D) ** 0.5, fnorm[:, 2:3], ALU.mult, ALU.add))
        done.settle()
        done.did(dve.tensor_scalar(g_back, g_back, 1e-20, 1.0 / F16_TOP, ALU.max, ALU.mult))
        done.did(dve.tensor_scalar(hid_back, f_back[:, 0:1], 1.0 / NORMED, None, ALU.mult))
        done.settle()
        done.did(dve.reciprocal(g_scale, g_back))
        done.did(dve.tensor_tensor(out_back, g_back, f_back[:, 1:2], ALU.mult))
        dve.reciprocal(f_scale, f_back).then_inc(milestone("fscale_done"), 1)

        STEP3 = 10
        dve.wait_ge(sem("be3_added"), T)
        dve.wait_ge(sem("lo3_done"), T)
        for t in range(HEAD):
            step3(t, t % 2, first=t == 0)
        with dve.Fori(0, LOOPS) as i:
            done.enter(i, STEP3 * 4)
            for k in range(HEAD, HEAD + RING):
                step3(i * RING + k, k % 2)
            done.leave(LOOPS)
        router(T - 1)
        dve.wait_ge(sem("w_done"), T)
        dve.tensor_scalar(wv, wv, brc[:, 0:1], None, ALU.add).then_inc(milestone("router_done"), 1)
        dve.wait_ge(milestone("router_done"), AFTER["router_done"])
        dve.tensor_scalar(pref, wv, -1.0, None, ALU.mult).then_inc(milestone("negw_done"), 1)

        def count_above(t):
            dve.wait_ge(sem("wall_loaded"), 16)
            done.settle()
            done.did(dve.tensor_scalar(gtjunk, wall, wv[:, t:t + 1], 0.0, ALU.is_gt, ALU.add,
                                       accum_out=gt[:, t:t + 1]))

        def take_y(t):
            dve.wait_ge(sem("ypart_done"), t // G * 8 + 8)
            dve.scalar_tensor_tensor(out=x_rows[:, t, :], in0=accumulator(t % G), scalar=out_back[:P],
                                     in1=fb2r, op0=ALU.mult, op1=ALU.add).then_inc(sem("yffn_evac"), 1)

        def take_low(c, m):
            dve.wait_ge(sem("ghigh_done"), c * 8 + m + 1)
            dve.scalar_tensor_tensor(out=gT16[:, m % GR, 1, :], in0=gtemp[m % GR], scalar=g_scale,
                                     in1=gT16[:, m % GR, 0, :], op0=ALU.mult, op1=ALU.subtract).then_inc(
                sem("glow_done"), 1)

        def finish(t):
            dve.wait_ge(sem("yffn_evac"), t + 1)
            dve.scalar_tensor_tensor(out=accv[:, t, :], in0=x_rows[:, t, :], scalar=wsel[:, t:t + 1],
                                     in1=accv[:, t, :], op0=ALU.mult, op1=ALU.add).then_inc(
                sem("final_done"), 1)

        for c in range(COUNTED):
            mine = T - ACT_COUNTS
            todo = list(range(c * mine // COUNTED, (c + 1) * mine // COUNTED))
            for m in range(8):
                take_low(c, m)
                if m == 0 and c >= 1:
                    for j in range(G):
                        take_y((c - 1) * G + j)
                if todo:
                    count_above(todo.pop(0))
            assert not todo
        take_low(NC - 1, 0)
        for j in range(G):
            take_y((NC - 2) * G + j)
        dve.wait_ge(sem("act_counted"), 2 * ACT_COUNTS)
        done.settle()
        done.did(dve.tensor_scalar(cc, gt, float(KSEL), None, ALU.is_lt))
        done.settle()
        done.did(dve.tensor_scalar(cd, cc, -HUGE, HUGE, ALU.mult, ALU.add))
        done.did(dve.tensor_tensor(sg, wv, cc, ALU.mult))
        done.settle()
        done.did(dve.tensor_tensor(sg, sg, cd, ALU.add))
        done.settle()
        dve.tensor_reduce(n4[:, 0:1], sg, AX, ALU.min).then_inc(milestone("least_done"), 1)
        take_low(NC - 1, 1)
        dve.wait_ge(sem("least_turned"), 1)
        dve.tensor_reduce(n4[0:1, 1:2], bank(7, 1, P), AX, ALU.min).then_inc(milestone("last_done"), 1)
        take_low(NC - 1, 2)
        take_low(NC - 1, 3)
        dve.wait_ge(sem("last_spread"), 1)
        done.did(dve.tensor_copy(n4[:, 2:3], bank(7, P, 1)))
        done.did(dve.memset(cd, 0.0))
        done.settle()
        done.did(dve.tensor_scalar(bnd, wv, n4[:, 2:3], None, ALU.is_equal))
        done.settle()
        dve.tensor_tensor_scan(pref, bnd, cd, 0.0, ALU.add, ALU.add).then_inc(
            milestone("prefix_done"), 1)
        take_low(NC - 1, 4)
        take_low(NC - 1, 5)
        dve.wait_ge(sem("before_done"), 1)
        done.did(dve.tensor_tensor(pref, pref, bnd, ALU.subtract))
        dve.tensor_copy(n4[:, 0:1], bank(7, P, 1)).then_inc(milestone("before_read"), 1)
        dve.wait_ge(milestone("before_read"), AFTER["before_read"])
        done.settle()
        done.did(dve.tensor_scalar(pref, pref, n4[:, 0:1], None, ALU.add))
        done.settle()
        done.did(dve.tensor_tensor(pref, pref, gt, ALU.add))
        done.settle()
        done.did(dve.tensor_scalar(pref, pref, float(KSEL), None, ALU.is_lt))
        done.did(dve.tensor_scalar(cd, bnd, -1.0, 1.0, ALU.mult, ALU.add))
        done.settle()
        done.did(dve.tensor_tensor(pref, pref, bnd, ALU.mult))
        done.did(dve.tensor_tensor(cd, cd, cc, ALU.mult))
        done.settle()
        done.did(dve.tensor_tensor(pref, pref, cd, ALU.add))
        done.settle()
        done.did(dve.tensor_tensor(wsel, pref, wv, ALU.mult))
        done.settle()
        dve.wait_ge(sem("xn2_added"), NC)
        for m in (6, 7):
            take_low(NC - 1, m)
            for t in range((m - 6) * 2 * G, (m - 5) * 2 * G):
                finish(t)
        for t in range(T - G, T):
            take_y(t)
            finish(t)

    @block.scalar
    def _(act):
        done = Steps(act, sem("act_steps"))
        for b in range(PB):
            both_oh = onehot[b % 2][0]
            act.wait_ge(sem("offset_done"), 2 * b + 2)
            done.did(act.activation(both_oh, both_oh, ACT.Square))
            done.settle()
            act.activation(both_oh, both_oh, ACT.Relu, scale=-1.0, bias=ones[:P, 0:1]).then_inc(
                sem("onehot_done"), 1)
        act.wait_ge(sem("eps_ready"), 2)
        act.copy(ident16[:, :], ident[:, :]).then_inc(milestone("ident16_ready"), 1)
        act.wait_ge(milestone("xvar_done"), AFTER["xvar_done"])
        act.activation(rstd, ca, ACT.Sqrt).then_inc(milestone("xroot_done"), 1)
        act.wait_ge(milestone("ratio2_done"), AFTER["ratio2_done"])
        act.activation(cb, cb, ACT.Sqrt, scale=float(D)).then_inc(milestone("norm_done"), 1)
        act.wait_ge(milestone("ratio_done"), AFTER["ratio_done"])
        act.activation(cd, cc, ACT.Ln).then_inc(milestone("log_done"), 1)
        act.wait_ge(sem("ident_ready"), 3)
        for c in range(NC):
            for k in range(2):
                act.wait_ge(sem("trz_done"), 3 * c + k + 1)
                act.copy(zT[:, k, c * CW:c * CW + 4 * P], bank(4 + k, 128, 4 * P)).then_inc(sem("zT_done"), 1)
            act.wait_ge(sem("trz_done"), 3 * c + 3)
            act.copy(zT[:, :, c * CW + 4 * P:c * CW + 5 * P],
                     bank(6, 128, 2 * P).rearrange("p (k q) -> p k q", k=2)).then_inc(sem("zT_done"), 1)
        act.wait_ge(sem("zsum_done"), 1)
        act.copy(zrow, bank(3, 1, D)).then_inc(milestone("zrow_done"), 1)
        act.wait_ge(milestone("dinv_read"), AFTER["dinv_read"])
        act.activation(dinv, dinv, ACT.Sqrt).then_inc(milestone("droot_done"), 1)
        act.wait_ge(sem("layerw_loaded"), 48)
        act.wait_ge(sem("cols_loaded"), 80)
        junk = sqw
        for c in range(4):
            done.settle()
            done.did(act.activation(junk, wa[:, c * 512:(c + 1) * 512], ACT.Square, accum_out=ss1[:, c:c + 1]))
        for L, (w, nk, width, g, be) in enumerate(((w2, 8, D2, g1c, be1c), (w3, 4, D3, g2c, be2c))):
            o = 8 * L
            for k in range(nk):
                done.settle()
                done.did(act.activation(junk[:, 0:width], w[:, k, :], ACT.Square,
                                        accum_out=ssw[:, o + k:o + k + 1]))
                done.settle()
                done.did(act.activation(junk[:, 0:width], w[:, k, :], ACT.Square, scale=g[:, k:k + 1],
                                        accum_out=ssg[:, o + k:o + k + 1]))
            done.settle()
            last = act.activation(ssb[:, o:o + nk], be, ACT.Square)
            last.then_inc(sem("squares_done"), 1)

        act.wait_ge(milestone("bnvar_done"), AFTER["bnvar_done"])
        act.activation(tmp6, tmp6, ACT.Sqrt, bias=eps).then_inc(milestone("bnroot_done"), 1)
        act.wait_ge(sem("bounds_done"), 1)
        done.did(act.activation(w1_back, bank(6, 128, 1, 22), ACT.Sqrt))
        act.activation(bound[:, 0:6], bank(6, 128, 6, 16), ACT.Sqrt).then_inc(milestone("bounds_read"), 1)
        act.wait_ge(milestone("bn_done"), AFTER["bn_done"])
        act.preload_act_table(ACT.Sqrt)

        def square(src, c, k):
            if c * 12 + k >= 3:
                act.wait_ge(sem("nc_done"), c * 12 + k - 2)
            dst = sq[:, k % 3, :]
            act.activation(halves(dst) if k >= NT else dst, src, ACT.Square).then_inc(sem("sq_done"), 1)

        def hidden(c, m):
            hT = hTs[c % 2]
            act.wait_ge(sem("qkv_done"), c * NT + (m + 1))
            if m == 0 and c >= 2:
                act.wait_ge(sem("res_done"), (c - 1) * G)
            act.activation(halves(hT[:, m, :]), pair(m % 2), ACT.Relu, scale=bns[:, m:m + 1],
                           bias=bnt[:, m:m + 1]).then_inc(sem("h_done"), 1)
            act.wait_ge(sem("h_done"), c * NT + (m + 1))
            square(hT[:, m, :], c, m)

        for m in range(NT):
            hidden(0, m)
            for c in (2 * m, 2 * m + 1):
                act.wait_ge(sem("wpiece_scaled"), c + 1)
                act.copy(wpieces[c][1][:, 0, :], wtemp[c % 2]).then_inc(sem("wpiece_high"), 1)
        for c in range(NC):
            hT = hTs[c % 2]
            for m in range(NT):
                act.wait_ge(sem("s_evac"), c * NT + (m + 1))
                square(pair(m % 2), c, NT + m)
            act.wait_ge(sem("u_done"), c + 1)
            act.activation(veps, umax, ACT.Sqrt, scale=1e-30).then_inc(sem("veps_done"), 1)
            for n in range(4):
                if n < 3 and c < NC - 1:
                    hidden(c + 1, 2 * n)
                    hidden(c + 1, 2 * n + 1)
                act.wait_ge(sem("o_done"), c * 4 + (n + 1))
                src, half = (hT, n) if n < 2 else (sT, n - 2)
                act.activation(src[:, 2 + half, :], src[:, half, :], ACT.Square).then_inc(sem("osq_done"), 1)
            act.wait_ge(sem("out_summed"), c + 1)
            act.activation(halves(out_row), pair(3, 1), ACT.Sqrt, scale=1.0 / RMAX ** 2).then_inc(
                sem("out_rooted"), 1)
            for j in range(G):
                t = c * G + j
                act.wait_ge(sem("ft_done"), t + 1)
                act.wait_ge(sem("n4_done"), t)
                act.activation(sqjunk, accv[:, t, :], ACT.Square, accum_out=n4[:, t:t + 1]).then_inc(
                    sem("n4_done"), 1)
        act.wait_ge(sem("n4_done"), T)
        act.activation(n4, n4, ACT.Sqrt).then_inc(milestone("n4root_done"), 1)
        act.wait_ge(milestone("n4_ready"), AFTER["n4_ready"])
        act.activation(f4, n4, ACT.Tanh).then_inc(milestone("tanh_done"), 1)
        act.preload_act_table(ACT.Sqrt)

        def turn_in(t, k_tiles, g, be, layer):
            act.wait_ge(sem(f"trx{layer}_done"), t + 1)
            act.wait_ge(sem(f"h{layer}_done"), t)
            for k in range(k_tiles):
                last = act.activation(xT[:, k, :], bank(5 + k // 4, 128, P, (k % 4) * P), ACT.Identity,
                                      scale=g[:, k:k + 1], bias=be[:, k:k + 1])
            last.then_inc(sem(f"xT{layer}_done"), 1)

        def root(t, n):
            act.wait_ge(sem(f"var{n}_done"), t + 1)
            act.activation(root2, mv2[:, 1:2], ACT.Sqrt, bias=eps[:P]).then_inc(sem(f"root{n}_done"), 1)

        def high(t, width, tile, layer):
            act.wait_ge(sem(f"hbuf{layer}_done"), t + 1)
            act.copy(tile[:, t, 0, :], hbuf[:, 0:width]).then_inc(sem(f"hi{layer}_done"), 1)

        def halve_rows(t, b):
            act.wait_ge(sem("agg_done"), t + 1)
            act.wait_ge(sem("ylo_done"), t)
            act.activation(yhi, bank(b, P, D), ACT.Identity, scale=y_scale[:, bass.ds(t, 1)]).then_inc(
                sem("yhi_done"), 1)
            act.wait_ge(sem("y_done"), t + 1)
            act.wait_ge(sem("try_done"), t)
            act.copy(y16[:, 0, :], ysum).then_inc(sem("y16_done"), 1)

        def turned_y(t):
            act.wait_ge(sem("try_done"), t + 1)
            act.wait_ge(sem("p1_done"), t)
            act.copy(yT16.rearrange("p h c q -> p (h c) q"), turned(2, 4)).then_inc(sem("yT_done"), 1)

        def turned_x(t):
            act.wait_ge(sem("trx2_done"), t + 1)
            act.wait_ge(sem("h2_done"), t)
            for h in range(2):
                last = act.copy(xT16[:, h, :, :], turned(5 + h, 8))
            last.then_inc(sem("xT2_done"), 1)

        def rows2_high(t):
            act.wait_ge(sem("hbuf2_done"), t + 1)
            act.activation(h2in[:, t, 0, :], hbuf, ACT.Identity, scale=h2_scale[:, bass.ds(t, 1)]).then_inc(
                sem("hi2_done"), 1)

        def hidden1(t):
            act.wait_ge(sem("pre1_done"), t + 1)
            act.activation(pre[0], pre[0], ACT.Relu).then_inc(sem("relu1_done"), 1)
            act.wait_ge(sem("var1_done"), t + 1)
            act.activation(root2, mv2[:, 1:2], ACT.Sqrt, scale=1.0 / XHAT ** 2, bias=eps_x[:P]).then_inc(
                sem("root1_done"), 1)
            act.wait_ge(sem("xnorm_done"), t + 1)
            act.wait_ge(sem("trx2_done"), t)
            act.copy(x16[:, 0, :], pre[0]).then_inc(sem("xhi_done"), 1)

        def step1(t, b, before=2):
            halve_rows(t, b)
            turned_y(t)
            if before >= 1:
                turned_x(t - 1)
            if before >= 2:
                rows2_high(t - 2)
            hidden1(t)

        act.wait_ge(sem("rows1_ready"), T)
        for t in range(HEAD):
            step1(t, t % 2, min(t, 2))
        with act.Fori(0, LOOPS) as i:
            for k in range(HEAD, HEAD + RING):
                step1(i * RING + k, k % 2)
        turned_x(T - 1)
        rows2_high(T - 2)
        rows2_high(T - 1)

        def ffn_norms():
            act.wait_ge(sem("ffnw_loaded"), 32)
            for n in range(4):
                w = (wa, wb)[n // 2]
                done.did(act.activation(fjunk, w[:, n % 2 * 1024:(n % 2 + 1) * 1024], ACT.Square,
                                        accum_out=ssf[:, n:n + 1]))
                done.settle()
            act.activation(fjunk[:, 0:8], fb1c, ACT.Square, accum_out=ssf[:, 4:5]).then_inc(sem("fsquares_done"), 1)

        def ffn_norms_rooted():
            act.wait_ge(sem("fsum_done"), 1)
            act.activation(fnorm, bank(6, 128, 3), ACT.Sqrt).then_inc(milestone("fnorm_done"), 1)

        def step2(t, b, first=False, last=False):
            if not first:
                turn_in(t - 1, 4, g2c, be2c, 3)
                high(t - 1, D3, x2, 3)
            if not last:
                act.wait_ge(sem("pre2_done"), t + 1)
                act.activation(pre[b][:, 0:D2], pre[b][:, 0:D2], ACT.Relu).then_inc(sem("relu2_done"), 1)
                root(t, 2)

        for t in range(HEAD):
            step2(t, t % 2, first=t == 0)
        ffn_norms()
        with act.Fori(0, LOOPS) as i:
            for k in range(HEAD, HEAD + RING):
                step2(i * RING + k, k % 2)
        step2(T, 1, last=True)

        def turned_rows(c, n):
            tiles = ROUNDS[n]
            act.wait_ge(sem("tr_done"), c * 3 + n + 1)
            dst = free(nT16[c % 2], tiles[0] * P, [[P, len(tiles)], [CW, 4], [1, P]])
            src = free(turned(7, 8), 0, [[4 * (P + 1), len(tiles)], [P + 1, 4], [1, P]])
            act.copy(dst, src).then_inc(sem("nT_done"), 1)

        def root3_(t):
            act.wait_ge(sem("var3_done"), t + 1)
            act.activation(root3, mv3[:, 1:2], ACT.Sqrt, bias=eps[:P]).then_inc(sem("root3_done"), 1)

        def root4_(t):
            act.wait_ge(sem("var4_done"), t + 1)
            act.activation(root4, mv4[:, 1:2], ACT.Sqrt, bias=eps[:P]).then_inc(sem("root4_done"), 1)
            act.copy(accv[:, t, :], pre[1][:, 0:D]).then_inc(sem("sum_done"), 1)

        def router_sum(t):
            act.wait_ge(sem("wprod_done"), t + 1)
            act.activation(pre[1][:, D:2 * D], pre[1][:, D:2 * D], ACT.Identity,
                           accum_out=wv[:, bass.ds(t, 1)]).then_inc(sem("w_done"), 1)

        ffn_norms_rooted()
        root3_(0)
        root4_(0)
        with act.Fori(1, T - RING) as t:
            root3_(t)
            router_sum(t - 1)
            root4_(t)
        for t in range(T - RING, T):
            root3_(t)
            router_sum(t - 1)
            root4_(t)
            if t < T - 1:
                turned_rows(0, t - (T - RING))
        router_sum(T - 1)

        act.preload_act_table(ACT.Gelu_apprx_tanh)

        def high_part(q):
            act.wait_ge(sem("gelu_done"), q + 1)
            if q >= GR:
                act.wait_ge(sem("ypart_done"), q - GR + 1)
            act.activation(gT16[:, q % GR, 0, :], gtemp[q % GR], ACT.Identity, scale=g_scale).then_inc(
                sem("ghigh_done"), 1)

        passes = 0
        for c in range(NC):
            for m in range(8):
                q = c * 8 + m
                act.wait_ge(sem("hid_done"), q + 1)
                if q >= GR:
                    act.wait_ge(sem("glow_done"), q - GR + 1)
                act.activation(halves(gtemp[q % GR]), inner(m), ACT.Gelu_apprx_tanh, scale=hid_back,
                               bias=fb1c[:, m:m + 1]).then_inc(sem("gelu_done"), 1)
                if q >= 1:
                    high_part(q - 1)
                if m in (2, 4, 6) and c + 1 < NC:
                    turned_rows(c + 1, m // 2 - 1)
                if m % 4 and c >= 1 and passes < 2 * ACT_COUNTS:
                    t = T - ACT_COUNTS + passes // 2
                    act.wait_ge(sem("wall_loaded"), 16)
                    act.wait_ge(milestone("negw_done"), AFTER["negw_done"])
                    act.wait_ge(sem("act_counted"), passes)
                    if passes % 2 == 0:
                        ins = act.activation(above, wall, ACT.Sign, bias=pref[:, t:t + 1])
                    else:
                        ins = act.activation(above, above, ACT.Relu, accum_out=gt[:, t:t + 1])
                    ins.then_inc(sem("act_counted"), 1)
                    passes += 1
        high_part(NC * 8 - 1)

    @block.tensor
    def _(pe):
        def mm(o, l, r, start, stop):
            return pe.matmul(o, l, r, start=start, stop=stop)

        pe.wait_ge(sem("ident_ready"), 3)
        pe.wait_ge(milestone("flag_part"), AFTER["flag_part"])
        mm(bank(7, 1, 1), ones[:P, 0:1], flagf[:P], True, True).then_inc(sem("flag_sum"), 1)

        pe.wait_ge(milestone("flag_ready"), AFTER["flag_ready"])
        def degree(b):
            both_oh, ohp, oht = onehot[b % 2]
            pe.wait_ge(sem("onehot_done"), b + 1)
            for j in range(EB):
                last = mm(bank(7, P, T), ohp[:, j, :], oht[:, j, :], b + j == 0, b == EC // EB - 1 and j == EB - 1)
            last.then_inc(sem("degree_used"), 1)

        for b in range(PB):
            degree(b)

        for c in range(NC):
            for k in range(2):
                pe.wait_ge(sem("z_done"), G * c + 4)
                pe.wait_ge(sem("zT_done"), 3 * c - 3 + k + 1 if c else 0)
                for j in range(4):
                    last = pe.transpose(bank(4 + k, 128, P, j * P), zv[:, G * c + j, k * 128:(k + 1) * 128],
                                        ident[:P, 0:P])
                last.then_inc(sem("trz_done"), 1)
            pe.wait_ge(sem("z_done"), G * c + 5)
            pe.wait_ge(sem("zT_done"), 3 * c)
            for k in range(2):
                last = pe.transpose(bank(6, 128, P, k * P), zv[:, G * c + 4, k * 128:(k + 1) * 128], ident[:P, 0:P])
            last.then_inc(sem("trz_done"), 1)
            if c >= 1:
                degree(PB + c - 1)
        left = list(range(PB + NC - 1, EC // EB))
        for t in range(T):
            if t % 4 == 3 and left:
                degree(left.pop(0))
            for m in range(2):
                mm(bank(m, 128, D), zv[:, t, m * 128:(m + 1) * 128], zv[:, t, :], t == 0, False)
            last = mm(bank(3, 1, D), ones[:P, 0:1], zv[:, t, :], t == 0, t == T - 1)
        assert not left
        last.then_inc(sem("zsum_done"), 1)
        pe.wait_ge(milestone("nzrow_done"), AFTER["nzrow_done"])
        for m in range(2):
            mm(bank(m, 128, D), nzrow[:, m * 128:(m + 1) * 128], zrow, False, True)
        for k in range(2):
            last = mm(bank(2, 128, 1, k), zrow[:, k * 128:(k + 1) * 128], ones[0:1, 0:1], True, True)
        last.then_inc(sem("gram_done"), 1)
        pe.wait_ge(milestone("gram_copied"), AFTER["gram_copied"])
        pe.wait_ge(sem("mixw_loaded"), 16 * 10)
        pe.wait_ge(sem("zT_done"), 3 * NC)
        pe.wait_ge(milestone("dinv_read"), AFTER["dinv_read"])
        for m in range(2):
            for n0, n1, b in ((0, 512, 4 + 2 * m), (512, 768, 5 + 2 * m)):
                for k in range(2):
                    last = mm(bank(b, 128, n1 - n0), gram[:, k, m * 128:(m + 1) * 128], wq[:, k, n0:n1],
                              k == 0, k == 1)
        last.then_inc(sem("gw_done"), 1)
        pe.wait_ge(sem("wgw_done"), 2)
        pe.wait_ge(milestone("zrow_done"), AFTER["zrow_done"])
        for m in range(NT):
            for k in range(2):
                mm(bank(3, 128, 1, m), gw[:, k, m * 128:(m + 1) * 128], ones[:, 0:1], k == 0, k == 1)
            for k in range(2):
                last = mm(bank(3, 128, 1, 16 + m), wq[:, k, m * 128:(m + 1) * 128], zcol[:, k:k + 1],
                          k == 0, k == 1)
        last.then_inc(sem("bnsum_done"), 1)
        pe.wait_ge(sem("layerw_loaded"), 48)
        pe.wait_ge(sem("cols_loaded"), 80)
        pe.wait_ge(sem("wgw_done"), 2)
        for k in range(8):
            last = mm(bank(5, P, D2), free(be1c[:, k:k + 1], 0, [[0, P]]), w2[:, k, :], k == 0, k == 7)
        last.then_inc(sem("be2w_done"), 1)
        pe.wait_ge(sem("squares_done"), 2)
        for k in range(4):
            mm(bank(6, 128, 1, 22), ones[:, :], ss1[:, k:k + 1], k == 0, k == 3)
        n = 0
        for L, nk in ((0, 8), (1, 4)):
            for s in (ssw, ssg, ssb):
                for k in range(nk):
                    last = mm(bank(6, 128, 1, 16 + n), ones[:, :], s[:, 8 * L + k:8 * L + k + 1], k == 0, k == nk - 1)
                n += 1
        last.then_inc(sem("bounds_done"), 1)

        pe.wait_ge(milestone("bn_done"), AFTER["bn_done"])
        pe.wait_ge(milestone("wp_done"), AFTER["wp_done"])
        pe.wait_ge(milestone("bounds_read"), AFTER["bounds_read"])
        def norm2(c, k):
            pe.wait_ge(sem("sq_done"), c * 12 + (k + 1))
            if k == 0:
                pe.wait_ge(sem("u_done"), c)
                pe.wait_ge(milestone("be2w_read"), AFTER["be2w_read"])
            for h in range(2):
                last = mm(bank(4 + h, 128, CH), ones[:, :], sq[:, k % 3, h * CH:(h + 1) * CH], k == 0, k == 11)
            last.then_inc(sem("nc_done"), 1)

        def hidden(c, m):
            if m < 2:
                pe.wait_ge(sem("s_evac"), c * NT)
                pe.wait_ge(sem("sq_done"), c * 12)
            else:
                pe.wait_ge(sem("h_done"), c * NT + (m - 1))
            for k in range(2):
                for h in range(2):
                    o = c * CW + h * CH
                    last = mm(bank(2 * (m % 2) + h, 128, CH), wq[:, k, m * 128:(m + 1) * 128],
                              zT[:, k, o:o + CH], k == 0, k == 1)
            last.then_inc(sem("qkv_done"), 1)
            if m >= 2:
                norm2(c, m - 2)

        for m in range(NT):
            hidden(0, m)
        norm2(0, NT - 2)
        norm2(0, NT - 1)
        for c in range(NC):
            hT = hTs[c % 2]
            for m in range(NT):
                if m < 2:
                    pe.wait_ge(sem("h_done"), c * NT + (m + 5))
                    if c >= 1:
                        pe.wait_ge(sem("ft_done"), (c - 1) * G + 2 * m + 2)
                else:
                    pe.wait_ge(sem("s_evac"), c * NT + (m - 1))
                    pe.wait_ge(sem("sq_done"), c * 12 + (NT + m - 1))
                pe.wait_ge(sem("h_done"), c * NT + (m + 1))
                for h in range(2):
                    last = mm(bank(2 * (m % 2) + h, 128, CH), wp[:, m, :], hT[:, m, h * CH:(h + 1) * CH], True, True)
                last.then_inc(sem("s_done"), 1)
                if m >= 2:
                    norm2(c, NT + m - 2)
            norm2(c, 10)
            norm2(c, 11)
            for n in range(4):
                src, half = (hT, n) if n < 2 else (sT, n - 2)
                pe.wait_ge(sem("qk_done"), c * 4 + n)
                if n == 0:
                    pe.wait_ge(sem("ft_done"), c * G)
                if n == 2:
                    pe.wait_ge(sem("s_evac"), c * NT + 4)
                for h in range(2):
                    last = mm(bank(6 + h, 128, CH), kones[:, :], src[:, 2 + half, h * CH:(h + 1) * CH], True, True)
                last.then_inc(sem("k_done"), 1)
                if n < 3 and c < NC - 1:
                    hidden(c + 1, 2 * n)
                    hidden(c + 1, 2 * n + 1)
            if c < NC - 1:
                norm2(c + 1, NT - 2)
                norm2(c + 1, NT - 1)

            def res(j):
                for n in range(4):
                    src, half = (hT, n) if n < 2 else (sT, n - 2)
                    last = mm(res_bank(j), src[:, half, j * P:(j + 1) * P], wres[:, n, :], n == 0, n == 3)
                last.then_inc(sem("res_done"), 1)

            if c < NC - 1:
                pe.wait_ge(sem("h_done"), (c + 1) * NT + NT)
            pe.wait_ge(sem("s_evac"), c * NT + NT)
            pe.wait_ge(sem("sq_done"), c * 12 + 12)
            pe.wait_ge(sem("o_done"), c * 4 + 4)
            res(0)
            pe.wait_ge(sem("qk_done"), c * 4 + 4)
            pe.wait_ge(sem("osq_done"), c * 4 + 4)
            for h in range(2):
                for n in range(4):
                    src, half = (hT, n) if n < 2 else (sT, n - 2)
                    last = mm(bank(6 + h, 1, CH), ones[:, 0:1], src[:, 2 + half, h * CH:(h + 1) * CH],
                              n == 0, n == 3)
            last.then_inc(sem("out_summed"), 1)
            for j in (1, 2, 3):
                res(j)
            pe.wait_ge(sem("out_row_done"), c + 1)
            for j in range(G):
                last = pe.transpose(bank(6, P, 1, j), out_row[:, j * P:(j + 1) * P], ident[0:1, 0:1])
            last.then_inc(sem("out_turned"), 1)
            res(4)

        def aggregate(layer, t, k, b, parts, visit, free_sem, free_at, between=()):
            slot = (layer * T + k) % RING
            pe.wait_ge(sem(f"ring_loaded{slot}"), visit)
            if free_at is not None:
                pe.wait_ge(sem(free_sem), free_at)
            for s in range(T):
                for at_s, work in between:
                    if s == at_s:
                        work()
                for h in range(len(parts)):
                    last = mm(bank(b, P, 512), ring[slot][:, s, :], parts[h](s), s == 0 and h == 0,
                              s == T - 1 and h == len(parts) - 1)
            last.then_inc(sem("agg_done"), 1)

        both = [lambda s: x2[:, s, :, :].rearrange("p h d -> p (h d)")]
        wide = [lambda s: h2in[:, s, 0, :], lambda s: h2in[:, s, 1, :]]

        def loads(layer, k, i):
            first = 16 * ((layer * T + k) // RING + 1)
            return first if i is None else i * 16 + first

        def free_from(t, k, i):
            return t - 1 if i is not None or k >= 2 else None

        def turn(t, b, k_tiles, layer):
            pe.wait_ge(sem(f"xhat{layer - 1}_done"), t + 1)
            pe.wait_ge(sem(f"xT{layer}_done"), t)
            for k in range(k_tiles):
                last = pe.transpose(bank(5 + k // 4, 128, P, (k % 4) * P), pre[b][:, k * 128:(k + 1) * 128],
                                    ident[:P, 0:P])
            last.then_inc(sem(f"trx{layer}_done"), 1)

        def product(t, k_tiles, w, width, layer):
            pe.wait_ge(sem(f"xT{layer}_done"), t + 1)
            pe.wait_ge(sem(f"hbuf{layer}_done"), t)
            for k in range(k_tiles):
                last = mm(bank(7, P, width), xT[:, k, :], w[:, k, :], k == 0, k == k_tiles - 1)
            last.then_inc(sem(f"h{layer}_done"), 1)

        def turn_y(t):
            pe.wait_ge(sem("ylo_done"), t + 1)
            pe.wait_ge(sem("yT_done"), t)
            for h in range(2):
                for c in range(2):
                    last = pe.transpose(turned(2, 4)[:, 2 * h + c, :],
                                        y16[:, h, c * 128:(c + 1) * 128], ident16[:P, 0:P])
            last.then_inc(sem("try_done"), 1)

        def turn_x(t):
            pe.wait_ge(sem("xlo_done"), t + 1)
            pe.wait_ge(sem("xT2_done"), t)
            for h in range(2):
                for k in range(8):
                    last = pe.transpose(turned(5 + h, 8)[:, k, :],
                                        x16[:, h, k * 128:(k + 1) * 128], ident16[:P, 0:P])
            last.then_inc(sem("trx2_done"), 1)

        PARTS = ((0, 0), (1, 0), (0, 1))

        def product1(t):
            pe.wait_ge(sem("yT_done"), t + 1)
            pe.wait_ge(sem("pre1_done"), t)
            for n in range(2):
                for c in range(2):
                    for hx, hw in PARTS:
                        last = mm(bank(3 + n, P, 512), yT16[:, hx, c, :], w1s[:, 2 * c + n, hw, :],
                                  c == 0 and (hx, hw) == (0, 0), c == 1 and (hx, hw) == (0, 1))
            last.then_inc(sem("p1_done"), 1)

        def product2(t):
            pe.wait_ge(sem("xT2_done"), t + 1)
            pe.wait_ge(sem("hbuf2_done"), t)
            for k in range(8):
                for hx, hw in PARTS:
                    last = mm(bank(7, P, D2), xT16[:, hx, k, :], w2s[:, k, hw, :],
                              k == 0 and (hx, hw) == (0, 0), k == 7 and (hx, hw) == (0, 1))
            last.then_inc(sem("h2_done"), 1)

        def step1(t, k, i, before=2):
            aggregate(0, t, k, k % 2, both, loads(0, k, i), "y_done", free_from(t, k, i))
            if before >= 2:
                product2(t - 2)
            turn_y(t)
            if before >= 1:
                turn_x(t - 1)
            product1(t)

        pe.wait_ge(sem("rows1_ready"), T)
        pe.wait_ge(sem("ft_done"), T)
        pe.wait_ge(sem("wpiece_done"), len(wpieces))
        pe.wait_ge(milestone("ident16_ready"), AFTER["ident16_ready"])
        for t in range(HEAD):
            step1(t, t, None, min(t, 2))
        with pe.Fori(0, LOOPS) as i:
            for k in range(HEAD, HEAD + RING):
                step1(i * RING + k, k, i)

        def step2(t, k, i, first=False):
            b = k % 2
            previous = [
                (12, lambda: product2(T - 2)), (16, lambda: turn_x(T - 1)), (21, lambda: product2(T - 1)),
                (T - 3, lambda: pe.wait_ge(sem("lo2_done"), T - 2)),
                (T - 2, lambda: pe.wait_ge(sem("lo2_done"), T - 1)),
                (T - 1, lambda: pe.wait_ge(sem("lo2_done"), T))] if first else [
                (12, lambda: turn(t - 1, (k - 1) % 2, 4, 3)),
                (19, lambda: product(t - 1, 4, w3, D3, 3))]
            aggregate(1, t, k, b, wide, loads(1, k, i), "pre2_done", free_from(t, k, i), previous)

        pe.wait_ge(sem("lo2_done"), T - 3)
        pe.wait_ge(sem("y_done"), T)
        for t in range(HEAD):
            step2(t, t, None, first=t == 0)
        with pe.Fori(0, LOOPS) as i:
            for k in range(HEAD, HEAD + RING):
                step2(i * RING + k, k, i)

        def turn_rows(c, n):
            pe.wait_ge(sem("stage_done"), c + 1)
            pe.wait_ge(sem("nT_done"), c * 3 + n)
            for at_j, j in enumerate(ROUNDS[n]):
                for h in range(2):
                    for k in range(2):
                        last = pe.transpose(turned(7, 8)[:, 4 * at_j + 2 * h + k, :],
                                            stage16[c % 2][:, h, j, k * 128:(k + 1) * 128], ident16[:P, 0:P])
            last.then_inc(sem("tr_done"), 1)

        def step3(t, k, i):
            previous = [
                (19, lambda: turn(T - 1, (T - 1) % 2, 4, 3)),
                (T - 2, lambda: product(T - 1, 4, w3, D3, 3)),
                (T - 2, lambda: pe.wait_ge(sem("lo3_done"), T - 1)),
                (T - 1, lambda: pe.wait_ge(sem("lo3_done"), T))] if k == 0 else ()
            aggregate(2, t, k, k % 2, both, loads(2, k, i), "pre3_done", free_from(t, k, i), previous)

        pe.wait_ge(sem("fsquares_done"), 1)
        for n, columns in enumerate(((0, 1), (2, 3), (4,))):
            for k in columns:
                last = mm(bank(6, 128, 1, n), ones[:, :], ssf[:, k:k + 1], k == columns[0], k == columns[-1])
        last.then_inc(sem("fsum_done"), 1)

        pe.wait_ge(sem("lo3_done"), T - 2)
        pe.wait_ge(sem("pre2_done"), T)
        for t in range(HEAD):
            step3(t, t, None)
        with pe.Fori(0, LOOPS - 1) as i:
            for k in range(HEAD, HEAD + RING):
                step3(i * RING + k, k, i)
        for t in range(T - RING, T):
            step3(t, t, None)
            if t < T - 1:
                turn_rows(0, t - (T - RING))

        def inner_product(c, m):
            q = c * 8 + m
            if m == 0:
                pe.wait_ge(sem("nT_done"), c * 3 + 3)
            if q >= 2:
                pe.wait_ge(sem("gelu_done"), q - 1)
            for h in range(2):
                for k in range(2):
                    for hx, hw in PARTS:
                        last = mm(inner(m)[:, h, :], f1s[:, 2 * k + m // 4, hw, m % 4 * 128:(m % 4 + 1) * 128],
                                  nT16[c % 2][:, 2 * hx + k, h * CH:(h + 1) * CH],
                                  k == 0 and (hx, hw) == (0, 0), k == 1 and (hx, hw) == (0, 1))
            last.then_inc(sem("hid_done"), 1)

        def outer_product(q):
            c, m = divmod(q, 8)
            pe.wait_ge(sem("glow_done"), q + 1)
            if m == 0:
                pe.wait_ge(sem("pre3_done"), T)
                pe.wait_ge(sem("yffn_evac"), c * G)
            for j in range(G):
                for hx, hw in PARTS:
                    last = mm(accumulator(j), gT16[:, m % GR, hx, j * P:(j + 1) * P],
                              f2s[:, m // 2, hw, m % 2 * D:(m % 2 + 1) * D],
                              m == 0 and j % 2 == 0 and (hx, hw) == (0, 0),
                              m == 7 and j in (1, 3, 4) and (hx, hw) == (0, 1))
            last.then_inc(sem("ypart_done"), 1)

        pe.wait_ge(sem("npad_done"), 2)
        pe.wait_ge(sem("fpiece_done"), 8)
        for c in range(NC):
            for m in range(8):
                inner_product(c, m)
                if c * 8 + m >= 3:
                    outer_product(c * 8 + m - 3)
                if m in (1, 3, 5) and c + 1 < NC:
                    turn_rows(c + 1, m // 2)
                if c == COUNTED and m == 3:
                    pe.wait_ge(milestone("least_done"), AFTER["least_done"])
                    pe.transpose(bank(7, 1, P), n4[:, 0:1], ident[:P, 0:P]).then_inc(sem("least_turned"), 1)
                if c == COUNTED and m == 5:
                    pe.wait_ge(milestone("last_done"), AFTER["last_done"])
                    pe.transpose(bank(7, P, 1), free(n4[0:1, 1:2], 0, [[0, P]]), ident[0:1, 0:1]).then_inc(
                        sem("last_spread"), 1)
                if c == COUNTED and m == 7:
                    pe.wait_ge(sem("tri"), 2)
                    pe.wait_ge(milestone("prefix_done"), AFTER["prefix_done"])
                    mm(bank(7, P, 1), tri[:P, 0:P], pref[:, T - 1:T], True, True).then_inc(
                        sem("before_done"), 1)
        outer_product(NC * 8 - 3)
        outer_product(NC * 8 - 2)
        outer_product(NC * 8 - 1)


def _plan(v):
    pad = lambda e, fill: np.concatenate([np.full(PADE, fill, e.dtype), e, np.full(PADE, fill, e.dtype)])
    order = np.concatenate([np.arange(32 * g, 32 * g + 32) for k in range(3) for g in range(k, 24, 3)])
    tiles = lambda x: np.ascontiguousarray(x.reshape(-1, 128).T)
    wpw = v["L0_mix_w_pw"][order, :, 0].reshape(NT, 4, 32, 32).transpose(1, 3, 0, 2)
    return {
        "x": v["x"], "src_pad": pad(v["src"], 100000), "dst_pad": pad(v["dst"], 75000),
        "w1": v["L0_gnn_W1"], "w2": v["L0_gnn_W2"], "w3": v["L0_gnn_W3"],
        "b1": v["L0_gnn_b1"], "b2": v["L0_gnn_b2"], "b3": v["L0_gnn_b3"],
        "g1": tiles(v["L0_gnn_g1"]), "be1": tiles(v["L0_gnn_beta1"]),
        "g2": tiles(v["L0_gnn_g2"]), "be2": tiles(v["L0_gnn_beta2"]),
        "g3": v["L0_gnn_g3"], "be3": v["L0_gnn_beta3"],
        "wq": np.ascontiguousarray(v["L0_mix_w_qkv"][order, :, 2].T),
        "bng": tiles(v["L0_mix_bn_gamma"][order]), "bnb": tiles(v["L0_mix_bn_beta"][order]),
        "wdw": tiles(v["L0_mix_w_dw"][order, 0, 2]), "wpw": np.ascontiguousarray(wpw),
        "wres": np.ascontiguousarray(v["L0_mix_w_res"][:, :, 0].T), "bres": v["L0_mix_b_res"],
        "wr": v["L0_ffn_wr"][:, 0], "br": v["L0_ffn_br"], "f1": v["L0_ffn_w1"],
        "fb1": tiles(v["L0_ffn_b1"]), "f2": v["L0_ffn_w2"], "fb2": v["L0_ffn_b2"],
    }


def kernel(**inputs):
    import concourse.bacc as bacc
    from concourse.bass_utils import run_bass_kernel_spmd

    nc = bacc.Bacc("TRN2", target_bir_lowering=False, num_devices=1)
    arrays, aps = {}, {}
    for name, x in _plan({k: np.asarray(x) for k, x in inputs.items()}).items():
        x = np.ascontiguousarray(x)
        arrays[f"in_{name}"] = x
        aps[name] = nc.dram_tensor(f"in_{name}", x.shape, mybir.dt.from_np(x.dtype), kind="ExternalInput").ap()
    out = nc.dram_tensor("out", (N, D), F32, kind="ExternalOutput").ap()
    scratch = {"counts": nc.dram_tensor("counts", (T, P, N), F16).ap(), "w": nc.dram_tensor("w_nodes", (N,), F32).ap()}
    build(nc, aps, out, scratch)
    return run_bass_kernel_spmd(nc, [arrays], core_ids=[0]).results[0]["out"]
```
